# Optimizing a Trainium2 kernel written in Bass

```python
import numpy as np
import jax
import jax.numpy as jnp

def _softmax(x, axis=-1):
    return jax.nn.softmax(x, axis=axis)

def _gelu(x):
    return jax.nn.gelu(x, approximate=True)

def _silu(x):
    return jax.nn.silu(x)

def _sigmoid(x):
    return jax.nn.sigmoid(x)

def _layernorm(x, axis=-1, eps=1e-05):
    m = jnp.mean(x, axis=axis, keepdims=True)
    v = jnp.var(x, axis=axis, keepdims=True)
    return (x - m) / jnp.sqrt(v + eps)

def _scatter_add(tgt, idx, src, axis=0):
    return tgt.at[idx].add(src)

def _segment_sum(src, seg, n):
    return jax.ops.segment_sum(src, seg, n)
kernel_name = 'mk_gps_d1_gnn_r8_4760b7'

def setup_inputs(seed: int=0):
    np.random.seed(seed)
    _w = jnp.asarray

    def _rec_inputs():
        import jax
        import jax.numpy as jnp
        _gk = jax.random.key(seed)
        x = -0.0003713 + 1 * jax.random.normal(jax.random.fold_in(_gk, 1), (6250, 256), jnp.float32)
        _s = jax.random.randint(jax.random.fold_in(_gk, 2), (100000,), 0, 6250, jnp.int32)
        _d = jax.random.randint(jax.random.fold_in(_gk, 3), (100000,), 0, 6250, jnp.int32)
        _loop = jnp.arange(6250, dtype=jnp.int32)
        src = jnp.concatenate([_s, _d, _loop])
        dst = jnp.concatenate([_d, _s, _loop])
        _o = jnp.argsort(dst, stable=True)
        src = src[_o]
        dst = dst[_o]
        return (x, src, dst)
    x, src, dst = _rec_inputs()

    def _L0_gnn_setup():
        import jax, jax.numpy as jnp
        import numpy as np
        N, IN_DIM, OUT_DIM, HEADS, E = (6250, 256, 256, 4, 100000)
        HEAD_DIM = OUT_DIM // HEADS
        NEG_SLOPE = 0.2
        key = jax.random.key(seed)
        k = jax.random.split(key, 6)
        h = jax.random.normal(k[0], (N, IN_DIM), dtype=jnp.float32)
        edge_index = jax.random.randint(k[1], (2, E), 0, N, dtype=jnp.int32)
        W = jax.random.normal(k[2], (OUT_DIM, IN_DIM), dtype=jnp.float32) * (1.0 / np.sqrt(IN_DIM))
        b = jnp.zeros((OUT_DIM,), dtype=jnp.float32)
        a_src = jax.random.normal(k[3], (HEADS, HEAD_DIM), dtype=jnp.float32) * (1.0 / np.sqrt(HEAD_DIM))
        a_dst = jax.random.normal(k[4], (HEADS, HEAD_DIM), dtype=jnp.float32) * (1.0 / np.sqrt(HEAD_DIM))
        return {'h': h, 'edge_index': edge_index, 'W': W, 'b': b, 'a_src': a_src, 'a_dst': a_dst}
    _L0_gnn_all = _L0_gnn_setup()
    _L0_gnn_in = {k: v for k, v in _L0_gnn_all.items() if k in ('W', 'b', 'a_src', 'a_dst')}
    del _L0_gnn_all

    def _L0_mix_setup():
        import jax, jax.numpy as jnp
        import numpy as np
        N, F, C, H = (32, 512, 256, 8)
        D = C // H
        EPS_ATTN = 1e-06
        EPS_LN = 1e-05

        def layer_norm(x, g, b):
            mu = jnp.mean(x, axis=-1, keepdims=True)
            var = jnp.var(x, axis=-1, keepdims=True)
            return (x - mu) * jax.lax.rsqrt(var + EPS_LN) * g + b
        key = jax.random.key(seed)
        ks = jax.random.split(key, 8)
        s = 1.0 / np.sqrt(C)
        return {'x': jax.random.normal(ks[0], (N, F, C), jnp.float32), 'Wqkv': jax.random.uniform(ks[1], (3 * C, C), jnp.float32, -s, s), 'ln1_g': jnp.ones((C,), jnp.float32), 'ln1_b': jnp.zeros((C,), jnp.float32), 'W1': jax.random.uniform(ks[2], (C, C), jnp.float32, -s, s), 'b1': jax.random.uniform(ks[3], (C,), jnp.float32, -s, s), 'W2': jax.random.uniform(ks[4], (C, C), jnp.float32, -s, s), 'b2': jax.random.uniform(ks[5], (C,), jnp.float32, -s, s), 'ln2_g': jnp.ones((C,), jnp.float32), 'ln2_b': jnp.zeros((C,), jnp.float32)}
    _L0_mix_all = _L0_mix_setup()
    _L0_mix_in = {k: v for k, v in _L0_mix_all.items() if k in ('Wqkv', 'ln1_g', 'ln1_b', 'W1', 'b1', 'W2', 'b2', 'ln2_g', 'ln2_b')}
    del _L0_mix_all

    def _L0_ffn_setup():
        import jax, jax.numpy as jnp
        import numpy as np
        B, A = (512, 8)
        IN, OUT = (256, 256)
        SH1, SH2 = (256, 128)
        EH1, EH2 = (128, 64)
        E, TOPK = (4, 2)

        def _shared_mlp(x, W1, b1, W2, b2, W3, b3):
            h = jax.nn.relu(x @ W1 + b1)
            h = jax.nn.relu(h @ W2 + b2)
            return h @ W3 + b3

        def _experts_mlp(x, eW1, eb1, eW2, eb2, eW3, eb3):
            h = jax.nn.relu(jnp.einsum('baf,efh->ebah', x, eW1) + eb1[:, None, None, :])
            h = jax.nn.relu(jnp.einsum('ebah,ehg->ebag', h, eW2) + eb2[:, None, None, :])
            o = jnp.einsum('ebag,ego->ebao', h, eW3) + eb3[:, None, None, :]
            return jnp.moveaxis(o, 0, -1)
        key = jax.random.key(seed)
        ks = jax.random.split(key, 16)
        s = 0.05
        return {'x': jax.random.normal(ks[0], (B, A, IN), jnp.float32), 'sW1': jax.random.normal(ks[1], (IN, SH1), jnp.float32) * s, 'sb1': jnp.zeros((SH1,), jnp.float32), 'sW2': jax.random.normal(ks[2], (SH1, SH2), jnp.float32) * s, 'sb2': jnp.zeros((SH2,), jnp.float32), 'sW3': jax.random.normal(ks[3], (SH2, OUT), jnp.float32) * s, 'sb3': jnp.zeros((OUT,), jnp.float32), 'eW1': jax.random.normal(ks[4], (E, IN, EH1), jnp.float32) * s, 'eb1': jnp.zeros((E, EH1), jnp.float32), 'eW2': jax.random.normal(ks[5], (E, EH1, EH2), jnp.float32) * s, 'eb2': jnp.zeros((E, EH2), jnp.float32), 'eW3': jax.random.normal(ks[6], (E, EH2, OUT), jnp.float32) * s, 'eb3': jnp.zeros((E, OUT), jnp.float32), 'gW': jax.random.normal(ks[7], (IN, E), jnp.float32) * s, 'gb': jnp.zeros((E,), jnp.float32)}
    _L0_ffn_all = _L0_ffn_setup()
    _L0_ffn_in = {k: v for k, v in _L0_ffn_all.items() if k in ('sW1', 'sb1', 'sW2', 'sb2', 'sW3', 'sb3', 'eW1', 'eb1', 'eW2', 'eb2', 'eW3', 'eb3', 'gW', 'gb')}
    del _L0_ffn_all
    return {'x': x, 'src': src, 'dst': dst, 'L0_gnn_W': _L0_gnn_in['W'], 'L0_gnn_b': _L0_gnn_in['b'], 'L0_gnn_a_src': _L0_gnn_in['a_src'], 'L0_gnn_a_dst': _L0_gnn_in['a_dst'], 'L0_mix_Wqkv': _L0_mix_in['Wqkv'], 'L0_mix_ln1_g': _L0_mix_in['ln1_g'], 'L0_mix_ln1_b': _L0_mix_in['ln1_b'], 'L0_mix_W1': _L0_mix_in['W1'], 'L0_mix_b1': _L0_mix_in['b1'], 'L0_mix_W2': _L0_mix_in['W2'], 'L0_mix_b2': _L0_mix_in['b2'], 'L0_mix_ln2_g': _L0_mix_in['ln2_g'], 'L0_mix_ln2_b': _L0_mix_in['ln2_b'], 'L0_ffn_sW1': _L0_ffn_in['sW1'], 'L0_ffn_sb1': _L0_ffn_in['sb1'], 'L0_ffn_sW2': _L0_ffn_in['sW2'], 'L0_ffn_sb2': _L0_ffn_in['sb2'], 'L0_ffn_sW3': _L0_ffn_in['sW3'], 'L0_ffn_sb3': _L0_ffn_in['sb3'], 'L0_ffn_eW1': _L0_ffn_in['eW1'], 'L0_ffn_eb1': _L0_ffn_in['eb1'], 'L0_ffn_eW2': _L0_ffn_in['eW2'], 'L0_ffn_eb2': _L0_ffn_in['eb2'], 'L0_ffn_eW3': _L0_ffn_in['eW3'], 'L0_ffn_eb3': _L0_ffn_in['eb3'], 'L0_ffn_gW': _L0_ffn_in['gW'], 'L0_ffn_gb': _L0_ffn_in['gb']}

def reference(x, src, dst, L0_gnn_W, L0_gnn_b, L0_gnn_a_src, L0_gnn_a_dst, L0_mix_Wqkv, L0_mix_ln1_g, L0_mix_ln1_b, L0_mix_W1, L0_mix_b1, L0_mix_W2, L0_mix_b2, L0_mix_ln2_g, L0_mix_ln2_b, L0_ffn_sW1, L0_ffn_sb1, L0_ffn_sW2, L0_ffn_sb2, L0_ffn_sW3, L0_ffn_sb3, L0_ffn_eW1, L0_ffn_eb1, L0_ffn_eW2, L0_ffn_eb2, L0_ffn_eW3, L0_ffn_eb3, L0_ffn_gW, L0_ffn_gb):
    import jax
    import jax.numpy as jnp

    def _L0_gnn_ref(h, edge_index, W, b, a_src, a_dst):
        import jax, jax.numpy as jnp
        import numpy as np
        N, IN_DIM, OUT_DIM, HEADS, E = (6250, 256, 256, 4, 100000)
        HEAD_DIM = OUT_DIM // HEADS
        NEG_SLOPE = 0.2
        idx_i, idx_j = (edge_index[0], edge_index[1])
        Wh = (h @ W.T + b).reshape(N, HEADS, HEAD_DIM)
        alpha_src = jnp.einsum('nhd,hd->nh', Wh, a_src)
        alpha_dst = jnp.einsum('nhd,hd->nh', Wh, a_dst)
        e = jax.nn.leaky_relu(alpha_src[idx_i] + alpha_dst[idx_j], NEG_SLOPE)
        m = jax.ops.segment_max(e, idx_i, num_segments=N)
        ex = jnp.exp(e - m[idx_i])
        denom = jax.ops.segment_sum(ex, idx_i, num_segments=N)
        att = ex / denom[idx_i]
        out = jax.ops.segment_sum(att[:, :, None] * Wh[idx_j], idx_i, num_segments=N)
        return out.reshape(N, OUT_DIM)

    def _L0_mix_ref(x, Wqkv, ln1_g, ln1_b, W1, b1, W2, b2, ln2_g, ln2_b):
        import jax, jax.numpy as jnp
        import numpy as np
        N, F, C, H = (32, 512, 256, 8)
        D = C // H
        EPS_ATTN = 1e-06
        EPS_LN = 1e-05

        def layer_norm(x, g, b):
            mu = jnp.mean(x, axis=-1, keepdims=True)
            var = jnp.var(x, axis=-1, keepdims=True)
            return (x - mu) * jax.lax.rsqrt(var + EPS_LN) * g + b
        n, f, c = x.shape
        qkv = jnp.einsum('nfc,oc->nfo', x, Wqkv)
        q, k, v = jnp.split(qkv, 3, axis=-1)
        q = q.reshape(n, f, H, D)
        k = k.reshape(n, f, H, D)
        v = v.reshape(n, f, H, D)
        q = jax.nn.elu(q) + 1.0
        k = jax.nn.elu(k) + 1.0
        kv = jnp.einsum('nshd,nshm->nhmd', k, v)
        ksum = jnp.sum(k, axis=1)
        z = 1.0 / (jnp.einsum('nlhd,nhd->nlh', q, ksum) + EPS_ATTN)
        t = jnp.einsum('nlhd,nhmd,nlh->nlhm', q, kv, z)
        t = t.reshape(n, f, c)
        x1 = layer_norm(t + x, ln1_g, ln1_b)
        h = jax.nn.gelu(jnp.einsum('nfc,oc->nfo', x1, W1) + b1, approximate=False)
        y = jnp.einsum('nfc,oc->nfo', h, W2) + b2
        return layer_norm(y + x1, ln2_g, ln2_b)

    def _L0_ffn_ref(x, sW1, sb1, sW2, sb2, sW3, sb3, eW1, eb1, eW2, eb2, eW3, eb3, gW, gb):
        import jax, jax.numpy as jnp
        import numpy as np
        B, A = (512, 8)
        IN, OUT = (256, 256)
        SH1, SH2 = (256, 128)
        EH1, EH2 = (128, 64)
        E, TOPK = (4, 2)

        def _shared_mlp(x, W1, b1, W2, b2, W3, b3):
            h = jax.nn.relu(x @ W1 + b1)
            h = jax.nn.relu(h @ W2 + b2)
            return h @ W3 + b3

        def _experts_mlp(x, eW1, eb1, eW2, eb2, eW3, eb3):
            h = jax.nn.relu(jnp.einsum('baf,efh->ebah', x, eW1) + eb1[:, None, None, :])
            h = jax.nn.relu(jnp.einsum('ebah,ehg->ebag', h, eW2) + eb2[:, None, None, :])
            o = jnp.einsum('ebag,ego->ebao', h, eW3) + eb3[:, None, None, :]
            return jnp.moveaxis(o, 0, -1)
        all_out = _experts_mlp(x, eW1, eb1, eW2, eb2, eW3, eb3)
        shared = _shared_mlp(x, sW1, sb1, sW2, sb2, sW3, sb3)
        gates = jax.nn.softmax(x @ gW + gb, axis=-1)
        topv, topi = jax.lax.top_k(gates, TOPK)
        topw = jax.nn.softmax(topv, axis=-1)
        sel = jnp.take_along_axis(all_out, topi[:, :, None, :], axis=-1)
        gated = jnp.sum(sel * topw[:, :, None, :], axis=-1)
        return shared + gated
    edge_index = jnp.stack([src, dst])
    xn = _layernorm(x, axis=-1)
    x = x + _L0_gnn_ref(xn, edge_index, L0_gnn_W, L0_gnn_b, L0_gnn_a_src, L0_gnn_a_dst) + _L0_mix_ref(xn[None], L0_mix_Wqkv, L0_mix_ln1_g, L0_mix_ln1_b, L0_mix_W1, L0_mix_b1, L0_mix_W2, L0_mix_b2, L0_mix_ln2_g, L0_mix_ln2_b)[0]
    x = x + _L0_ffn_ref(_layernorm(x, axis=-1)[None], L0_ffn_sW1, L0_ffn_sb1, L0_ffn_sW2, L0_ffn_sb2, L0_ffn_sW3, L0_ffn_sb3, L0_ffn_eW1, L0_ffn_eb1, L0_ffn_eW2, L0_ffn_eb2, L0_ffn_eW3, L0_ffn_eb3, L0_ffn_gW, L0_ffn_gb)[0]
    return x

_drawn_inputs = setup_inputs


def setup_inputs(seed=0):
    import zlib

    import numpy as np

    out = dict(_drawn_inputs(seed))
    spreads = {'L0_gnn_b': (0.0, 0.1),
     'L0_mix_ln1_g': (1.0, 0.2),
     'L0_mix_ln1_b': (0.0, 0.1),
     'L0_mix_ln2_g': (1.0, 0.2),
     'L0_mix_ln2_b': (0.0, 0.1),
     'L0_ffn_sb1': (0.0, 0.8),
     'L0_ffn_sb2': (0.0, 0.387),
     'L0_ffn_sb3': (0.0, 0.1),
     'L0_ffn_eb1': (0.0, 2.0),
     'L0_ffn_eb2': (0.0, 0.8),
     'L0_ffn_eb3': (0.0, 0.1),
     'L0_ffn_gb': (0.0, 0.689)}
    factors = {'L0_mix_Wqkv': 8.0, 'L0_mix_b1': 8.0, 'L0_mix_b2': 3.199, 'L0_ffn_eW1': 2.679}
    for name, (base, spread) in spreads.items():
        noise = np.random.default_rng([zlib.crc32(name.encode()), seed]).standard_normal(out[name].shape)
        drawn = base * np.exp(spread * noise) if base else spread * noise
        out[name] = jnp.asarray(drawn.astype(out[name].dtype))
    for name, factor in factors.items():
        out[name] = (out[name] * factor).astype(out[name].dtype)
    return out
```

```python
import numpy as np
import concourse.bass as bass
from concourse import mybir
from contextlib import ExitStack

F32, BF16, I32, U16 = mybir.dt.float32, mybir.dt.bfloat16, mybir.dt.int32, mybir.dt.uint16
ALU = mybir.AluOpType
ACT = mybir.ActivationFunctionType
AX = mybir.AxisListType
ds = bass.ds

P = 128
N, C, H = 6250, 256, 4
HD = C // H
E_ALL = 206250
NB = -(-N // P)
TAIL = N - (NB - 1) * P
BATCH = 4
NBP = -(-NB // BATCH) * BATCH
ITERS = NBP // BATCH
W4 = BATCH * P
NBK = NB + 1
TE = -(-E_ALL // P)
TE_LAST = E_ALL - (P - 1) * TE
QUARTERS = 4
TQ = TE // QUARTERS
SUB = 31
SUBS = (16, 15)
G = 2
GR = G * P
GROUPS = 4
EIT = -(-((E_ALL + NB * (GR - 1)) // GR) // (2 * GROUPS))
NG = EIT * 2 * GROUPS
LIST = (NG + 1) * GR
TB = C + H
NO_NODE = 200.0
EPS_LN, EPS_ATTN, SLOPE = 1e-5, 1e-6, 0.2
MH, MD = 8, 32
KVC = 132
SH1, SH2, EH1, EH2, NE = 256, 128, 128, 64, 4
assert TE == QUARTERS * TQ and TQ % SUB == 0 and sum(SUBS) == SUB and NB <= NBK < P


def wait_freed(engine, semaphore, count):
    if not (isinstance(count, int) and count == 0):
        engine.wait_ge(semaphore, count)


def first_and_rest(engine, count, body):
    body(0)
    with engine.Fori(1, count) as it:
        body(it)


def stage_sort_and_mix(nc, A, sh):
    ctx = ExitStack()
    with ctx:
        sb = lambda name, shape, dt=F32: ctx.enter_context(nc.sbuf_tensor(name, shape, dt))
        sem = lambda name: ctx.enter_context(nc.semaphore(name))
        x, xn = sh["x"], sh["xn"]
        ident, iota_row, ones_row = sh["ident"], sh["iota_row"], sh["ones_row"]
        node_col = sh["node_col"]
        banks = [ctx.enter_context(nc.psum_tensor(f"bank1_{i}", [P, 512], F32)) for i in range(8)]

        pos = sb("pos", [P, TE], I32)
        payload = sb("payload", [P, TE, 2], I32)
        spare = xn[:, :, :].rearrange("p b c -> p (b c)")
        at = [0]

        def carve(words):
            at[0] += words
            return spare[:, at[0] - words:at[0]]

        src_i = carve(TE).bitcast(I32)
        dst_i = carve(TE).bitcast(I32)
        int_tmp = carve(TE).bitcast(I32)
        bucket = carve(TE // 2).bitcast(BF16)
        hit = carve(TE // 2).bitcast(BF16)
        running = carve(TQ).bitcast(I32)
        places = carve(TQ).bitcast(I32)
        pad_rows = carve(2 * (LIST // P)).rearrange("p (r w) -> p r w", w=2)
        grp_cmp = carve(7 * NB)
        counts = sb("counts", [P, NBK])
        totals = sb("totals", [P, NBK])
        grp_i = sb("grp_i", [P, NBK], I32)
        grp_end = sb("grp_end", [P, NBK])
        base = sb("base", [P, NBK])
        carry = sb("carry", [P, NBK])
        grp_no = sb("grp_no", [P, 7])
        grp_blk = sb("grp_blk", [P, 7])
        grp_blk_i = sb("grp_blk_i", [P, 7], I32)
        before = sb("before", [P, P])
        ones_sq = sb("ones_sq", [P, P])
        stage_pos = [sb(f"stage_pos{i}", [P, SUBS[i]], I32) for i in range(2)]
        stage_pay = [sb(f"stage_pay{i}", [P, SUBS[i], 2], I32) for i in range(2)]

        NW = 3 * C + 3 * C
        w_nat = sb("w_nat", [P, NW // P, C])
        wT = sb("wT", [P, 2, NW])
        QKV, WG, W1, W2 = 0, 3 * C, 4 * C, 5 * C
        a_mat = sb("a_mat", [P, 2, 2 * H])
        b_col = sb("b_col", [P, 2])
        b_row = sb("b_row", [1, C + 2 * H])
        g_w = sb("g_w", [P, 2, C + 2 * H])
        b1_col = sb("b1_col", [P, 2])
        b2_row = sb("b2_row", [1, C])
        ln = sb("ln", [P, 4, C])
        valid = sb("valid", [P, NBP])
        tail_rows = sb("tail_rows", [P, 1])
        kv_bd = sb("kv_bd", [P, 2, KVC])

        stats = sb("stats", [P, BATCH, 6])
        mv = sb("mv", [P, BATCH, 2])
        std = sb("std", [P, BATCH])
        inv = sb("inv", [P, BATCH])
        xT = sb("xT", [P, 2, W4])
        wh = sb("wh", [P, BATCH, C + 2 * H])
        k_min = sb("k_min", [P, 2, C])
        k_exp = sb("k_exp", [P, 2, C])
        kk = sb("kk", [P, 2, C])
        vv = sb("vv", [P, 2, 2, KVC])
        q_min = sb("q_min", [P, 2, W4])
        qT = sb("qT", [P, 2, W4])
        den = sb("den", [P, BATCH, MH])
        y = sb("y", [P, BATCH, C])
        x1 = sb("x1", [P, BATCH, C])

        (s_pads_set, s_src, s_dst, s_x, s_xtail, s_w, s_misc, s_fill, s_filled, s_const) = map(sem, (
            "s_pads_set", "s_src", "s_dst", "s_x", "s_xtail", "s_w", "s_misc", "s_fill", "s_filled", "s_const"))
        (s_counts, s_base, s_pos, s_staged0, s_staged1, s_scat0, s_scat1, s_blk, s_blkd, s_blkr) = map(sem, (
            "s_counts", "s_base", "s_pos", "s_staged0", "s_staged1", "s_scat0", "s_scat1", "s_blk", "s_blkd", "s_blkr"))
        (s_wtr, s_wtc, s_gw, s_gwc, s_kv0) = map(sem, ("s_wtr", "s_wtc", "s_gw", "s_gwc", "s_kv0"))
        (s_var, s_std, s_xn, s_tr, s_xT, s_g, s_wh, s_tab, s_kv, s_kmin, s_kexp, s_vc, s_kk, s_acc, s_nd) = map(sem, (
            "s_var", "s_std", "s_xn", "s_tr", "s_xT", "s_g", "s_wh", "s_tab", "s_kv", "s_kmin", "s_kexp", "s_vc",
            "s_kk", "s_acc", "s_nd"))
        (s_bd, s_tr2, s_xT2, s_q, s_qmin, s_qexp, s_qT, s_t, s_var2, s_std2, s_x1, s_tr3, s_xT3, s_h, s_h1, s_y2,
         s_y2r) = map(sem, ("s_bd", "s_tr2", "s_xT2", "s_q", "s_qmin", "s_qexp", "s_qT", "s_t", "s_var2", "s_std2",
                            "s_x1", "s_tr3", "s_xT3", "s_h", "s_h1", "s_y2", "s_y2r"))
        s_dve, s_pool, s_xc = sem("s_dve"), sem("s_pool"), sem("s_xc")
        s_staged, s_scat = (s_staged0, s_staged1), (s_scat0, s_scat1)
        block = ctx.enter_context(nc.Block())

        @block.sync
        def _(sp):
            sp.wait_ge(s_pads_set, 4)
            for dst, src, s in ((src_i, A["src"], s_src), (dst_i, A["dst"], s_dst)):
                sp.dma_start(dst[0:P - 1, :], src[0:(P - 1) * TE].rearrange("(p t) -> p t", t=TE)).then_inc(s, 16)
                sp.dma_start(dst[P - 1:P, 0:TE_LAST],
                             src[(P - 1) * TE:E_ALL].rearrange("(p t) -> p t", p=1)).then_inc(s, 16)
            sp.dma_start(w_nat[:, 0:6, :], A["L0_mix_Wqkv"].rearrange("(a p) c -> p a c", p=P)).then_inc(s_w, 16)
            for i, name in enumerate(("L0_gnn_W", "L0_mix_W1", "L0_mix_W2")):
                sp.dma_start(w_nat[:, 6 + 2 * i:8 + 2 * i, :],
                             A[name].rearrange("(a p) c -> p a c", p=P)).then_inc(s_w, 16)
            for i, name in enumerate(("L0_gnn_a_dst", "L0_gnn_a_src")):
                for h in range(H):
                    sp.dma_start(a_mat[HD * (h % 2):HD * (h % 2) + HD, h // 2, H * i + h:H * i + h + 1],
                                 A[name][h, :].rearrange("(d a) -> d a", a=1)).then_inc(s_misc, 16)
            sp.dma_start(b_row[:, 0:C], A["L0_gnn_b"].rearrange("(a c) -> a c", a=1)).then_inc(s_misc, 16)
            sp.dma_start(b2_row[:, :], A["L0_mix_b2"].rearrange("(a c) -> a c", a=1)).then_inc(s_misc, 16)
            for dst, name in ((b_col, "L0_gnn_b"), (b1_col, "L0_mix_b1")):
                for a in range(2):
                    sp.dma_start(dst[:, a:a + 1],
                                 A[name][a * P:(a + 1) * P].rearrange("(p a) -> p a", a=1)).then_inc(s_misc, 16)
            for i, name in enumerate(("ln1_g", "ln1_b", "ln2_g", "ln2_b")):
                sp.dma_start(ln[:, i, :], A["L0_mix_" + name].partition_broadcast(P)).then_inc(s_misc, 16)
            sp.dma_start(x[:, 0:NB - 1, :],
                         A["x"][0:(NB - 1) * P, :].rearrange("(b p) c -> p b c", p=P)).then_inc(s_x, 16)
            sp.dma_start(x[0:TAIL, NB - 1, :], A["x"][(NB - 1) * P:N, :]).then_inc(s_x, 16)
            sp.wait_ge(s_fill, 2)
            sp.dma_start(sh["list"].rearrange("(p r) w -> p r w", p=P),
                         pad_rows.bitcast(I32)).then_inc(s_filled, 16)
            sp.wait_ge(s_blk, 1)
            sp.dma_start(sh["blk_dram"].rearrange("(p r) -> p r", r=7), grp_blk_i[:, :]).then_inc(s_blkd, 16)
            sp.wait_ge(s_blkd, 16)
            sp.dma_start(sh["blk"][0:1, :], sh["blk_dram"].rearrange("(a g) -> a g", a=1)).then_inc(s_blkr, 16)
            sp.wait_ge(s_blkr, 16)
            def columns(it):
                first = 0
                for half, n in enumerate(SUBS):
                    wait_freed(sp, s_scat[half], it * (16 * n))
                    sp.dma_start(stage_pos[half][:, :], pos[:, ds(it * SUB + first, n)]).then_inc(s_staged[half], 16)
                    sp.dma_start(stage_pay[half][:, :, :], payload[:, ds(it * SUB + first, n), :])\
                        .then_inc(s_staged[half], 16)
                    first += n

            sp.wait_ge(s_pos, 1)
            first_and_rest(sp, TQ // SUB, columns)
            for quarter in range(1, QUARTERS):
                sp.wait_ge(s_pos, quarter + 1)
                with sp.Fori(quarter * (TQ // SUB), (quarter + 1) * (TQ // SUB)) as it:
                    columns(it)

        @block.gpsimd
        def _(pool):
            g = nc.gpsimd
            done = [0]

            def step(ins):
                done[0] += 1
                ins.then_inc(s_pool, 1)
                pool.wait_ge(s_pool, done[0])

            step(g.memset(ident[:, :], 0.0))
            step(g.affine_select(out=ident[:, :], in_=ident[:, :], compare_op=ALU.not_equal, fill=1.0, base=0,
                                 pattern=[[-1, P]], channel_multiplier=1))
            step(g.memset(ones_sq[:, :], 1.0))
            step(g.affine_select(out=before[:, :], in_=ones_sq[:, :], compare_op=ALU.is_gt, fill=0.0, base=0,
                                 pattern=[[1, P]], channel_multiplier=-1))
            step(g.iota(iota_row[:, :], [[1, P]], base=0, channel_multiplier=0, allow_small_or_imprecise_dtypes=True))
            step(g.iota(node_col[:, :], [[1, 1]], base=0, channel_multiplier=1, allow_small_or_imprecise_dtypes=True))
            step(g.iota(grp_no[:, :], [[1, 7]], base=0, channel_multiplier=7, allow_small_or_imprecise_dtypes=True))
            step(g.affine_select(out=tail_rows[:, :], in_=ones_sq[:, 0:1], compare_op=ALU.is_gt, fill=0.0, base=TAIL,
                                 pattern=[[0, 1]], channel_multiplier=-1))
            g.memset(ones_row[:, :], 1.0).then_inc(s_const, 1)
            g.memset(pad_rows[:, :, 0], 0.0).then_inc(s_fill, 1)
            g.memset(pad_rows[:, :, 1], NO_NODE).then_inc(s_fill, 1)
            due = [pool.alloc_register(f"due_staged{half}") for half in range(2)]
            for half in range(2):
                pool.reg_mov(due[half], 32)
            pool.wait_ge(s_filled, 16)
            with pool.Fori(0, TE // SUB) as it:
                for half, n in enumerate(SUBS):
                    pool.wait_ge(s_staged[half], due[half])
                    pool.reg_add(due[half], due[half], 32)
                    for t in range(n):
                        g.indirect_dma_start(sh["list"], bass.IndirectOffsetOnAxis(ap=stage_pos[half][:, t:t + 1], axis=0),
                                             stage_pay[half][:, t, :], None).then_inc(s_scat[half], 16)
            for half, n in enumerate(SUBS):
                pool.wait_ge(s_scat[half], 16 * n * (TE // SUB))

        @block.vector
        def _(dve):
            v = nc.vector
            done = [0]

            def step(ins):
                done[0] += 1
                ins.then_inc(s_dve, 1)
                dve.wait_ge(s_dve, done[0])

            last_t = slice(TE_LAST, TE)
            v.memset(src_i[96:P, last_t], NB * P).then_inc(s_pads_set, 1)
            v.memset(dst_i[96:P, last_t], 0).then_inc(s_pads_set, 1)
            v.memset(a_mat[:, :, :], 0.0).then_inc(s_pads_set, 1)
            v.memset(x[:, NB - 1:NBP, :], 0.0).then_inc(s_pads_set, 1)
            dve.wait_ge(s_src, 32)
            step(v.tensor_scalar(int_tmp, src_i, 7, None, ALU.logical_shift_right))
            step(v.tensor_copy(bucket, int_tmp))
            step(v.tensor_scalar(int_tmp, src_i, P - 1, None, ALU.bitwise_and))
            step(v.tensor_copy(payload[:, :, 1].bitcast(F32), int_tmp))
            dve.wait_ge(s_dst, 32)
            step(v.tensor_copy(payload[:, :, 0], dst_i))
            dve.wait_ge(s_const, 1)
            with dve.Fori(0, NBK) as b:
                v.tensor_scalar(hit, bucket, iota_row[:, ds(b, 1)], 0.0, ALU.is_equal, ALU.add,
                                accum_out=counts[:, ds(b, 1)]).then_inc(s_counts, 1)
                dve.wait_ge(s_counts, b + 1)
            dve.wait_ge(s_base, 1)
            step(v.tensor_scalar(totals[:, :], banks[7][:, 0:NBK], float(GR - 1), None, ALU.add))
            step(v.tensor_copy(grp_i[:, :], totals[:, :]))
            step(v.tensor_scalar(grp_i[:, :], grp_i[:, :], GR.bit_length() - 1, None, ALU.logical_shift_right))
            step(v.tensor_copy(totals[:, :], grp_i[:, :]))
            step(v.tensor_tensor_scan(grp_end[:, :], totals[:, :], totals[:, :], 0.0, ALU.add, ALU.bypass))
            step(v.tensor_tensor(totals[:, :], grp_end[:, :], totals[:, :], ALU.subtract))
            step(v.memset(totals[:, NB:NBK], float(NG)))
            step(v.scalar_tensor_tensor(base[:, :], totals[:, :], float(GR), banks[7][:, 64:64 + NBK], ALU.mult, ALU.add))
            step(v.tensor_scalar(carry[:, :], base[:, :], -1.0, None, ALU.add))
            ge = grp_cmp.rearrange("p (r b) -> p r b", b=NB)
            step(v.tensor_tensor(ge, grp_no[:, :].unsqueeze(2).broadcast_to([P, 7, NB]),
                                 grp_end[:, 0:NB].unsqueeze(1).broadcast_to([P, 7, NB]), ALU.is_ge))
            step(v.tensor_reduce(grp_blk[:, :], ge, AX.X, ALU.add))
            step(v.tensor_scalar(grp_blk[:, :], grp_blk[:, :], float(NB - 1), None, ALU.min))
            v.tensor_copy(grp_blk_i[:, :], grp_blk[:, :]).then_inc(s_blk, 1)
            with dve.Fori(0, QUARTERS) as quarter:
                with dve.Fori(0, NBK) as b:
                    done[0] = 0
                    dve.sem_clear(s_dve)
                    step(v.tensor_scalar(hit[:, 0:TQ], bucket[:, ds(quarter * TQ, TQ)], iota_row[:, ds(b, 1)], None,
                                         ALU.is_equal))
                    step(v.tensor_tensor_scan(running, hit[:, 0:TQ], hit[:, 0:TQ], carry[:, ds(b, 1)],
                                              ALU.add, ALU.bypass))
                    step(v.tensor_copy(carry[:, ds(b, 1)], running[:, TQ - 1:TQ]))
                    step(v.copy_predicated(places, hit[:, 0:TQ].bitcast(U16), running))
                v.tensor_copy(pos[:, ds(quarter * TQ, TQ)], places).then_inc(s_pos, 1)
                dve.wait_ge(s_pos, quarter + 1)
            done[0] = 0
            dve.sem_clear(s_dve)
            step(v.memset(valid[:, :], 1.0))
            step(v.memset(valid[:, NB - 1:NBP], 0.0))
            step(v.tensor_copy(valid[:, NB - 1:NB], tail_rows[:, :]))
            step(v.memset(kv_bd[:, :, :], 0.0))
            dve.wait_ge(s_gwc, 1)
            v.memset(banks[6][:, 0:258], 0.0).then_inc(s_kv0, 1)
            dve.wait_ge(s_x, 32)
            dve.wait_ge(s_filled, 16)

            def one_turn(it):
                done[0] = 0
                dve.sem_clear(s_dve)
                for u in range(BATCH):
                    v.bn_stats(stats[:, u, :], x[:, ds(it * BATCH + u, 1), :].rearrange("p a c -> p (a c)"))\
                        .then_inc(s_dve, 1)
                done[0] += BATCH
                dve.wait_ge(s_dve, done[0])
                for u in range(BATCH):
                    v.bn_aggr(mv[:, u, :], stats[:, u, :]).then_inc(s_dve, 1)
                done[0] += BATCH
                dve.wait_ge(s_dve, done[0])
                v.tensor_scalar(inv[:, :], mv[:, :, 1], EPS_LN, None, ALU.add).then_inc(s_var, 1)
                dve.wait_ge(s_std, it + 1)
                step(v.reciprocal(inv[:, :], std[:, :]))
                for u in range(BATCH):
                    last = v.tensor_scalar(y[:, u, :],
                                           x[:, ds(it * BATCH + u, 1), :].rearrange("p a c -> p (a c)"),
                                           mv[:, u, 0:1], inv[:, u:u + 1], ALU.subtract, ALU.mult)
                last.then_inc(s_xn, 1)
                dve.wait_ge(s_xn, it + 1)
                v.tensor_copy(xn[:, ds(it * BATCH, BATCH), :], y[:, :, :])
                for u in range(BATCH):
                    bank = banks[4 + u % 2]
                    dve.wait_ge(s_kv, it * BATCH + u + 1)
                    v.tensor_scalar(k_min[:, u % 2, :], bank[:, 0:C], 0.0, None, ALU.min).then_inc(s_kmin, 1)
                    wait_freed(dve, s_acc, it * BATCH + max(u - 1, 0))
                    v.tensor_copy(vv[:, u % 2, :, P:P + 1],
                                  valid[:, ds(it * BATCH + u, 1)].unsqueeze(1).broadcast_to([P, 2, 1])).then_inc(s_nd, 1)
                    dve.wait_ge(s_kexp, it * BATCH + u + 1)
                    dve.wait_ge(s_vc, it * BATCH + u + 1)
                    v.scalar_tensor_tensor(kk[:, u % 2, :], bank[:, 0:C], 0.0, k_exp[:, u % 2, :], ALU.max, ALU.add)\
                        .then_inc(s_kk, 1)

            first_and_rest(dve, ITERS, one_turn)

            dve.wait_ge(s_acc, NBP)
            for half in range(2):
                for j in range(4):
                    r = slice(MD * j, MD * j + MD)
                    o = half * 129
                    v.tensor_copy(kv_bd[r, half, MD * j:MD * j + MD], banks[6][r, o + MD * j:o + MD * j + MD])
                    last = v.tensor_copy(kv_bd[r, half, P + j:P + j + 1], banks[6][r, o + P:o + P + 1])
            last.then_inc(s_bd, 1)

            def one_turn(it):
                done[0] = 0
                dve.sem_clear(s_dve)

                def norm(count, gamma):
                    for u in range(BATCH):
                        v.bn_stats(stats[:, u, :], y[:, u, :]).then_inc(s_dve, 1)
                    done[0] += BATCH
                    dve.wait_ge(s_dve, done[0])
                    for u in range(BATCH):
                        v.bn_aggr(mv[:, u, :], stats[:, u, :]).then_inc(s_dve, 1)
                    done[0] += BATCH
                    dve.wait_ge(s_dve, done[0])
                    v.tensor_scalar(inv[:, :], mv[:, :, 1], EPS_LN, None, ALU.add).then_inc(s_var2, 1)
                    dve.wait_ge(s_std2, it * 2 + count)
                    step(v.reciprocal(inv[:, :], std[:, :]))
                    for u in range(BATCH):
                        last = v.tensor_scalar(y[:, u, :], y[:, u, :], mv[:, u, 0:1], inv[:, u:u + 1],
                                               ALU.subtract, ALU.mult)
                    step(last)
                    step(v.tensor_tensor(y[:, :, :], y[:, :, :],
                                         ln[:, gamma, :].unsqueeze(1).broadcast_to([P, BATCH, C]), ALU.mult))

                v.tensor_copy(y[:, :, :], xn[:, ds(it * BATCH, BATCH), :]).then_inc(s_xc, 1)
                for m in range(2):
                    dve.wait_ge(s_q, it * 2 + m + 1)
                    v.tensor_scalar(q_min[:, m, :], banks[2 + m][:, :], 0.0, None, ALU.min).then_inc(s_qmin, 1)
                for m in range(2):
                    dve.wait_ge(s_qexp, it * 2 + m + 1)
                    v.scalar_tensor_tensor(qT[:, m, :], banks[2 + m][:, :], 0.0, q_min[:, m, :], ALU.max, ALU.add)\
                        .then_inc(s_qT, 1)
                for u in range(BATCH):
                    halves = banks[4 + u][:, 0:2 * KVC].rearrange("p (a w) -> p a w", w=KVC)
                    dve.wait_ge(s_t, it * BATCH + u + 1)
                    step(v.tensor_scalar(den[:, u, :].rearrange("p (a h) -> p a h", a=2), halves[:, :, P:KVC],
                                         EPS_ATTN, None, ALU.add))
                    step(v.reciprocal(den[:, u, :], den[:, u, :]))
                    for a in range(2):
                        last = v.tensor_tensor(
                            y[:, u, a * P:(a + 1) * P].rearrange("p (h d) -> p h d", d=MD),
                            halves[:, a, 0:P].rearrange("p (h d) -> p h d", d=MD),
                            den[:, u, 4 * a:4 * a + 4].unsqueeze(2).broadcast_to([P, 4, MD]), ALU.mult)
                    step(last)
                step(v.tensor_tensor(y[:, :, :], y[:, :, :], xn[:, ds(it * BATCH, BATCH), :], ALU.add))
                norm(1, 0)
                v.tensor_tensor(x1[:, :, :], y[:, :, :], ln[:, 1, :].unsqueeze(1).broadcast_to([P, BATCH, C]), ALU.add)\
                    .then_inc(s_x1, 1)
                for u in range(BATCH):
                    dve.wait_ge(s_y2, it * BATCH + u + 1)
                    last = v.tensor_tensor(y[:, u, :], banks[4 + u][:, 0:C], x1[:, u, :], ALU.add)
                last.then_inc(s_y2r, 1)
                dve.wait_ge(s_y2r, it + 1)
                norm(2, 2)
                step(v.tensor_tensor(y[:, :, :], y[:, :, :],
                                     ln[:, 3, :].unsqueeze(1).broadcast_to([P, BATCH, C]), ALU.add))
                step(v.tensor_tensor(x[:, ds(it * BATCH, BATCH), :], x[:, ds(it * BATCH, BATCH), :], y[:, :, :], ALU.add))

            first_and_rest(dve, ITERS, one_turn)

        @block.scalar
        def _(act):
            s = nc.scalar
            for i in range(2 * NW // 512):
                act.wait_ge(s_wtr, i + 1)
                s.copy(wT[:, i // 3, 512 * (i % 3):512 * (i % 3) + 512], banks[i][:, :]).then_inc(s_wtc, 1)
            act.wait_ge(s_gw, 1)
            for k in range(2):
                s.copy(g_w[:, k, C:C + 2 * H], banks[6][:, 8 * k:8 * k + 8])
            s.copy(b_row[:, C:C + 2 * H], banks[6][0:1, 16:24])
            act.wait_ge(s_wtc, 6)
            s.copy(g_w[:, :, 0:C], wT[:, :, WG:WG + C]).then_inc(s_gwc, 1)
            def one_turn(it):
                act.wait_ge(s_var, it + 1)
                s.activation(std[:, :], inv[:, :], ACT.Sqrt).then_inc(s_std, 1)
                act.wait_ge(s_tr, it + 1)
                for k in range(2):
                    last = s.copy(xT[:, k, :], banks[k][:, :])
                last.then_inc(s_xT, 1)
                for u in range(BATCH):
                    n = it * BATCH + u
                    act.wait_ge(s_g, n + 1)
                    if u == 0:
                        wait_freed(act, s_tab, it * 16)
                        act.wait_ge(s_gwc, 1)
                    s.copy(wh[:, u, :], banks[2 + u % 2][:, 0:C + 2 * H]).then_inc(s_wh, 1)
                    act.wait_ge(s_kmin, n + 1)
                    s.activation(k_exp[:, u % 2, :], k_min[:, u % 2, :], ACT.Exp).then_inc(s_kexp, 1)
                    act.wait_ge(s_nd, n + 1)
                    s.copy(vv[:, u % 2, :, 0:P], banks[4 + u % 2][:, C:2 * C].rearrange("p (a d) -> p a d", a=2))\
                        .then_inc(s_vc, 1)
                act.wait_ge(s_wh, it * BATCH + BATCH)
                act.wait_ge(s_gwc, 1)
                act.dma_start(sh["table"][ds(it * W4, W4), :].rearrange("(b p) c -> p b c", p=P),
                              wh[:, :, 0:TB]).then_inc(s_tab, 16)
                s.copy(sh["ad"][:, ds(it * BATCH, BATCH), :], wh[:, :, C:C + H])
                s.copy(sh["t8"][:, ds(it * BATCH, BATCH), 0:H], wh[:, :, C + H:C + 2 * H])

            first_and_rest(act, ITERS, one_turn)
            def one_turn(it):
                act.wait_ge(s_tr2, it + 1)
                for k in range(2):
                    last = s.copy(xT[:, k, :], banks[k][:, :])
                last.then_inc(s_xT2, 1)
                for m in range(2):
                    act.wait_ge(s_qmin, it * 2 + m + 1)
                    s.activation(q_min[:, m, :], q_min[:, m, :], ACT.Exp).then_inc(s_qexp, 1)
                act.wait_ge(s_var2, it * 2 + 1)
                s.activation(std[:, :], inv[:, :], ACT.Sqrt).then_inc(s_std2, 1)
                act.wait_ge(s_tr3, it + 1)
                for k in range(2):
                    last = s.copy(xT[:, k, :], banks[k][:, :])
                last.then_inc(s_xT3, 1)
                for m in range(2):
                    act.wait_ge(s_h, it * 2 + m + 1)
                    s.activation(qT[:, m, :], banks[2 + m][:, :], ACT.Gelu, bias=b1_col[:, m:m + 1]).then_inc(s_h1, 1)
                act.wait_ge(s_var2, it * 2 + 2)
                s.activation(std[:, :], inv[:, :], ACT.Sqrt).then_inc(s_std2, 1)

            first_and_rest(act, ITERS, one_turn)
            act.wait_ge(s_tab, 16 * ITERS)

        @block.tensor
        def _(pe):
            t = nc.tensor
            pe.wait_ge(s_const, 1)
            pe.wait_ge(s_w, 64)
            for i in range(2 * NW // 512):
                for j in range(4):
                    chunk = 4 * (i % 3) + j
                    last = t.transpose(banks[i][:, P * j:P * j + P], w_nat[:, chunk, P * (i // 3):P * (i // 3) + P],
                                       ident[:, :])
                last.then_inc(s_wtr, 1)
            pe.wait_ge(s_misc, 16 * 18)
            for k in range(2):
                for o in range(2):
                    t.matmul(banks[6][:, 8 * k:8 * k + 8], w_nat[:, 6 + o, P * k:P * k + P], a_mat[:, o, :],
                             start=o == 0, stop=o == 1)
            for o in range(2):
                last = t.matmul(banks[6][0:1, 16:24], b_col[:, o:o + 1], a_mat[:, o, :], start=o == 0, stop=o == 1)
            last.then_inc(s_gw, 1)
            pe.wait_ge(s_counts, NBK)
            t.matmul(banks[7][:, 0:NBK], ones_sq[:, :], counts[:, :], start=True, stop=True)
            t.matmul(banks[7][:, 64:64 + NBK], before[:, :], counts[:, :], start=True, stop=True).then_inc(s_base, 1)
            pe.wait_ge(s_gwc, 1)
            pe.wait_ge(s_kv0, 1)
            def one_turn(it):
                pe.wait_ge(s_xn, it + 1)
                for k in range(2):
                    for u in range(BATCH):
                        last = t.transpose(banks[k][:, P * u:P * u + P], y[:, u, P * k:P * k + P], ident[:, :])
                last.then_inc(s_tr, 1)
                pe.wait_ge(s_xT, it + 1)
                for u in range(BATCH):
                    n = it * BATCH + u
                    wait_freed(pe, s_wh, it * BATCH + max(u - 1, 0))
                    for k in range(2):
                        t.matmul(banks[2 + u % 2][:, 0:C + 2 * H], xT[:, k, P * u:P * u + P], g_w[:, k, :],
                                 start=k == 0, stop=False)
                    t.matmul(banks[2 + u % 2][:, 0:C + 2 * H], ones_row[:, :], b_row[:, :], start=False, stop=True)\
                        .then_inc(s_g, 1)
                    wait_freed(pe, s_kk, it * BATCH + max(u - 1, 0))
                    wait_freed(pe, s_vc, it * BATCH + max(u - 1, 0))
                    for k in range(2):
                        last = t.matmul(banks[4 + u % 2][:, :], xT[:, k, P * u:P * u + P], wT[:, k, C:3 * C],
                                        start=k == 0, stop=k == 1)
                    last.then_inc(s_kv, 1)
                    pe.wait_ge(s_kk, n + 1)
                    pe.wait_ge(s_vc, n + 1)
                    for a in range(2):
                        last = t.matmul(banks[6][:, 129 * a:129 * a + 129], kk[:, u % 2, P * a:P * a + P],
                                        vv[:, u % 2, a, 0:129], start=False, stop=False, skip_group_check=True)
                    last.then_inc(s_acc, 1)

            first_and_rest(pe, ITERS, one_turn)
            pe.wait_ge(s_bd, 1)
            def one_turn(it):
                pe.wait_ge(s_xc, it + 1)
                for k in range(2):
                    for u in range(BATCH):
                        last = t.transpose(banks[k][:, P * u:P * u + P], y[:, u, P * k:P * k + P], ident[:, :])
                last.then_inc(s_tr2, 1)
                pe.wait_ge(s_xT2, it + 1)
                for m in range(2):
                    for k in range(2):
                        last = t.matmul(banks[2 + m][:, :], wT[:, k, P * m:P * m + P], xT[:, k, :],
                                        start=k == 0, stop=k == 1)
                    last.then_inc(s_q, 1)
                pe.wait_ge(s_qT, it * 2 + 2)
                wait_freed(pe, s_y2r, it)
                for u in range(BATCH):
                    for a in range(2):
                        last = t.matmul(banks[4 + u][:, KVC * a:KVC * a + KVC], qT[:, a, P * u:P * u + P],
                                        kv_bd[:, a, :], start=True, stop=True)
                    last.then_inc(s_t, 1)
                pe.wait_ge(s_x1, it + 1)
                for k in range(2):
                    for u in range(BATCH):
                        last = t.transpose(banks[k][:, P * u:P * u + P], x1[:, u, P * k:P * k + P], ident[:, :])
                last.then_inc(s_tr3, 1)
                pe.wait_ge(s_xT3, it + 1)
                for m in range(2):
                    for k in range(2):
                        last = t.matmul(banks[2 + m][:, :], wT[:, k, W1 + P * m:W1 + P * m + P], xT[:, k, :],
                                        start=k == 0, stop=k == 1)
                    last.then_inc(s_h, 1)
                pe.wait_ge(s_h1, it * 2 + 2)
                for u in range(BATCH):
                    for k in range(2):
                        t.matmul(banks[4 + u][:, 0:C], qT[:, k, P * u:P * u + P], wT[:, k, W2:W2 + C],
                                 start=k == 0, stop=False)
                    t.matmul(banks[4 + u][:, 0:C], ones_row[:, :], b2_row[:, :], start=False, stop=True)\
                        .then_inc(s_y2, 1)

            first_and_rest(pe, ITERS, one_turn)


def stage_edges(nc, A, sh):
    TILES = GROUPS * G
    QUAD = 4
    ctx = ExitStack()
    with ctx:
        sb = lambda name, shape, dt=F32: ctx.enter_context(nc.sbuf_tensor(name, shape, dt))
        sem = lambda name: ctx.enter_context(nc.semaphore(name))
        sems = lambda name, n: [sem(f"{name}{i}") for i in range(n)]
        banks = [ctx.enter_context(nc.psum_tensor(f"bank2_{i}", [P, 512], F32)) for i in range(8)]
        acc, t8, ad, blk = sh["acc"], sh["t8"], sh["ad"], sh["blk"]
        iota_row, node_col = sh["iota_row"], sh["node_col"]
        col = [sb(f"col{i}", [P, GROUPS, G, 2], I32) for i in range(2)]
        row = [sb(f"row{i}", [1, TILES * P, 2], I32) for i in range(2)]
        ones_bf = sb("ones_bf", [1, P], BF16)
        gathered = sb("gathered", [P, 2, TILES, TB])
        weighted = sb("weighted", [P, 2, TILES, TB])
        onehot = sb("onehot", [P, 2, TILES, P])
        dist = sb("dist", [P, 2, QUAD * P])
        onehot_t = sb("onehot_t", [P, 2, TILES, P])
        z = sb("z", [P, 2, TILES, H])
        e = sb("e", [P, 2, TILES, H])
        minus_node = sb("minus_node", [P, 1])
        ad_max = sb("ad_max", [P, H])
        ad_top = sb("ad_top", [P, H])

        s_col, s_row, s_gath, s_sel, s_as, s_d, s_p, s_mul, s_main = (
            sems(n, 2) for n in ("s_col", "s_row", "s_gath", "s_sel", "s_as", "s_d", "s_p", "s_mul", "s_main"))
        s_sum = sems("s_sum", GROUPS)
        s_max, s_top, s_ready, s_bc, s_dist, s_ot, s_zr = map(sem, (
            "s_max", "s_top", "s_ready", "s_bc", "s_dist", "s_ot", "s_zr"))
        s_dve = sem("s_dve2")
        block = ctx.enter_context(nc.Block())

        @block.sync
        def _(sp):
            sp.wait_ge(s_ready, 1)
            def rows(it):
                for h in range(2):
                    part = sh["list"][ds((it * 2 + h) * (TILES * P), TILES * P), :]
                    wait_freed(sp, s_gath[h], it * (16 * TILES))
                    wait_freed(sp, s_sel[h], it)
                    sp.wait_ge(s_ready, 1)
                    sp.dma_start(col[h][:, :, :, :], part.rearrange("(g p k) w -> p g (k w)", g=GROUPS, p=P))\
                        .then_inc(s_col[h], 16)
                    wait_freed(sp, s_bc, it * 4 + 2 * h)
                    sp.wait_ge(s_ready, 1)
                    sp.dma_start(row[h][:, :, :], part.rearrange("(a e) w -> a e w", a=1)).then_inc(s_row[h], 16)

            first_and_rest(sp, EIT, rows)

        @block.gpsimd
        def _(pool):
            g = nc.gpsimd
            pool.wait_ge(s_max, 1)
            g.partition_all_reduce(ad_top[:, :], ad_max[:, :], P, sh["RMAX"]).then_inc(s_top, 1)
            due = [pool.alloc_register(f"due_col{h}") for h in range(2)]
            for h in range(2):
                pool.reg_mov(due[h], 16)
            def gathers(it):
                for h in range(2):
                    wait_freed(pool, s_mul[h], it * GROUPS)
                    pool.wait_ge(s_col[h], due[h])
                    pool.reg_add(due[h], due[h], 16)
                    for t in range(TILES):
                        g.indirect_dma_start(
                            gathered[:, h, t, :], None, sh["table"],
                            bass.IndirectOffsetOnAxis(ap=col[h][:, t // G, t % G, 0:1], axis=0))\
                            .then_inc(s_gath[h], 16)

            first_and_rest(pool, EIT, gathers)

        @block.tensor
        def _(pe):
            t = nc.tensor

            def spread(it, h):
                pe.wait_ge(s_row[h], 16 * it + 16)
                for q in range(2):
                    wait_freed(pe, s_dist, it * 4 + 2 * h)
                    words = row[h][:, :, :].bitcast(BF16).rearrange("a (g p k) w -> a g k p w", g=GROUPS, p=P)
                    t.matmul(banks[q][:, :], ones_bf[:, :], words[:, 2 * q:2 * q + 2, :, :, 3], start=True, stop=True)\
                        .then_inc(s_bc, 1)

            def by_node(it, h):
                wait_freed(pe, s_zr, it * 2 + h)
                pe.wait_ge(s_ot, it * 4 + 2 * h + 2)
                for g in range(GROUPS):
                    b = pe.value_load(blk[0:1, ds((it * 2 + h) * GROUPS + g, 1)], min_val=0, max_val=NB - 1)
                    for k in range(G):
                        tile = g * G + k
                        last = t.matmul(banks[2 + h][:, 8 * tile:8 * tile + 8], onehot_t[:, h, tile, :],
                                        t8[:, ds(b, 1), :].rearrange("p a w -> p (a w)"), start=True, stop=True)
                last.then_inc(s_as[h], 1)

            def sums(it, h, groups):
                for g in groups:
                    pe.wait_ge(s_mul[h], it * GROUPS + g + 1)
                    pe.wait_ge(s_p[h], it + 1)
                    wait_freed(pe, s_sum[g], it * 2 + h)
                    for k in range(G):
                        last = t.matmul(banks[4 + g][:, 0:TB], onehot[:, h, g * G + k, :],
                                        weighted[:, h, g * G + k, :], start=k == 0, stop=k == G - 1)
                    last.then_inc(s_main[h], 1)

            def body(it, h, more=True):
                nxt = (it, 1) if h == 0 else (it + 1, 0)
                if more:
                    spread(*nxt)
                sums(it, h, (0, 1))
                if more:
                    by_node(*nxt)
                sums(it, h, (2, 3))

            pe.wait_ge(s_ready, 1)
            spread(0, 0)
            by_node(0, 0)
            body(0, 0)
            body(0, 1)
            with pe.Fori(1, EIT - 1) as it:
                body(it, 0)
                body(it, 1)
            body(EIT - 1, 0)
            body(EIT - 1, 1, more=False)

        @block.scalar
        def _(act):
            s = nc.scalar
            act.wait_ge(s_ready, 1)
            def one_turn(it):
                for h in range(2):
                    for q in range(2):
                        n = it * 4 + 2 * h + q
                        act.wait_ge(s_bc, n + 1)
                        s.activation(dist[:, q, :], banks[q][:, :], ACT.Abs, bias=minus_node[:, 0:1])\
                            .then_inc(s_dist, 1)
                        act.wait_ge(s_dist, n + 1)
                        wait_freed(act, s_as[h], it)
                        s.activation(onehot_t[:, h, q * QUAD:(q + 1) * QUAD, :].rearrange("p t e -> p (t e)"),
                                     dist[:, q, :], ACT.Relu, bias=1.0, scale=-1.0).then_inc(s_ot, 1)
                    act.wait_ge(s_d[h], it + 1)
                    wait_freed(act, s_main[h], it * GROUPS)
                    s.activation(weighted[:, h, :, C:TB], e[:, h, :, :], ACT.Exp).then_inc(s_p[h], 1)

            first_and_rest(act, EIT, one_turn)

        @block.vector
        def _(dve):
            v = nc.vector
            done = [0]

            def step(ins):
                done[0] += 1
                ins.then_inc(s_dve, 1)
                dve.wait_ge(s_dve, done[0])

            v.tensor_reduce(ad_max[:, :], ad[:, 0:NB, :].rearrange("p b h -> p h b"), AX.X, ALU.max).then_inc(s_max, 1)
            v.memset(acc[:, :, :], 0.0)
            v.memset(ones_bf[:, :], 1.0)
            v.tensor_scalar(minus_node[:, :], node_col[:, :], -1.0, None, ALU.mult)
            dve.wait_ge(s_top, 1)
            step(v.tensor_tensor(t8[:, :, H:2 * H], t8[:, :, 0:H],
                                 ad_top[:, :].unsqueeze(1).broadcast_to([P, NBP, H]), ALU.add))
            v.scalar_tensor_tensor(t8[:, :, H:2 * H], t8[:, :, H:2 * H], SLOPE, t8[:, :, H:2 * H],
                                   ALU.mult, ALU.max).then_inc(s_ready, 1)

            def weigh(it, h):
                wait_freed(dve, s_main[h], it * GROUPS)
                dve.wait_ge(s_col[h], 16 * it + 16)
                within = col[h][:, :, :, :].rearrange("p g k w -> p (g k) w")[:, :, 1:2].bitcast(F32)
                v.tensor_tensor(onehot[:, h, :, :], iota_row[:, :].unsqueeze(1).broadcast_to([P, TILES, P]),
                                within.broadcast_to([P, TILES, P]), ALU.is_equal).then_inc(s_sel[h], 1)
                dve.wait_ge(s_gath[h], it * (16 * TILES) + 16 * TILES)
                dve.wait_ge(s_as[h], it + 1)
                from_node = banks[2 + h][:, 0:8 * TILES].rearrange("p (t w) -> p t w", w=8)
                step(v.tensor_tensor(z[:, h, :, :], gathered[:, h, :, C:TB], from_node[:, :, 0:H], ALU.add))
                step(v.scalar_tensor_tensor(z[:, h, :, :], z[:, h, :, :], SLOPE, z[:, h, :, :], ALU.mult, ALU.max))
                v.tensor_tensor(e[:, h, :, :], z[:, h, :, :], from_node[:, :, H:2 * H], ALU.subtract)\
                    .then_inc(s_d[h], 1)
                dve.wait_ge(s_d[h], it + 1)
                v.tensor_copy(z[:, h, 0:1, 0:1], z[:, h, 0:1, 0:1]).then_inc(s_zr, 1)

            def product(it, h):
                dve.wait_ge(s_p[h], it + 1)
                for g in range(GROUPS):
                    tiles = slice(g * G, g * G + G)
                    v.tensor_tensor(weighted[:, h, tiles, 0:C].rearrange("p k (a d) -> p k a d", d=HD),
                                    gathered[:, h, tiles, 0:C].rearrange("p k (a d) -> p k a d", d=HD),
                                    weighted[:, h, tiles, C:TB].unsqueeze(3).broadcast_to([P, G, H, HD]),
                                    ALU.mult).then_inc(s_mul[h], 1)

            def add(it, h, groups):
                for g in groups:
                    b = dve.value_load(blk[0:1, ds((it * 2 + h) * GROUPS + g, 1)], min_val=0, max_val=NB - 1)
                    dve.wait_ge(s_main[h], it * GROUPS + g + 1)
                    dve.wait_ge(s_ready, 1)
                    place = acc[:, ds(b, 1), :].rearrange("p a c -> p (a c)")
                    v.tensor_tensor(place, place, banks[4 + g][:, 0:TB], ALU.add).then_inc(s_sum[g], 1)
                    dve.wait_ge(s_sum[g], it * 2 + h + 1)

            def body(it, h, more=True):
                nxt = (it, 1) if h == 0 else (it + 1, 0)
                if more:
                    weigh(*nxt)
                add(it, h, (0, 1))
                if more:
                    product(*nxt)
                add(it, h, (2, 3))

            weigh(0, 0)
            product(0, 0)
            body(0, 0)
            body(0, 1)
            with dve.Fori(1, EIT - 1) as it:
                done[0] = 0
                dve.sem_clear(s_dve)
                body(it, 0)
                body(it, 1)
            body(EIT - 1, 0)
            body(EIT - 1, 1, more=False)


def stage_feed_forward(nc, A, sh):
    ctx = ExitStack()
    with ctx:
        sb = lambda name, shape, dt=F32: ctx.enter_context(nc.sbuf_tensor(name, shape, dt))
        sem = lambda name: ctx.enter_context(nc.semaphore(name))
        banks = [ctx.enter_context(nc.psum_tensor(f"bank3_{i}", [P, 512], F32)) for i in range(8)]
        x, acc = sh["x"], sh["acc"]
        ident, ones_row = sh["ident"], sh["ones_row"]
        CH = 7
        assert NB % CH == 0
        sW1, sW2, sW3 = sb("sW1", [P, 2, SH1]), sb("sW2", [P, 2, SH2]), sb("sW3", [P, C])
        eW1, eW2, eW3 = sb("eW1", [P, NE, 2, EH1]), sb("eW2", [P, NE, EH2]), sb("eW3", [P, 2, C])
        sb1, sb2, sb3 = sb("sb1", [P, 2]), sb("sb2", [P, 1]), sb("sb3", [1, C])
        eb1, eb2, eb3 = sb("eb1", [P, NE]), sb("eb2", [P, 2]), sb("eb3", [NE, C])
        gW, gb = sb("gW", [P, 2, NE]), sb("gb", [1, NE])
        expert_rows = sb("expert_rows", [NE, 2 * P])
        lower = sb("lower", [P, NE, NE])
        recip = sb("recip", [P, CH, H])
        quot = sb("quot", [P, CH, C])
        stats, mv = sb("stats3", [P, BATCH, 6]), sb("mv3", [P, BATCH, 2])
        std, inv = sb("std3", [P, BATCH]), sb("inv3", [P, BATCH])
        xf = sb("xf", [P, BATCH, C])
        xT = sb("xT3", [P, 2, W4])
        top = sb("top", [P, BATCH])
        gate = sb("gate", [P, BATCH, NE])
        gate_e = sb("gate_e", [P, BATCH, NE])
        cmp = sb("cmp", [P, BATCH, NE, NE])
        cmp2 = sb("cmp2", [P, BATCH, NE, NE])
        wgt = sb("wgt", [P, BATCH, NE])
        wT = sb("wT3", [NE, W4])
        h1, h2 = sb("h1", [P, 2, W4]), sb("h2", [P, W4])
        he1, he2 = sb("he1", [P, NE, W4]), sb("he2", [P, 2, W4])
        (s_w, s_exp, s_var, s_std, s_xf, s_tr, s_xT, s_lg, s_lgs, s_ex, s_ga, s_ga2, s_wg, s_wt, s_wT) = map(sem, (
            "f_w", "f_exp", "f_var", "f_std", "f_xf", "f_tr", "f_xT", "f_lg", "f_lgs", "f_ex", "f_ga", "f_ga2",
            "f_wg", "f_wt", "f_wT"))
        (s_p1, s_h1, s_p2, s_h2, s_q1, s_he1, s_q2, s_he2, s_wb, s_hw, s_o, s_x, s_out) = map(sem, (
            "f_p1", "f_h1", "f_p2", "f_h2", "f_q1", "f_he1", "f_q2", "f_he2", "f_wb", "f_hw", "f_o", "f_x", "f_out"))
        s_dve, s_pool, s_set = sem("f_dve"), sem("f_pool"), sem("f_set")
        block = ctx.enter_context(nc.Block())

        @block.sync
        def _(sp):
            loads = [(sW1[:, :, :], A["L0_ffn_sW1"].rearrange("(k p) o -> p k o", p=P)),
                     (sW2[:, :, :], A["L0_ffn_sW2"].rearrange("(k p) o -> p k o", p=P)),
                     (sW3[:, :], A["L0_ffn_sW3"]),
                     (eW2[:, :, :], A["L0_ffn_eW2"].rearrange("e h g -> h e g")),
                     (eW3[:, :, :], A["L0_ffn_eW3"].rearrange("(a e) g o -> (e g) a o", e=2)),
                     (sb2[:, :], A["L0_ffn_sb2"].rearrange("(p a) -> p a", a=1)),
                     (sb3[:, :], A["L0_ffn_sb3"].rearrange("(a o) -> a o", a=1)),
                     (eb3[:, :], A["L0_ffn_eb3"]),
                     (gb[:, :], A["L0_ffn_gb"].rearrange("(a o) -> a o", a=1))]
            for e in range(NE):
                loads.append((eW1[:, e, :, :], A["L0_ffn_eW1"][e].rearrange("(k p) h -> p k h", p=P)))
                loads.append((eb1[:, e:e + 1], A["L0_ffn_eb1"][e].rearrange("(p a) -> p a", a=1)))
                loads.append((eb2[64 * (e % 2):64 * (e % 2) + 64, e // 2:e // 2 + 1],
                              A["L0_ffn_eb2"][e].rearrange("(p a) -> p a", a=1)))
            for k in range(2):
                loads.append((sb1[:, k:k + 1], A["L0_ffn_sb1"][k * P:k * P + P].rearrange("(p a) -> p a", a=1)))
                loads.append((gW[:, k, :], A["L0_ffn_gW"][k * P:k * P + P, :]))
            assert len(loads) == LOADS3
            for dst, src in loads:
                sp.dma_start(dst, src).then_inc(s_w, 16)
            with sp.Fori(0, ITERS - 1) as it:
                sp.wait_ge(s_x, it * BATCH + BATCH)
                sp.wait_ge(s_w, 16 * LOADS3)
                sp.dma_start(A["out"][ds(it * W4, W4), :].rearrange("(b p) c -> p b c", p=P),
                             x[:, ds(it * BATCH, BATCH), :]).then_inc(s_out, 16)
            sp.wait_ge(s_x, NBP)
            sp.dma_start(A["out"][(NB - 1) * P:N, :], x[0:TAIL, NB - 1, :]).then_inc(s_out, 16)
            sp.wait_ge(s_out, 16 * ITERS)

        @block.gpsimd
        def _(pool):
            g = nc.gpsimd
            g.memset(expert_rows[:, :], 1.0).then_inc(s_pool, 1)
            pool.wait_ge(s_pool, 1)
            g.affine_select(out=expert_rows[:, :], in_=expert_rows[:, :], compare_op=ALU.is_ge, fill=0.0, base=0,
                            pattern=[[1, NE * EH2]], channel_multiplier=-EH2).then_inc(s_pool, 1)
            pool.wait_ge(s_pool, 2)
            g.affine_select(out=expert_rows[:, :], in_=expert_rows[:, :], compare_op=ALU.is_gt, fill=0.0, base=EH2,
                            pattern=[[-1, NE * EH2]], channel_multiplier=EH2).then_inc(s_set, 1)
            g.memset(lower[:, :, :], 1.0).then_inc(s_pool, 1)
            pool.wait_ge(s_pool, 3)
            g.affine_select(out=lower[:, :, :], in_=lower[:, :, :], compare_op=ALU.is_gt, fill=0.0, base=0,
                            pattern=[[1, NE], [-1, NE]], channel_multiplier=0).then_inc(s_set, 1)

        @block.vector
        def _(dve):
            v = nc.vector
            done = [0]

            def step(ins):
                done[0] += 1
                ins.then_inc(s_dve, 1)
                dve.wait_ge(s_dve, done[0])

            with dve.Fori(0, NB // CH) as i:
                done[0] = 0
                dve.sem_clear(s_dve)
                part = acc[:, ds(i * CH, CH), :]
                step(v.tensor_scalar(recip[:, :, :], part[:, :, C:TB], 1e-37, None, ALU.max))
                step(v.reciprocal(recip[:, :, :], recip[:, :, :]))
                step(v.tensor_tensor(quot[:, :, :].rearrange("p b (a d) -> p b a d", d=HD),
                                     part[:, :, 0:C].rearrange("p b (a d) -> p b a d", d=HD),
                                     recip[:, :, :].unsqueeze(3).broadcast_to([P, CH, H, HD]), ALU.mult))
                step(v.tensor_tensor(x[:, ds(i * CH, CH), :], x[:, ds(i * CH, CH), :], quot[:, :, :], ALU.add))
            dve.wait_ge(s_set, 2)
            def one_turn(it):
                done[0] = 0
                dve.sem_clear(s_dve)
                for u in range(BATCH):
                    v.bn_stats(stats[:, u, :], x[:, ds(it * BATCH + u, 1), :].rearrange("p a c -> p (a c)"))\
                        .then_inc(s_dve, 1)
                done[0] += BATCH
                dve.wait_ge(s_dve, done[0])
                for u in range(BATCH):
                    v.bn_aggr(mv[:, u, :], stats[:, u, :]).then_inc(s_dve, 1)
                done[0] += BATCH
                dve.wait_ge(s_dve, done[0])
                v.tensor_scalar(inv[:, :], mv[:, :, 1], EPS_LN, None, ALU.add).then_inc(s_var, 1)
                dve.wait_ge(s_std, it + 1)
                step(v.reciprocal(inv[:, :], std[:, :]))
                for u in range(BATCH):
                    last = v.tensor_scalar(xf[:, u, :], x[:, ds(it * BATCH + u, 1), :].rearrange("p a c -> p (a c)"),
                                           mv[:, u, 0:1], inv[:, u:u + 1], ALU.subtract, ALU.mult)
                last.then_inc(s_xf, 1)
                dve.wait_ge(s_lg, it + 1)
                logits = banks[7][:, 0:BATCH * NE].rearrange("p (u e) -> p u e", e=NE)
                step(v.tensor_reduce(top[:, :], logits, AX.X, ALU.max))
                v.tensor_tensor(gate[:, :, :], logits, top[:, :].unsqueeze(2).broadcast_to([P, BATCH, NE]),
                                ALU.subtract).then_inc(s_lgs, 1)
                dve.wait_ge(s_ex, it + 1)
                step(v.tensor_reduce(top[:, :], gate_e[:, :, :], AX.X, ALU.add))
                step(v.reciprocal(top[:, :], top[:, :]))
                v.tensor_tensor(gate[:, :, :], gate_e[:, :, :], top[:, :].unsqueeze(2).broadcast_to([P, BATCH, NE]),
                                ALU.mult).then_inc(s_ga, 1)
                dve.wait_ge(s_ga, it + 1)
                mine = gate[:, :, :].unsqueeze(3).broadcast_to([P, BATCH, NE, NE])
                others = gate[:, :, :].unsqueeze(2).broadcast_to([P, BATCH, NE, NE])
                step(v.tensor_tensor(cmp2[:, :, :, :], others, mine, ALU.is_equal))
                step(v.tensor_tensor(cmp2[:, :, :, :], cmp2[:, :, :, :],
                                     lower[:, :, :].unsqueeze(1).broadcast_to([P, BATCH, NE, NE]), ALU.mult))
                step(v.tensor_tensor(cmp[:, :, :, :], others, mine, ALU.is_gt))
                step(v.tensor_tensor(cmp[:, :, :, :], cmp[:, :, :, :], cmp2[:, :, :, :], ALU.add))
                step(v.tensor_reduce(wgt[:, :, :], cmp[:, :, :, :], AX.X, ALU.add))
                dve.wait_ge(s_ga2, it + 1)
                step(v.scalar_tensor_tensor(wgt[:, :, :], wgt[:, :, :], 1.5, gate_e[:, :, :], ALU.is_lt, ALU.mult))
                step(v.tensor_reduce(top[:, :], wgt[:, :, :], AX.X, ALU.add))
                step(v.reciprocal(top[:, :], top[:, :]))
                v.tensor_tensor(wgt[:, :, :], wgt[:, :, :], top[:, :].unsqueeze(2).broadcast_to([P, BATCH, NE]),
                                ALU.mult).then_inc(s_wg, 1)
                for a in range(2):
                    dve.wait_ge(s_he2, it * 2 + a + 1)
                    dve.wait_ge(s_wb, it * 2 + a + 1)
                    v.tensor_tensor(he2[:, a, :], he2[:, a, :], banks[a][:, :], ALU.mult).then_inc(s_hw, 1)
                for u in range(BATCH):
                    dve.wait_ge(s_o, it * BATCH + u + 1)
                    dve.wait_ge(s_set, 2)
                    xu = x[:, ds(it * BATCH + u, 1), :].rearrange("p a c -> p (a c)")
                    v.tensor_tensor(xu, xu, banks[2 + u % 2][:, 0:C], ALU.add).then_inc(s_x, 1)

            first_and_rest(dve, ITERS, one_turn)

        @block.scalar
        def _(act):
            s = nc.scalar
            act.wait_ge(s_w, 16 * LOADS3)
            def one_turn(it):
                act.wait_ge(s_var, it + 1)
                s.activation(std[:, :], inv[:, :], ACT.Sqrt).then_inc(s_std, 1)
                act.wait_ge(s_tr, it + 1)
                for k in range(2):
                    last = s.copy(xT[:, k, :], banks[k][:, :])
                last.then_inc(s_xT, 1)
                act.wait_ge(s_lgs, it + 1)
                s.activation(gate_e[:, :, :], gate[:, :, :], ACT.Exp).then_inc(s_ex, 1)
                act.wait_ge(s_ga, it + 1)
                s.activation(gate_e[:, :, :], gate[:, :, :], ACT.Exp).then_inc(s_ga2, 1)
                for m in range(2):
                    act.wait_ge(s_p1, it * 2 + m + 1)
                    s.activation(h1[:, m, :], banks[2 + m][:, :], ACT.Relu, bias=sb1[:, m:m + 1]).then_inc(s_h1, 1)
                act.wait_ge(s_p2, it + 1)
                s.activation(h2[:, :], banks[4][:, :], ACT.Relu, bias=sb2[:, 0:1]).then_inc(s_h2, 1)
                for e in range(NE):
                    act.wait_ge(s_q1, it * NE + e + 1)
                    s.activation(he1[:, e, :], banks[2 + e % 2][:, :], ACT.Relu, bias=eb1[:, e:e + 1])\
                        .then_inc(s_he1, 1)
                for a in range(2):
                    act.wait_ge(s_q2, it * 2 + a + 1)
                    s.activation(he2[:, a, :], banks[5 + a][:, :], ACT.Relu, bias=eb2[:, a:a + 1]).then_inc(s_he2, 1)
                act.wait_ge(s_wt, it + 1)
                s.copy(wT[:, :], banks[4][0:NE, :]).then_inc(s_wT, 1)

            first_and_rest(act, ITERS, one_turn)

        @block.tensor
        def _(pe):
            t = nc.tensor
            pe.wait_ge(s_w, 16 * LOADS3)
            pe.wait_ge(s_set, 2)
            def one_turn(it):
                pe.wait_ge(s_xf, it + 1)
                wait_freed(pe, s_hw, it * 2)
                for k in range(2):
                    for u in range(BATCH):
                        last = t.transpose(banks[k][:, P * u:P * u + P], xf[:, u, P * k:P * k + P], ident[:, :])
                last.then_inc(s_tr, 1)
                pe.wait_ge(s_xT, it + 1)
                for u in range(BATCH):
                    for k in range(2):
                        t.matmul(banks[7][:, NE * u:NE * u + NE], xT[:, k, P * u:P * u + P], gW[:, k, :],
                                 start=k == 0, stop=False)
                    last = t.matmul(banks[7][:, NE * u:NE * u + NE], ones_row[:, :], gb[:, :], start=False, stop=True)
                last.then_inc(s_lg, 1)
                wait_freed(pe, s_x, it * BATCH)
                for m in range(2):
                    for k in range(2):
                        last = t.matmul(banks[2 + m][:, :], sW1[:, k, P * m:P * m + P], xT[:, k, :],
                                        start=k == 0, stop=k == 1)
                    last.then_inc(s_p1, 1)
                pe.wait_ge(s_h1, it * 2 + 2)
                for k in range(2):
                    last = t.matmul(banks[4][:, :], sW2[:, k, :], h1[:, k, :], start=k == 0, stop=k == 1)
                last.then_inc(s_p2, 1)
                for e in range(NE):
                    if e >= 2:
                        pe.wait_ge(s_he1, it * NE + e - 1)
                    for k in range(2):
                        last = t.matmul(banks[2 + e % 2][:, :], eW1[:, e, k, :], xT[:, k, :],
                                        start=k == 0, stop=k == 1)
                    last.then_inc(s_q1, 1)
                for e in range(NE):
                    pe.wait_ge(s_he1, it * NE + e + 1)
                    last = t.matmul(banks[5 + e // 2][64 * (e % 2):64 * (e % 2) + 64, :], eW2[:, e, :], he1[:, e, :],
                                    start=True, stop=True)
                    if e % 2:
                        last.then_inc(s_q2, 1)
                pe.wait_ge(s_wg, it + 1)
                pe.wait_ge(s_h2, it + 1)
                for u in range(BATCH):
                    last = t.transpose(banks[4][0:NE, P * u:P * u + P], wgt[:, u, :], ident[:, :])
                last.then_inc(s_wt, 1)
                pe.wait_ge(s_wT, it + 1)
                for a in range(2):
                    t.matmul(banks[a][:, :], expert_rows[:, P * a:P * a + P], wT[:, :], start=True, stop=True)\
                        .then_inc(s_wb, 1)
                pe.wait_ge(s_hw, it * 2 + 2)
                for u in range(BATCH):
                    if u >= 2:
                        pe.wait_ge(s_x, it * BATCH + u - 1)
                    o = banks[2 + u % 2][:, 0:C]
                    us = slice(P * u, P * u + P)
                    t.matmul(o, h2[:, us], sW3[:, :], start=True, stop=False)
                    for a in range(2):
                        t.matmul(o, he2[:, a, us], eW3[:, a, :], start=False, stop=False)
                    t.matmul(o, wT[:, us], eb3[:, :], start=False, stop=False)
                    t.matmul(o, ones_row[:, :], sb3[:, :], start=False, stop=True).then_inc(s_o, 1)

            first_and_rest(pe, ITERS, one_turn)


LOADS3 = 9 + 3 * NE + 4


def graph_layer(nc, A):
    ctx = ExitStack()
    with ctx:
        sb = lambda name, shape, dt=F32: ctx.enter_context(nc.sbuf_tensor(name, shape, dt))
        x = sb("x_all", [P, NBP, C])
        xn = sb("xn_all", [P, NBP, C])
        sh = {
            "x": x, "xn": xn,
            "acc": xn[:, :, :].rearrange("p b c -> p (b c)")[:, 0:NB * TB].rearrange("p (b c) -> p b c", c=TB),
            "ident": sb("ident", [P, P]), "iota_row": sb("iota_row", [P, P]), "ones_row": sb("ones_row", [1, P]),
            "node_col": sb("node_col", [P, 1]),
            "t8": sb("t8", [P, NBP, 2 * H]), "ad": sb("ad", [P, NBP, H]), "blk": sb("blk", [1, P * 7], I32),
            "table": nc.dram_tensor("table", (NBP * P, TB), F32, kind="Internal").ap(),
            "list": nc.dram_tensor("edge_list", (LIST, 2), I32, kind="Internal").ap(),
            "blk_dram": nc.dram_tensor("blk_dram", (P * 7,), I32, kind="Internal").ap(),
            "RMAX": bass.bass_isa.ReduceOp.max,
        }
        stage_sort_and_mix(nc, A, sh)
        stage_edges(nc, A, sh)
        stage_feed_forward(nc, A, sh)


_INS = ["x", "src", "dst", "L0_gnn_W", "L0_gnn_b", "L0_gnn_a_src", "L0_gnn_a_dst", "L0_mix_Wqkv", "L0_mix_ln1_g",
        "L0_mix_ln1_b", "L0_mix_W1", "L0_mix_b1", "L0_mix_W2", "L0_mix_b2", "L0_mix_ln2_g", "L0_mix_ln2_b",
        "L0_ffn_sW1", "L0_ffn_sb1", "L0_ffn_sW2", "L0_ffn_sb2", "L0_ffn_sW3", "L0_ffn_sb3", "L0_ffn_eW1",
        "L0_ffn_eb1", "L0_ffn_eW2", "L0_ffn_eb2", "L0_ffn_eW3", "L0_ffn_eb3", "L0_ffn_gW", "L0_ffn_gb"]


def kernel(**inputs):
    import concourse.bacc as _bacc
    from concourse.bass_utils import run_bass_kernel_spmd as _run

    nc = _bacc.Bacc("TRN2", target_bir_lowering=False, num_devices=1)
    arrays, args = {}, {}
    for name in _INS:
        a = np.ascontiguousarray(inputs[name])
        arrays[f"in_{name}"] = a
        args[name] = nc.dram_tensor(f"in_{name}", a.shape, mybir.dt.from_np(a.dtype), kind="ExternalInput").ap()
    args["out"] = nc.dram_tensor("out", (N, C), F32, kind="ExternalOutput").ap()
    graph_layer(nc, args)
    r = _run(nc, [arrays], core_ids=[0])
    return r.results[0]["out"]
```

```python
import numpy as np
import concourse.bass as bass
from concourse import mybir
from contextlib import ExitStack

F32, BF16, I32, U16 = mybir.dt.float32, mybir.dt.bfloat16, mybir.dt.int32, mybir.dt.uint16
ALU = mybir.AluOpType
ACT = mybir.ActivationFunctionType
AX = mybir.AxisListType
ds = bass.ds

P = 128
N, C, H = 6250, 256, 4
HD = C // H
E_ALL = 206250
NB = -(-N // P)
TAIL = N - (NB - 1) * P
BATCH = 4
NBP = -(-NB // BATCH) * BATCH
ITERS = NBP // BATCH
W4 = BATCH * P
NBK = NB + 1
TE = -(-E_ALL // P)
TE_LAST = E_ALL - (P - 1) * TE
QUARTERS = 4
TQ = TE // QUARTERS
SUB = 31
SUBS = (16, 15)
G = 2
GR = G * P
GROUPS = 4
LOTS = 6
IT_MAX = -(-((E_ALL + NB * (GR - 1)) // GR) // (LOTS * GROUPS)) + ITERS
NG = (IT_MAX * LOTS + 4) * GROUPS
BLK_COLS = -(-NG // P)
LIST = (NG + 1) * GR
TB = C + H
NO_NODE = 200.0
EPS_LN, EPS_ATTN, SLOPE = 1e-5, 1e-6, 0.2
MH, MD = 8, 32
KVC = 132
SH1, SH2, EH1, EH2, NE = 256, 128, 128, 64, 4
assert TE == QUARTERS * TQ and TQ % SUB == 0 and sum(SUBS) == SUB and NB <= NBK < P


def wait_freed(engine, semaphore, count):
    if not (isinstance(count, int) and count == 0):
        engine.wait_ge(semaphore, count)


def first_and_rest(engine, count, body):
    body(0)
    with engine.Fori(1, count) as it:
        body(it)


def stage_sort_and_mix(nc, A, sh):
    ctx = ExitStack()
    with ctx:
        sb = lambda name, shape, dt=F32: ctx.enter_context(nc.sbuf_tensor(name, shape, dt))
        sem = lambda name: ctx.enter_context(nc.semaphore(name))
        x = sb("x_all", [P, NBP, C])
        xn = sb("xn_all", [P, NBP, C])
        ident, iota_row, ones_row = sh["ident"], sh["iota_row"], sh["ones_row"]
        node_col = sh["node_col"]
        banks = [ctx.enter_context(nc.psum_tensor(f"bank1_{i}", [P, 512], F32)) for i in range(8)]

        pos = sb("pos", [P, TE], I32)
        payload = sb("payload", [P, TE, 2], I32)
        spare = xn[:, :, :].rearrange("p b c -> p (b c)")
        at = [0]

        def carve(words):
            at[0] += words
            return spare[:, at[0] - words:at[0]]

        src_i = carve(TE).bitcast(I32)
        dst_i = carve(TE).bitcast(I32)
        int_tmp = carve(TE).bitcast(I32)
        bucket = carve(TE // 2).bitcast(BF16)
        hit = carve(TE // 2).bitcast(BF16)
        running = carve(TQ).bitcast(I32)
        places = carve(TQ).bitcast(I32)
        pad_rows = carve(2 * (LIST // P)).rearrange("p (r w) -> p r w", w=2)
        grp_cmp = carve(BLK_COLS * NB)
        counts = sb("counts", [P, NBK])
        totals = sb("totals", [P, NBK])
        grp_i = sb("grp_i", [P, NBK], I32)
        grp_end = sb("grp_end", [P, NBK])
        base = sb("base", [P, NBK])
        carry = sb("carry", [P, NBK])
        grp_no = sb("grp_no", [P, BLK_COLS])
        grp_blk = sb("grp_blk", [P, BLK_COLS])
        grp_blk_i = sb("grp_blk_i", [P, BLK_COLS], I32)
        it_cmp = sb("it_cmp", [P, ITERS, IT_MAX])
        it_end = sb("it_end", [P, ITERS + 1])
        it_ones = sb("it_ones", [P, ITERS])
        before = sb("before", [P, P])
        ones_sq = sb("ones_sq", [P, P])
        stage_pos = [sb(f"stage_pos{i}", [P, SUBS[i]], I32) for i in range(2)]
        stage_pay = [sb(f"stage_pay{i}", [P, SUBS[i], 2], I32) for i in range(2)]

        NW = 3 * C + 3 * C
        w_nat = sb("w_nat", [P, NW // P, C])
        wT = sb("wT", [P, 2, NW])
        QKV, WG, W1, W2 = 0, 3 * C, 4 * C, 5 * C
        a_mat = sb("a_mat", [P, 2, 2 * H])
        b_col = sb("b_col", [P, 2])
        b_row = sb("b_row", [1, C + 2 * H])
        g_w = sb("g_w", [P, 2, C + 2 * H])
        b1_col = sb("b1_col", [P, 2])
        b2_row = sb("b2_row", [1, C])
        ln = sb("ln", [P, 4, C])
        valid = sb("valid", [P, NBP])
        tail_rows = sb("tail_rows", [P, 1])
        kv_bd = sb("kv_bd", [P, 2, KVC])

        stats = sb("stats", [P, BATCH, 6])
        mv = sb("mv", [P, BATCH, 2])
        std = sb("std", [P, BATCH])
        inv = sb("inv", [P, BATCH])
        xT = sb("xT", [P, 2, W4])
        wh = sb("wh", [P, BATCH, C + 2 * H])
        k_min = sb("k_min", [P, 2, C])
        k_exp = sb("k_exp", [P, 2, C])
        kk = sb("kk", [P, 2, C])
        vv = sb("vv", [P, 2, 2, KVC])
        q_min = sb("q_min", [P, 2, W4])
        qT = sb("qT", [P, 2, W4])
        den = sb("den", [P, BATCH, MH])
        y = sb("y", [P, BATCH, C])
        x1 = sb("x1", [P, BATCH, C])

        (s_pads_set, s_src, s_dst, s_x, s_xtail, s_w, s_misc, s_fill, s_filled, s_const) = map(sem, (
            "s_pads_set", "s_src", "s_dst", "s_x", "s_xtail", "s_w", "s_misc", "s_fill", "s_filled", "s_const"))
        (s_counts, s_base, s_pos, s_staged0, s_staged1, s_scat0, s_scat1, s_blk, s_blkd, s_blkr) = map(sem, (
            "s_counts", "s_base", "s_pos", "s_staged0", "s_staged1", "s_scat0", "s_scat1", "s_blk", "s_blkd", "s_blkr"))
        (s_wtr, s_wtc, s_gw, s_gwc, s_kv0) = map(sem, ("s_wtr", "s_wtc", "s_gw", "s_gwc", "s_kv0"))
        (s_var, s_std, s_xn, s_tr, s_xT, s_g, s_wh, s_tab, s_kv, s_kmin, s_kexp, s_vc, s_kk, s_acc, s_nd) = map(sem, (
            "s_var", "s_std", "s_xn", "s_tr", "s_xT", "s_g", "s_wh", "s_tab", "s_kv", "s_kmin", "s_kexp", "s_vc",
            "s_kk", "s_acc", "s_nd"))
        (s_bd, s_tr2, s_xT2, s_q, s_qmin, s_qexp, s_qT, s_t, s_var2, s_std2, s_x1, s_tr3, s_xT3, s_h, s_h1, s_y2,
         s_y2r) = map(sem, ("s_bd", "s_tr2", "s_xT2", "s_q", "s_qmin", "s_qexp", "s_qT", "s_t", "s_var2", "s_std2",
                            "s_x1", "s_tr3", "s_xT3", "s_h", "s_h1", "s_y2", "s_y2r"))
        s_dve, s_pool, s_xc, s_mixed, s_mout = map(sem, ("s_dve", "s_pool", "s_xc", "s_mixed", "s_mout"))
        s_staged, s_scat = (s_staged0, s_staged1), (s_scat0, s_scat1)
        block = ctx.enter_context(nc.Block())

        @block.sync
        def _(sp):
            sp.wait_ge(s_pads_set, 4)
            for dst, src, s in ((src_i, A["src"], s_src), (dst_i, A["dst"], s_dst)):
                sp.dma_start(dst[0:P - 1, :], src[0:(P - 1) * TE].rearrange("(p t) -> p t", t=TE)).then_inc(s, 16)
                sp.dma_start(dst[P - 1:P, 0:TE_LAST],
                             src[(P - 1) * TE:E_ALL].rearrange("(p t) -> p t", p=1)).then_inc(s, 16)
            sp.dma_start(w_nat[:, 0:6, :], A["L0_mix_Wqkv"].rearrange("(a p) c -> p a c", p=P)).then_inc(s_w, 16)
            for i, name in enumerate(("L0_gnn_W", "L0_mix_W1", "L0_mix_W2")):
                sp.dma_start(w_nat[:, 6 + 2 * i:8 + 2 * i, :],
                             A[name].rearrange("(a p) c -> p a c", p=P)).then_inc(s_w, 16)
            for i, name in enumerate(("L0_gnn_a_dst", "L0_gnn_a_src")):
                for h in range(H):
                    sp.dma_start(a_mat[HD * (h % 2):HD * (h % 2) + HD, h // 2, H * i + h:H * i + h + 1],
                                 A[name][h, :].rearrange("(d a) -> d a", a=1)).then_inc(s_misc, 16)
            sp.dma_start(b_row[:, 0:C], A["L0_gnn_b"].rearrange("(a c) -> a c", a=1)).then_inc(s_misc, 16)
            sp.dma_start(b2_row[:, :], A["L0_mix_b2"].rearrange("(a c) -> a c", a=1)).then_inc(s_misc, 16)
            for dst, name in ((b_col, "L0_gnn_b"), (b1_col, "L0_mix_b1")):
                for a in range(2):
                    sp.dma_start(dst[:, a:a + 1],
                                 A[name][a * P:(a + 1) * P].rearrange("(p a) -> p a", a=1)).then_inc(s_misc, 16)
            for i, name in enumerate(("ln1_g", "ln1_b", "ln2_g", "ln2_b")):
                sp.dma_start(ln[:, i, :], A["L0_mix_" + name].partition_broadcast(P)).then_inc(s_misc, 16)
            sp.dma_start(x[:, 0:NB - 1, :],
                         A["x"][0:(NB - 1) * P, :].rearrange("(b p) c -> p b c", p=P)).then_inc(s_x, 16)
            sp.dma_start(x[0:TAIL, NB - 1, :], A["x"][(NB - 1) * P:N, :]).then_inc(s_x, 16)
            sp.wait_ge(s_fill, 2)
            sp.dma_start(sh["list"].rearrange("(p r) w -> p r w", p=P),
                         pad_rows.bitcast(I32)).then_inc(s_filled, 16)
            sp.wait_ge(s_blk, 1)
            sp.dma_start(sh["blk_dram"].rearrange("(p r) -> p r", r=BLK_COLS), grp_blk_i[:, :]).then_inc(s_blkd, 16)
            sp.wait_ge(s_blkd, 16)
            sp.dma_start(sh["blk"][0:1, :], sh["blk_dram"].rearrange("(a g) -> a g", a=1)).then_inc(s_blkr, 16)
            sp.wait_ge(s_blkr, 16)
            def columns(it):
                first = 0
                for half, n in enumerate(SUBS):
                    wait_freed(sp, s_scat[half], it * (16 * n))
                    sp.dma_start(stage_pos[half][:, :], pos[:, ds(it * SUB + first, n)]).then_inc(s_staged[half], 16)
                    sp.dma_start(stage_pay[half][:, :, :], payload[:, ds(it * SUB + first, n), :])\
                        .then_inc(s_staged[half], 16)
                    first += n

            sp.wait_ge(s_pos, 1)
            first_and_rest(sp, TQ // SUB, columns)
            for quarter in range(1, QUARTERS):
                sp.wait_ge(s_pos, quarter + 1)
                with sp.Fori(quarter * (TQ // SUB), (quarter + 1) * (TQ // SUB)) as it:
                    columns(it)

        @block.gpsimd
        def _(pool):
            g = nc.gpsimd
            done = [0]

            def step(ins):
                done[0] += 1
                ins.then_inc(s_pool, 1)
                pool.wait_ge(s_pool, done[0])

            step(g.memset(ident[:, :], 0.0))
            step(g.affine_select(out=ident[:, :], in_=ident[:, :], compare_op=ALU.not_equal, fill=1.0, base=0,
                                 pattern=[[-1, P]], channel_multiplier=1))
            step(g.memset(ones_sq[:, :], 1.0))
            step(g.affine_select(out=before[:, :], in_=ones_sq[:, :], compare_op=ALU.is_gt, fill=0.0, base=0,
                                 pattern=[[1, P]], channel_multiplier=-1))
            step(g.iota(iota_row[:, :], [[1, P]], base=0, channel_multiplier=0, allow_small_or_imprecise_dtypes=True))
            step(g.iota(node_col[:, :], [[1, 1]], base=0, channel_multiplier=1, allow_small_or_imprecise_dtypes=True))
            step(g.iota(grp_no[:, :], [[1, BLK_COLS]], base=0, channel_multiplier=BLK_COLS, allow_small_or_imprecise_dtypes=True))
            step(g.affine_select(out=tail_rows[:, :], in_=ones_sq[:, 0:1], compare_op=ALU.is_gt, fill=0.0, base=TAIL,
                                 pattern=[[0, 1]], channel_multiplier=-1))
            g.memset(ones_row[:, :], 1.0).then_inc(s_const, 1)
            g.memset(pad_rows[:, :, 0], 0.0).then_inc(s_fill, 1)
            g.memset(pad_rows[:, :, 1], NO_NODE).then_inc(s_fill, 1)
            due = [pool.alloc_register(f"due_staged{half}") for half in range(2)]
            for half in range(2):
                pool.reg_mov(due[half], 32)
            pool.wait_ge(s_filled, 16)
            with pool.Fori(0, TE // SUB) as it:
                for half, n in enumerate(SUBS):
                    pool.wait_ge(s_staged[half], due[half])
                    pool.reg_add(due[half], due[half], 32)
                    for t in range(n):
                        g.indirect_dma_start(sh["list"], bass.IndirectOffsetOnAxis(ap=stage_pos[half][:, t:t + 1], axis=0),
                                             stage_pay[half][:, t, :], None).then_inc(s_scat[half], 16)
            for half, n in enumerate(SUBS):
                pool.wait_ge(s_scat[half], 16 * n * (TE // SUB))

        @block.vector
        def _(dve):
            v = nc.vector
            done = [0]

            def step(ins):
                done[0] += 1
                ins.then_inc(s_dve, 1)
                dve.wait_ge(s_dve, done[0])

            last_t = slice(TE_LAST, TE)
            v.memset(src_i[96:P, last_t], NB * P).then_inc(s_pads_set, 1)
            v.memset(dst_i[96:P, last_t], 0).then_inc(s_pads_set, 1)
            v.memset(a_mat[:, :, :], 0.0).then_inc(s_pads_set, 1)
            v.memset(x[:, NB - 1:NBP, :], 0.0).then_inc(s_pads_set, 1)
            dve.wait_ge(s_src, 32)
            step(v.tensor_scalar(int_tmp, src_i, 7, None, ALU.logical_shift_right))
            step(v.tensor_copy(bucket, int_tmp))
            step(v.tensor_scalar(int_tmp, src_i, P - 1, None, ALU.bitwise_and))
            step(v.tensor_copy(payload[:, :, 1].bitcast(F32), int_tmp))
            dve.wait_ge(s_dst, 32)
            step(v.tensor_copy(payload[:, :, 0], dst_i))
            dve.wait_ge(s_const, 1)
            with dve.Fori(0, NBK) as b:
                v.tensor_scalar(hit, bucket, iota_row[:, ds(b, 1)], 0.0, ALU.is_equal, ALU.add,
                                accum_out=counts[:, ds(b, 1)]).then_inc(s_counts, 1)
                dve.wait_ge(s_counts, b + 1)
            dve.wait_ge(s_base, 1)
            step(v.tensor_scalar(totals[:, :], banks[7][:, 0:NBK], float(GR - 1), None, ALU.add))
            step(v.tensor_copy(grp_i[:, :], totals[:, :]))
            step(v.tensor_scalar(grp_i[:, :], grp_i[:, :], GR.bit_length() - 1, None, ALU.logical_shift_right))
            step(v.tensor_copy(totals[:, :], grp_i[:, :]))
            step(v.tensor_tensor_scan(grp_end[:, :], totals[:, :], totals[:, :], 0.0, ALU.add, ALU.bypass))
            step(v.tensor_tensor(totals[:, :], grp_end[:, :], totals[:, :], ALU.subtract))
            step(v.memset(totals[:, NB:NBK], float(NG)))
            step(v.scalar_tensor_tensor(base[:, :], totals[:, :], float(GR), banks[7][:, 64:64 + NBK], ALU.mult, ALU.add))
            step(v.tensor_scalar(carry[:, :], base[:, :], -1.0, None, ALU.add))
            ge = grp_cmp.rearrange("p (r b) -> p r b", b=NB)
            step(v.tensor_tensor(ge, grp_no[:, :].unsqueeze(2).broadcast_to([P, BLK_COLS, NB]),
                                 grp_end[:, 0:NB].unsqueeze(1).broadcast_to([P, BLK_COLS, NB]), ALU.is_ge))
            step(v.tensor_reduce(grp_blk[:, :], ge, AX.X, ALU.add))
            step(v.tensor_scalar(grp_blk[:, :], grp_blk[:, :], float(NB - 1), None, ALU.min))
            v.tensor_copy(grp_blk_i[:, :], grp_blk[:, :]).then_inc(s_blk, 1)
            for k in range(ITERS):
                last_block = min(BATCH * k + BATCH, NB) - 1
                last = v.tensor_scalar(it_cmp[:, k, :], iota_row[:, 0:IT_MAX], float(LOTS * GROUPS),
                                       grp_end[:, last_block:last_block + 1], ALU.mult, ALU.is_lt)
            step(last)
            step(v.memset(it_end[:, 0:1], 1.0))
            step(v.tensor_reduce(it_end[:, 1:ITERS + 1], it_cmp[:, :, :], AX.X, ALU.add))
            step(v.memset(it_ones[:, :], 1.0))
            step(v.tensor_tensor_scan(it_cmp[:, :, 0], it_ones[:, :], it_end[:, 1:ITERS + 1], 1.0, ALU.add, ALU.max))
            step(v.tensor_copy(it_end[:, 1:ITERS + 1], it_cmp[:, :, 0]))
            step(v.tensor_copy(sh["bounds"][:, :], it_end[0:1, :]))
            with dve.Fori(0, QUARTERS) as quarter:
                with dve.Fori(0, NBK) as b:
                    done[0] = 0
                    dve.sem_clear(s_dve)
                    step(v.tensor_scalar(hit[:, 0:TQ], bucket[:, ds(quarter * TQ, TQ)], iota_row[:, ds(b, 1)], None,
                                         ALU.is_equal))
                    step(v.tensor_tensor_scan(running, hit[:, 0:TQ], hit[:, 0:TQ], carry[:, ds(b, 1)],
                                              ALU.add, ALU.bypass))
                    step(v.tensor_copy(carry[:, ds(b, 1)], running[:, TQ - 1:TQ]))
                    step(v.copy_predicated(places, hit[:, 0:TQ].bitcast(U16), running))
                v.tensor_copy(pos[:, ds(quarter * TQ, TQ)], places).then_inc(s_pos, 1)
                dve.wait_ge(s_pos, quarter + 1)
            done[0] = 0
            dve.sem_clear(s_dve)
            step(v.memset(valid[:, :], 1.0))
            step(v.memset(valid[:, NB - 1:NBP], 0.0))
            step(v.tensor_copy(valid[:, NB - 1:NB], tail_rows[:, :]))
            step(v.memset(kv_bd[:, :, :], 0.0))
            dve.wait_ge(s_gwc, 1)
            v.memset(banks[6][:, 0:258], 0.0).then_inc(s_kv0, 1)
            dve.wait_ge(s_x, 32)
            dve.wait_ge(s_filled, 16)

            def one_turn(it):
                done[0] = 0
                dve.sem_clear(s_dve)
                for u in range(BATCH):
                    v.bn_stats(stats[:, u, :], x[:, ds(it * BATCH + u, 1), :].rearrange("p a c -> p (a c)"))\
                        .then_inc(s_dve, 1)
                done[0] += BATCH
                dve.wait_ge(s_dve, done[0])
                for u in range(BATCH):
                    v.bn_aggr(mv[:, u, :], stats[:, u, :]).then_inc(s_dve, 1)
                done[0] += BATCH
                dve.wait_ge(s_dve, done[0])
                v.tensor_scalar(inv[:, :], mv[:, :, 1], EPS_LN, None, ALU.add).then_inc(s_var, 1)
                dve.wait_ge(s_std, it + 1)
                step(v.reciprocal(inv[:, :], std[:, :]))
                for u in range(BATCH):
                    last = v.tensor_scalar(y[:, u, :],
                                           x[:, ds(it * BATCH + u, 1), :].rearrange("p a c -> p (a c)"),
                                           mv[:, u, 0:1], inv[:, u:u + 1], ALU.subtract, ALU.mult)
                last.then_inc(s_xn, 1)
                dve.wait_ge(s_xn, it + 1)
                v.tensor_copy(xn[:, ds(it * BATCH, BATCH), :], y[:, :, :])
                for u in range(BATCH):
                    bank = banks[4 + u % 2]
                    dve.wait_ge(s_kv, it * BATCH + u + 1)
                    v.tensor_scalar(k_min[:, u % 2, :], bank[:, 0:C], 0.0, None, ALU.min).then_inc(s_kmin, 1)
                    wait_freed(dve, s_acc, it * BATCH + max(u - 1, 0))
                    v.tensor_copy(vv[:, u % 2, :, P:P + 1],
                                  valid[:, ds(it * BATCH + u, 1)].unsqueeze(1).broadcast_to([P, 2, 1])).then_inc(s_nd, 1)
                    dve.wait_ge(s_kexp, it * BATCH + u + 1)
                    dve.wait_ge(s_vc, it * BATCH + u + 1)
                    v.scalar_tensor_tensor(kk[:, u % 2, :], bank[:, 0:C], 0.0, k_exp[:, u % 2, :], ALU.max, ALU.add)\
                        .then_inc(s_kk, 1)

            first_and_rest(dve, ITERS, one_turn)

            dve.wait_ge(s_acc, NBP)
            for half in range(2):
                for j in range(4):
                    r = slice(MD * j, MD * j + MD)
                    o = half * 129
                    v.tensor_copy(kv_bd[r, half, MD * j:MD * j + MD], banks[6][r, o + MD * j:o + MD * j + MD])
                    last = v.tensor_copy(kv_bd[r, half, P + j:P + j + 1], banks[6][r, o + P:o + P + 1])
            last.then_inc(s_bd, 1)

            def one_turn(it):
                done[0] = 0
                dve.sem_clear(s_dve)

                def norm(count, gamma):
                    for u in range(BATCH):
                        v.bn_stats(stats[:, u, :], y[:, u, :]).then_inc(s_dve, 1)
                    done[0] += BATCH
                    dve.wait_ge(s_dve, done[0])
                    for u in range(BATCH):
                        v.bn_aggr(mv[:, u, :], stats[:, u, :]).then_inc(s_dve, 1)
                    done[0] += BATCH
                    dve.wait_ge(s_dve, done[0])
                    v.tensor_scalar(inv[:, :], mv[:, :, 1], EPS_LN, None, ALU.add).then_inc(s_var2, 1)
                    dve.wait_ge(s_std2, it * 2 + count)
                    step(v.reciprocal(inv[:, :], std[:, :]))
                    for u in range(BATCH):
                        last = v.tensor_scalar(y[:, u, :], y[:, u, :], mv[:, u, 0:1], inv[:, u:u + 1],
                                               ALU.subtract, ALU.mult)
                    step(last)
                    step(v.tensor_tensor(y[:, :, :], y[:, :, :],
                                         ln[:, gamma, :].unsqueeze(1).broadcast_to([P, BATCH, C]), ALU.mult))

                v.tensor_copy(y[:, :, :], xn[:, ds(it * BATCH, BATCH), :]).then_inc(s_xc, 1)
                for m in range(2):
                    dve.wait_ge(s_q, it * 2 + m + 1)
                    v.tensor_scalar(q_min[:, m, :], banks[2 + m][:, :], 0.0, None, ALU.min).then_inc(s_qmin, 1)
                for m in range(2):
                    dve.wait_ge(s_qexp, it * 2 + m + 1)
                    v.scalar_tensor_tensor(qT[:, m, :], banks[2 + m][:, :], 0.0, q_min[:, m, :], ALU.max, ALU.add)\
                        .then_inc(s_qT, 1)
                for u in range(BATCH):
                    halves = banks[4 + u][:, 0:2 * KVC].rearrange("p (a w) -> p a w", w=KVC)
                    dve.wait_ge(s_t, it * BATCH + u + 1)
                    step(v.tensor_scalar(den[:, u, :].rearrange("p (a h) -> p a h", a=2), halves[:, :, P:KVC],
                                         EPS_ATTN, None, ALU.add))
                    step(v.reciprocal(den[:, u, :], den[:, u, :]))
                    for a in range(2):
                        last = v.tensor_tensor(
                            y[:, u, a * P:(a + 1) * P].rearrange("p (h d) -> p h d", d=MD),
                            halves[:, a, 0:P].rearrange("p (h d) -> p h d", d=MD),
                            den[:, u, 4 * a:4 * a + 4].unsqueeze(2).broadcast_to([P, 4, MD]), ALU.mult)
                    step(last)
                step(v.tensor_tensor(y[:, :, :], y[:, :, :], xn[:, ds(it * BATCH, BATCH), :], ALU.add))
                norm(1, 0)
                v.tensor_tensor(x1[:, :, :], y[:, :, :], ln[:, 1, :].unsqueeze(1).broadcast_to([P, BATCH, C]), ALU.add)\
                    .then_inc(s_x1, 1)
                for u in range(BATCH):
                    dve.wait_ge(s_y2, it * BATCH + u + 1)
                    last = v.tensor_tensor(y[:, u, :], banks[4 + u][:, 0:C], x1[:, u, :], ALU.add)
                last.then_inc(s_y2r, 1)
                dve.wait_ge(s_y2r, it + 1)
                norm(2, 2)
                step(v.tensor_tensor(y[:, :, :], y[:, :, :],
                                     ln[:, 3, :].unsqueeze(1).broadcast_to([P, BATCH, C]), ALU.add))
                v.tensor_tensor(x[:, ds(it * BATCH, BATCH), :], x[:, ds(it * BATCH, BATCH), :], y[:, :, :], ALU.add)\
                    .then_inc(s_mixed, 1)
                dve.wait_ge(s_mixed, it + 1)

            first_and_rest(dve, ITERS, one_turn)

        @block.scalar
        def _(act):
            s = nc.scalar
            for i in range(2 * NW // 512):
                act.wait_ge(s_wtr, i + 1)
                s.copy(wT[:, i // 3, 512 * (i % 3):512 * (i % 3) + 512], banks[i][:, :]).then_inc(s_wtc, 1)
            act.wait_ge(s_gw, 1)
            for k in range(2):
                s.copy(g_w[:, k, C:C + 2 * H], banks[6][:, 8 * k:8 * k + 8])
            s.copy(b_row[:, C:C + 2 * H], banks[6][0:1, 16:24])
            act.wait_ge(s_wtc, 6)
            s.copy(g_w[:, :, 0:C], wT[:, :, WG:WG + C]).then_inc(s_gwc, 1)
            def one_turn(it):
                act.wait_ge(s_var, it + 1)
                s.activation(std[:, :], inv[:, :], ACT.Sqrt).then_inc(s_std, 1)
                act.wait_ge(s_tr, it + 1)
                for k in range(2):
                    last = s.copy(xT[:, k, :], banks[k][:, :])
                last.then_inc(s_xT, 1)
                for u in range(BATCH):
                    n = it * BATCH + u
                    act.wait_ge(s_g, n + 1)
                    if u == 0:
                        wait_freed(act, s_tab, it * 16)
                        act.wait_ge(s_gwc, 1)
                    s.copy(wh[:, u, :], banks[2 + u % 2][:, 0:C + 2 * H]).then_inc(s_wh, 1)
                    act.wait_ge(s_kmin, n + 1)
                    s.activation(k_exp[:, u % 2, :], k_min[:, u % 2, :], ACT.Exp).then_inc(s_kexp, 1)
                    act.wait_ge(s_nd, n + 1)
                    s.copy(vv[:, u % 2, :, 0:P], banks[4 + u % 2][:, C:2 * C].rearrange("p (a d) -> p a d", a=2))\
                        .then_inc(s_vc, 1)
                act.wait_ge(s_wh, it * BATCH + BATCH)
                act.wait_ge(s_gwc, 1)
                act.dma_start(sh["table"][ds(it * W4, W4), :].rearrange("(b p) c -> p b c", p=P),
                              wh[:, :, 0:TB]).then_inc(s_tab, 16)
                s.copy(sh["ad"][:, ds(it * BATCH, BATCH), :], wh[:, :, C:C + H])
                s.copy(sh["t8"][:, ds(it * BATCH, BATCH), 0:H], wh[:, :, C + H:C + 2 * H])

            first_and_rest(act, ITERS, one_turn)
            def one_turn(it):
                act.wait_ge(s_tr2, it + 1)
                for k in range(2):
                    last = s.copy(xT[:, k, :], banks[k][:, :])
                last.then_inc(s_xT2, 1)
                for m in range(2):
                    act.wait_ge(s_qmin, it * 2 + m + 1)
                    s.activation(q_min[:, m, :], q_min[:, m, :], ACT.Exp).then_inc(s_qexp, 1)
                act.wait_ge(s_var2, it * 2 + 1)
                s.activation(std[:, :], inv[:, :], ACT.Sqrt).then_inc(s_std2, 1)
                act.wait_ge(s_tr3, it + 1)
                for k in range(2):
                    last = s.copy(xT[:, k, :], banks[k][:, :])
                last.then_inc(s_xT3, 1)
                for m in range(2):
                    act.wait_ge(s_h, it * 2 + m + 1)
                    s.activation(qT[:, m, :], banks[2 + m][:, :], ACT.Gelu, bias=b1_col[:, m:m + 1]).then_inc(s_h1, 1)
                act.wait_ge(s_var2, it * 2 + 2)
                s.activation(std[:, :], inv[:, :], ACT.Sqrt).then_inc(s_std2, 1)
                if not isinstance(it, int):
                    mixed_out(it - 1)

            def mixed_out(it):
                act.wait_ge(s_mixed, it + 1)
                act.wait_ge(s_gwc, 1)
                act.dma_start(sh["mixed"][ds(it * W4, W4), :].rearrange("(b p) c -> p b c", p=P),
                              x[:, ds(it * BATCH, BATCH), :]).then_inc(s_mout, 16)

            first_and_rest(act, ITERS, one_turn)
            mixed_out(ITERS - 1)
            act.wait_ge(s_mout, 16 * ITERS)
            act.wait_ge(s_tab, 16 * ITERS)

        @block.tensor
        def _(pe):
            t = nc.tensor
            pe.wait_ge(s_const, 1)
            pe.wait_ge(s_w, 64)
            for i in range(2 * NW // 512):
                for j in range(4):
                    chunk = 4 * (i % 3) + j
                    last = t.transpose(banks[i][:, P * j:P * j + P], w_nat[:, chunk, P * (i // 3):P * (i // 3) + P],
                                       ident[:, :])
                last.then_inc(s_wtr, 1)
            pe.wait_ge(s_misc, 16 * 18)
            for k in range(2):
                for o in range(2):
                    t.matmul(banks[6][:, 8 * k:8 * k + 8], w_nat[:, 6 + o, P * k:P * k + P], a_mat[:, o, :],
                             start=o == 0, stop=o == 1)
            for o in range(2):
                last = t.matmul(banks[6][0:1, 16:24], b_col[:, o:o + 1], a_mat[:, o, :], start=o == 0, stop=o == 1)
            last.then_inc(s_gw, 1)
            pe.wait_ge(s_counts, NBK)
            t.matmul(banks[7][:, 0:NBK], ones_sq[:, :], counts[:, :], start=True, stop=True)
            t.matmul(banks[7][:, 64:64 + NBK], before[:, :], counts[:, :], start=True, stop=True).then_inc(s_base, 1)
            pe.wait_ge(s_gwc, 1)
            pe.wait_ge(s_kv0, 1)
            def one_turn(it):
                pe.wait_ge(s_xn, it + 1)
                for k in range(2):
                    for u in range(BATCH):
                        last = t.transpose(banks[k][:, P * u:P * u + P], y[:, u, P * k:P * k + P], ident[:, :])
                last.then_inc(s_tr, 1)
                pe.wait_ge(s_xT, it + 1)
                for u in range(BATCH):
                    n = it * BATCH + u
                    wait_freed(pe, s_wh, it * BATCH + max(u - 1, 0))
                    for k in range(2):
                        t.matmul(banks[2 + u % 2][:, 0:C + 2 * H], xT[:, k, P * u:P * u + P], g_w[:, k, :],
                                 start=k == 0, stop=False)
                    t.matmul(banks[2 + u % 2][:, 0:C + 2 * H], ones_row[:, :], b_row[:, :], start=False, stop=True)\
                        .then_inc(s_g, 1)
                    wait_freed(pe, s_kk, it * BATCH + max(u - 1, 0))
                    wait_freed(pe, s_vc, it * BATCH + max(u - 1, 0))
                    for k in range(2):
                        last = t.matmul(banks[4 + u % 2][:, :], xT[:, k, P * u:P * u + P], wT[:, k, C:3 * C],
                                        start=k == 0, stop=k == 1)
                    last.then_inc(s_kv, 1)
                    pe.wait_ge(s_kk, n + 1)
                    pe.wait_ge(s_vc, n + 1)
                    for a in range(2):
                        last = t.matmul(banks[6][:, 129 * a:129 * a + 129], kk[:, u % 2, P * a:P * a + P],
                                        vv[:, u % 2, a, 0:129], start=False, stop=False, skip_group_check=True)
                    last.then_inc(s_acc, 1)

            first_and_rest(pe, ITERS, one_turn)
            pe.wait_ge(s_bd, 1)
            def one_turn(it):
                pe.wait_ge(s_xc, it + 1)
                for k in range(2):
                    for u in range(BATCH):
                        last = t.transpose(banks[k][:, P * u:P * u + P], y[:, u, P * k:P * k + P], ident[:, :])
                last.then_inc(s_tr2, 1)
                pe.wait_ge(s_xT2, it + 1)
                for m in range(2):
                    for k in range(2):
                        last = t.matmul(banks[2 + m][:, :], wT[:, k, P * m:P * m + P], xT[:, k, :],
                                        start=k == 0, stop=k == 1)
                    last.then_inc(s_q, 1)
                pe.wait_ge(s_qT, it * 2 + 2)
                wait_freed(pe, s_y2r, it)
                for u in range(BATCH):
                    for a in range(2):
                        last = t.matmul(banks[4 + u][:, KVC * a:KVC * a + KVC], qT[:, a, P * u:P * u + P],
                                        kv_bd[:, a, :], start=True, stop=True)
                    last.then_inc(s_t, 1)
                pe.wait_ge(s_x1, it + 1)
                for k in range(2):
                    for u in range(BATCH):
                        last = t.transpose(banks[k][:, P * u:P * u + P], x1[:, u, P * k:P * k + P], ident[:, :])
                last.then_inc(s_tr3, 1)
                pe.wait_ge(s_xT3, it + 1)
                for m in range(2):
                    for k in range(2):
                        last = t.matmul(banks[2 + m][:, :], wT[:, k, W1 + P * m:W1 + P * m + P], xT[:, k, :],
                                        start=k == 0, stop=k == 1)
                    last.then_inc(s_h, 1)
                pe.wait_ge(s_h1, it * 2 + 2)
                for u in range(BATCH):
                    for k in range(2):
                        t.matmul(banks[4 + u][:, 0:C], qT[:, k, P * u:P * u + P], wT[:, k, W2:W2 + C],
                                 start=k == 0, stop=False)
                    t.matmul(banks[4 + u][:, 0:C], ones_row[:, :], b2_row[:, :], start=False, stop=True)\
                        .then_inc(s_y2, 1)

            first_and_rest(pe, ITERS, one_turn)


def stage_edges_and_feed_forward(nc, A, sh):
    TILES = GROUPS * G
    QUAD = 4
    ctx = ExitStack()
    with ctx:
        sb = lambda name, shape, dt=F32: ctx.enter_context(nc.sbuf_tensor(name, shape, dt))
        sem = lambda name: ctx.enter_context(nc.semaphore(name))
        sems = lambda name, n: [sem(f"{name}{i}") for i in range(n)]
        banks = [ctx.enter_context(nc.psum_tensor(f"bank2_{i}", [P, 512], F32)) for i in range(8)]
        t8, ad, blk, bounds = sh["t8"], sh["ad"], sh["blk"], sh["bounds"]
        iota_row, node_col, ident = sh["iota_row"], sh["node_col"], sh["ident"]
        ones_row = sh["ones_row"]
        acc = sb("acc", [P, NBP, TB])
        col = [sb(f"col{i}", [P, GROUPS, G, 2], I32) for i in range(LOTS)]
        row = [sb(f"row{i}", [1, TILES * P, 2], I32) for i in range(2)]
        ones_bf = sb("ones_bf", [1, P], BF16)
        gathered = sb("gathered", [P, LOTS, TILES, TB])
        weighted = sb("weighted", [P, 2, TILES, TB])
        onehot = sb("onehot", [P, 2, TILES, P])
        dist = sb("dist", [P, 2, QUAD * P])
        onehot_t = sb("onehot_t", [P, 2, TILES, P])
        z = sb("z", [P, 2, TILES, H])
        e = sb("e", [P, 2, TILES, H])
        minus_node = sb("minus_node", [P, 1])
        ad_max = sb("ad_max", [P, H])
        ad_top = sb("ad_top", [P, H])

        s_col, s_gath, s_sel, s_mul = (sems(n, LOTS) for n in ("s_col", "s_gath", "s_sel", "s_mul"))
        s_row, s_as, s_d, s_p, s_main = (sems(n, 2) for n in ("s_row", "s_as", "s_d", "s_p", "s_main"))
        s_sum = sems("s_sum", GROUPS)
        s_max, s_top, s_ready, s_bc, s_dist, s_ot = map(sem, (
            "s_max", "s_top", "s_ready", "s_bc", "s_dist", "s_ot"))
        s_dve = sem("s_dve2")

        sW1, sW2, sW3 = sb("sW1", [P, 2, SH1]), sb("sW2", [P, 2, SH2]), sb("sW3", [P, C])
        eW1, eW2, eW3 = sb("eW1", [P, NE, 2, EH1]), sb("eW2", [P, NE, EH2]), sb("eW3", [P, 2, C])
        sb1, sb2, eb1, eb2 = sb("sb1", [P, 2]), sb("sb2", [P, 1]), sb("eb1", [P, NE]), sb("eb2", [P, 2])
        bias3 = sb("bias3", [NE + 1, C])
        gW, gb = sb("gW", [P, 2, NE]), sb("gb", [1, NE])
        expert_rows = sb("expert_rows", [NE + 1, 2 * P])
        lower = sb("lower", [P, NE, NE])
        recip = sb("recip", [P, BATCH, H])
        stats, mv = sb("stats3", [P, BATCH, 6]), sb("mv3", [P, BATCH, 2])
        std, inv = sb("std3", [P, BATCH]), sb("inv3", [P, BATCH])
        x = sb("x_batch", [P, BATCH, C])
        xf = sb("xf", [P, BATCH, C])
        xo = xf
        xT = sb("xT3", [P, 2, W4])
        top = sb("top", [P, BATCH])
        gate = sb("gate", [P, BATCH, NE])
        gate_e = sb("gate_e", [P, BATCH, NE])
        cmp = sb("cmp", [P, BATCH, NE, NE])
        cmp2 = sb("cmp2", [P, BATCH, NE, NE])
        wgt = sb("wgt", [P, BATCH, NE])
        wT = sb("wT3", [NE + 1, W4])
        h2, he1, he2 = sb("h2", [P, W4]), sb("he1", [P, NE, W4]), sb("he2", [P, 2, W4])
        h1 = he2
        (s_w, s_xin, s_var, s_std, s_xf, s_tr, s_xT, s_lg, s_lgs, s_ex, s_ga, s_ga2, s_wg, s_wt, s_wT) = map(sem, (
            "f_w", "f_xin", "f_var", "f_std", "f_xf", "f_tr", "f_xT", "f_lg", "f_lgs", "f_ex", "f_ga", "f_ga2",
            "f_wg", "f_wt", "f_wT"))
        (s_p1, s_h1, s_p2, s_h2, s_q1, s_he1, s_q2, s_he2, s_wb, s_hw, s_o, s_x, s_out) = map(sem, (
            "f_p1", "f_h1", "f_p2", "f_h2", "f_q1", "f_he1", "f_q2", "f_he2", "f_wb", "f_hw", "f_o", "f_x", "f_out"))
        s_pool, s_set = sem("f_pool"), sem("f_set")
        block = ctx.enter_context(nc.Block())

        def after(it, l, lots):
            return it + (l + lots) // LOTS, (l + lots) % LOTS

        def blocks_of(engine, it, l):
            _, values = nc.values_load_multi_w_load_instructions(
                blk[0:1, ds((it * LOTS + l) * GROUPS, GROUPS)], engines=[engine], min_val=0, max_val=NB - 1,
                skip_runtime_bounds_check_because="stage 1 clamps the blocks to NB - 1")
            return values

        def all_segments(engine, segment_lot, start, feed_forward):
            def iterations(k):
                begin = engine.value_load(bounds[0:1, ds(k, 1)], min_val=1, max_val=IT_MAX - 2)
                end = engine.value_load(bounds[0:1, ds(k + 1, 1)], min_val=2, max_val=IT_MAX - 1)
                with engine.Fori(begin, end) as it:
                    for l in range(LOTS):
                        segment_lot(it, l)

            start(0)
            for l in range(LOTS):
                segment_lot(0, l)
            iterations(0)
            feed_forward(0)
            with engine.Fori(1, ITERS) as k:
                start(k)
                iterations(k)
                feed_forward(k)

        @block.sync
        def _(sp):
            def column(it, l):
                wait_freed(sp, s_gath[l], it * (16 * TILES))
                wait_freed(sp, s_sel[l], it)
                sp.dma_start(col[l][:, :, :, :],
                             sh["list"][ds((it * LOTS + l) * (TILES * P), TILES * P), :]
                             .rearrange("(g p k) w -> p g (k w)", g=GROUPS, p=P)).then_inc(s_col[l], 16)

            for l in range(LOTS):
                column(0, l)
            loads = [(sW1[:, :, :], A["L0_ffn_sW1"].rearrange("(k p) o -> p k o", p=P)),
                     (sW2[:, :, :], A["L0_ffn_sW2"].rearrange("(k p) o -> p k o", p=P)),
                     (sW3[:, :], A["L0_ffn_sW3"]),
                     (eW2[:, :, :], A["L0_ffn_eW2"].rearrange("e h g -> h e g")),
                     (eW3[:, :, :], A["L0_ffn_eW3"].rearrange("(a e) g o -> (e g) a o", e=2)),
                     (sb2[:, :], A["L0_ffn_sb2"].rearrange("(p a) -> p a", a=1)),
                     (bias3[NE:NE + 1, :], A["L0_ffn_sb3"].rearrange("(a o) -> a o", a=1)),
                     (bias3[0:NE, :], A["L0_ffn_eb3"]),
                     (gb[:, :], A["L0_ffn_gb"].rearrange("(a o) -> a o", a=1))]
            for i in range(NE):
                loads.append((eW1[:, i, :, :], A["L0_ffn_eW1"][i].rearrange("(k p) h -> p k h", p=P)))
                loads.append((eb1[:, i:i + 1], A["L0_ffn_eb1"][i].rearrange("(p a) -> p a", a=1)))
                loads.append((eb2[64 * (i % 2):64 * (i % 2) + 64, i // 2:i // 2 + 1],
                              A["L0_ffn_eb2"][i].rearrange("(p a) -> p a", a=1)))
            for k in range(2):
                loads.append((sb1[:, k:k + 1], A["L0_ffn_sb1"][k * P:k * P + P].rearrange("(p a) -> p a", a=1)))
                loads.append((gW[:, k, :], A["L0_ffn_gW"][k * P:k * P + P, :]))
            assert len(loads) == LOADS3
            for dst, src in loads:
                sp.dma_start(dst, src).then_inc(s_w, 16)
            end = sp.value_load(bounds[0:1, ITERS:ITERS + 1], min_val=2, max_val=IT_MAX - 1)
            with sp.Fori(1, end) as it:
                for l in range(LOTS):
                    column(it, l)
            for l in range(2):
                column(sp.snap(end), l)

        @block.gpsimd
        def _(pool):
            g = nc.gpsimd
            pool.wait_ge(s_max, 1)
            g.partition_all_reduce(ad_top[:, :], ad_max[:, :], P, sh["RMAX"]).then_inc(s_top, 1)
            due = [pool.alloc_register(f"due_col{l}") for l in range(LOTS)]
            for l in range(LOTS):
                pool.reg_mov(due[l], 16)

            def gathers(it, l):
                wait_freed(pool, s_mul[l], it * GROUPS)
                pool.wait_ge(s_col[l], due[l])
                pool.reg_add(due[l], due[l], 16)
                for t in range(TILES):
                    g.indirect_dma_start(
                        gathered[:, l, t, :], None, sh["table"],
                        bass.IndirectOffsetOnAxis(ap=col[l][:, t // G, t % G, 0:1], axis=0)).then_inc(s_gath[l], 16)

            for l in range(LOTS):
                gathers(0, l)
            g.memset(expert_rows[:, :], 1.0).then_inc(s_pool, 1)
            pool.wait_ge(s_pool, 1)
            g.affine_select(out=expert_rows[:, :], in_=expert_rows[:, :], compare_op=ALU.is_ge, fill=0.0, base=0,
                            pattern=[[1, NE * EH2]], channel_multiplier=-EH2).then_inc(s_pool, 1)
            pool.wait_ge(s_pool, 2)
            g.affine_select(out=expert_rows[:, :], in_=expert_rows[:, :], compare_op=ALU.is_gt, fill=0.0, base=EH2,
                            pattern=[[-1, NE * EH2]], channel_multiplier=EH2).then_inc(s_set, 1)
            g.memset(lower[:, :, :], 1.0).then_inc(s_pool, 1)
            pool.wait_ge(s_pool, 3)
            g.affine_select(out=lower[:, :, :], in_=lower[:, :, :], compare_op=ALU.is_gt, fill=0.0, base=0,
                            pattern=[[1, NE], [-1, NE]], channel_multiplier=0).then_inc(s_set, 1)
            end = pool.value_load(bounds[0:1, ITERS:ITERS + 1], min_val=2, max_val=IT_MAX - 1)
            with pool.Fori(1, end) as it:
                for l in range(LOTS):
                    gathers(it, l)
            with pool.Fori(end, pool.snap(end + 1)) as it:
                for l in range(2):
                    gathers(it, l)

        @block.tensor
        def _(pe):
            t = nc.tensor

            def spread(it, l):
                pe.wait_ge(s_row[l % 2], 16 * (it * (LOTS // 2) + l // 2) + 16)
                for q in range(2):
                    wait_freed(pe, s_dist, (it * LOTS + l) * 2)
                    words = row[l % 2][:, :, :].bitcast(BF16).rearrange("a (g p k) w -> a g k p w", g=GROUPS, p=P)
                    t.matmul(banks[q][:, :], ones_bf[:, :], words[:, 2 * q:2 * q + 2, :, :, 3], start=True, stop=True)\
                        .then_inc(s_bc, 1)

            def by_node(it, l):
                wait_freed(pe, s_d[l % 2], it * (LOTS // 2) + l // 2)
                pe.wait_ge(s_ot, (it * LOTS + l) * 2 + 2)
                for g, b in enumerate(blocks_of(mybir.EngineType.PE, it, l)):
                    for k in range(G):
                        tile = g * G + k
                        last = t.matmul(banks[2 + l % 2][:, 8 * tile:8 * tile + 8], onehot_t[:, l % 2, tile, :],
                                        t8[:, ds(b, 1), :].rearrange("p a w -> p (a w)"), start=True, stop=True)
                last.then_inc(s_as[l % 2], 1)

            def sums(it, l):
                for g in range(GROUPS):
                    pe.wait_ge(s_mul[l], it * GROUPS + g + 1)
                    wait_freed(pe, s_sum[g], it * LOTS + l)
                    for k in range(G):
                        last = t.matmul(banks[4 + g][:, 0:TB], onehot[:, l % 2, g * G + k, :],
                                        weighted[:, l % 2, g * G + k, :], start=k == 0, stop=k == G - 1)
                    last.then_inc(s_main[l % 2], 1)

            def lot(it, l):
                spread(*after(it, l, 3))
                sums(it, l)
                by_node(*after(it, l, 2))

            def start(k):
                wait_freed(pe, s_x, k * BATCH)

            def feed_forward(it):
                pe.wait_ge(s_xf, it + 1)
                for k in range(2):
                    for u in range(BATCH):
                        last = t.transpose(banks[k][:, P * u:P * u + P], xf[:, u, P * k:P * k + P], ident[:, :])
                last.then_inc(s_tr, 1)
                pe.wait_ge(s_xT, it + 1)
                for u in range(BATCH):
                    for k in range(2):
                        t.matmul(banks[7][:, NE * u:NE * u + NE], xT[:, k, P * u:P * u + P], gW[:, k, :],
                                 start=k == 0, stop=False)
                    last = t.matmul(banks[7][:, NE * u:NE * u + NE], ones_row[:, :], gb[:, :], start=False, stop=True)
                last.then_inc(s_lg, 1)
                for m in range(2):
                    for k in range(2):
                        last = t.matmul(banks[2 + m][:, :], sW1[:, k, P * m:P * m + P], xT[:, k, :],
                                        start=k == 0, stop=k == 1)
                    last.then_inc(s_p1, 1)
                for e in range(2):
                    for k in range(2):
                        last = t.matmul(banks[5 + e][:, :], eW1[:, e, k, :], xT[:, k, :], start=k == 0, stop=k == 1)
                    last.then_inc(s_q1, 1)
                pe.wait_ge(s_h1, it * 2 + 2)
                for k in range(2):
                    last = t.matmul(banks[4][:, :], sW2[:, k, :], h1[:, k, :], start=k == 0, stop=k == 1)
                last.then_inc(s_p2, 1)
                for e in range(2, NE):
                    for k in range(2):
                        last = t.matmul(banks[e][:, :], eW1[:, e, k, :], xT[:, k, :], start=k == 0, stop=k == 1)
                    last.then_inc(s_q1, 1)
                pe.wait_ge(s_h2, it + 1)
                pe.wait_ge(s_wg, it + 1)
                for u in range(BATCH):
                    last = t.transpose(banks[4][0:NE, P * u:P * u + P], wgt[:, u, :], ident[:, :])
                last.then_inc(s_wt, 1)
                for e in range(NE):
                    pe.wait_ge(s_he1, it * NE + max(e, 1) + 1)
                    last = t.matmul(banks[5 + e // 2][64 * (e % 2):64 * (e % 2) + 64, :], eW2[:, e, :], he1[:, e, :],
                                    start=True, stop=True)
                    if e % 2:
                        last.then_inc(s_q2, 1)
                pe.wait_ge(s_wT, it + 1)
                for a in range(2):
                    t.matmul(banks[a][:, :], expert_rows[:, P * a:P * a + P], wT[:, :], start=True, stop=True)\
                        .then_inc(s_wb, 1)
                def shared(u):
                    us = slice(P * u, P * u + P)
                    t.matmul(banks[2 + u % 2][:, 0:C], h2[:, us], sW3[:, :], start=True, stop=False)
                    t.matmul(banks[2 + u % 2][:, 0:C], wT[:, us], bias3[:, :], start=False, stop=False)
                pe.wait_ge(s_he1, it * NE + NE)
                shared(0)
                shared(1)
                pe.wait_ge(s_hw, it * 2 + 2)
                for u in range(BATCH):
                    if u >= 2:
                        pe.wait_ge(s_x, it * BATCH + u - 1)
                        shared(u)
                    for a in range(2):
                        last = t.matmul(banks[2 + u % 2][:, 0:C], he2[:, a, P * u:P * u + P], eW3[:, a, :],
                                        start=False, stop=a == 1)
                    last.then_inc(s_o, 1)

            pe.wait_ge(s_ready, 1)
            for l in range(2):
                spread(0, l)
                by_node(0, l)
            spread(0, 2)
            pe.wait_ge(s_w, 16 * LOADS3)
            pe.wait_ge(s_set, 2)
            all_segments(pe, lot, start, feed_forward)

        @block.scalar
        def _(act):
            s = nc.scalar

            def load_row(it, l):
                act.dma_start(row[l % 2][:, :, :], sh["list"][ds((it * LOTS + l) * (TILES * P), TILES * P), :]
                              .rearrange("(a e) w -> a e w", a=1)).then_inc(s_row[l % 2], 16)

            def transposed(it, l):
                n, m = it * LOTS + l, it * (LOTS // 2) + l // 2
                for q in range(2):
                    act.wait_ge(s_bc, n * 2 + q + 1)
                    s.activation(dist[:, q, :], banks[q][:, :], ACT.Abs, bias=minus_node[:, 0:1]).then_inc(s_dist, 1)
                    act.wait_ge(s_dist, n * 2 + q + 1)
                    wait_freed(act, s_as[l % 2], m)
                    s.activation(onehot_t[:, l % 2, q * QUAD:(q + 1) * QUAD, :].rearrange("p t e -> p (t e)"),
                                 dist[:, q, :], ACT.Relu, bias=1.0, scale=-1.0).then_inc(s_ot, 1)
                load_row(*after(it, l, 2))

            def weights(it, l):
                m = it * (LOTS // 2) + l // 2
                act.wait_ge(s_d[l % 2], m + 1)
                wait_freed(act, s_main[l % 2], m * GROUPS)
                s.activation(weighted[:, l % 2, :, C:TB], e[:, l % 2, :, :], ACT.Exp).then_inc(s_p[l % 2], 1)

            def lot(it, l):
                transposed(*after(it, l, 3))
                weights(*after(it, l, 2))

            def start(k):
                if not isinstance(k, int):
                    act.wait_ge(s_x, k * BATCH)
                    act.wait_ge(s_ready, 1)
                    act.dma_start(A["out"][ds((k - 1) * W4, W4), :].rearrange("(b p) c -> p b c", p=P), xo[:, :, :])\
                        .then_inc(s_out, 16)
                act.dma_start(x[:, :, :], sh["mixed"][ds(k * W4, W4), :].rearrange("(b p) c -> p b c", p=P))\
                    .then_inc(s_xin, 16)

            def feed_forward(it):
                act.wait_ge(s_var, it + 1)
                s.activation(std[:, :], inv[:, :], ACT.Sqrt).then_inc(s_std, 1)
                act.wait_ge(s_tr, it + 1)
                for k in range(2):
                    last = s.copy(xT[:, k, :], banks[k][:, :])
                last.then_inc(s_xT, 1)
                act.wait_ge(s_lgs, it + 1)
                s.activation(gate_e[:, :, :], gate[:, :, :], ACT.Exp).then_inc(s_ex, 1)
                for m in range(2):
                    act.wait_ge(s_p1, it * 2 + m + 1)
                    s.activation(h1[:, m, :], banks[2 + m][:, :], ACT.Relu, bias=sb1[:, m:m + 1]).then_inc(s_h1, 1)
                act.wait_ge(s_ga, it + 1)
                s.activation(gate_e[:, :, :], gate[:, :, :], ACT.Exp).then_inc(s_ga2, 1)
                for e in range(2):
                    act.wait_ge(s_q1, it * NE + e + 1)
                    s.activation(he1[:, e, :], banks[5 + e][:, :], ACT.Relu, bias=eb1[:, e:e + 1]).then_inc(s_he1, 1)
                act.wait_ge(s_p2, it + 1)
                s.activation(h2[:, :], banks[4][:, :], ACT.Relu, bias=sb2[:, 0:1]).then_inc(s_h2, 1)
                for e in range(2, NE):
                    act.wait_ge(s_q1, it * NE + e + 1)
                    s.activation(he1[:, e, :], banks[e][:, :], ACT.Relu, bias=eb1[:, e:e + 1]).then_inc(s_he1, 1)
                act.wait_ge(s_wt, it + 1)
                s.copy(wT[0:NE, :], banks[4][0:NE, :]).then_inc(s_wT, 1)
                for a in range(2):
                    act.wait_ge(s_q2, it * 2 + a + 1)
                    s.activation(he2[:, a, :], banks[5 + a][:, :], ACT.Relu, bias=eb2[:, a:a + 1]).then_inc(s_he2, 1)

            load_row(0, 0)
            load_row(0, 1)
            act.wait_ge(s_ready, 1)
            for l in range(2):
                transposed(0, l)
                weights(0, l)
            transposed(0, 2)
            act.wait_ge(s_w, 16 * LOADS3)
            all_segments(act, lot, start, feed_forward)
            end = act.value_load(bounds[0:1, ITERS:ITERS + 1], min_val=2, max_val=IT_MAX - 1)
            for i in range(2):
                act.wait_ge(s_row[i], end * (16 * (LOTS // 2)) + (48 - 16 * i))
            act.wait_ge(s_x, NBP)
            act.dma_start(A["out"][(NB - 1) * P:N, :], xo[0:TAIL, 0, :]).then_inc(s_out, 16)
            act.wait_ge(s_out, 16 * ITERS)

        @block.vector
        def _(dve):
            v = nc.vector
            done = [0]

            def step(ins):
                done[0] += 1
                ins.then_inc(s_dve, 1)
                dve.wait_ge(s_dve, done[0])

            def new_chain():
                done[0] = 0
                dve.sem_clear(s_dve)

            v.tensor_reduce(ad_max[:, :], ad[:, 0:NB, :].rearrange("p b h -> p h b"), AX.X, ALU.max).then_inc(s_max, 1)
            v.memset(acc[:, :, :], 0.0)
            v.memset(ones_bf[:, :], 1.0)
            v.memset(wT[:, :], 1.0)
            v.tensor_scalar(minus_node[:, :], node_col[:, :], -1.0, None, ALU.mult)
            dve.wait_ge(s_top, 1)
            step(v.tensor_tensor(t8[:, :, H:2 * H], t8[:, :, 0:H],
                                 ad_top[:, :].unsqueeze(1).broadcast_to([P, NBP, H]), ALU.add))
            v.scalar_tensor_tensor(t8[:, :, H:2 * H], t8[:, :, H:2 * H], SLOPE, t8[:, :, H:2 * H],
                                   ALU.mult, ALU.max).then_inc(s_ready, 1)

            def weigh(it, l):
                m, i = it * (LOTS // 2) + l // 2, l % 2
                wait_freed(dve, s_main[i], m * GROUPS)
                dve.wait_ge(s_col[l], 16 * it + 16)
                within = col[l][:, :, :, :].rearrange("p g k w -> p (g k) w")[:, :, 1:2].bitcast(F32)
                v.tensor_tensor(onehot[:, i, :, :], iota_row[:, :].unsqueeze(1).broadcast_to([P, TILES, P]),
                                within.broadcast_to([P, TILES, P]), ALU.is_equal).then_inc(s_sel[l], 1)
                new_chain()
                dve.wait_ge(s_gath[l], it * (16 * TILES) + 16 * TILES)
                dve.wait_ge(s_as[i], m + 1)
                from_node = banks[2 + i][:, 0:8 * TILES].rearrange("p (t w) -> p t w", w=8)
                step(v.tensor_tensor(z[:, i, :, :], gathered[:, l, :, C:TB], from_node[:, :, 0:H], ALU.add))
                step(v.scalar_tensor_tensor(z[:, i, :, :], z[:, i, :, :], SLOPE, z[:, i, :, :], ALU.mult, ALU.max))
                v.tensor_tensor(e[:, i, :, :], z[:, i, :, :], from_node[:, :, H:2 * H], ALU.subtract)\
                    .then_inc(s_d[i], 1)

            def product(it, l):
                m, i = it * (LOTS // 2) + l // 2, l % 2
                dve.wait_ge(s_p[i], m + 1)
                for g in range(GROUPS):
                    tiles = slice(g * G, g * G + G)
                    v.tensor_tensor(weighted[:, i, tiles, 0:C].rearrange("p k (a d) -> p k a d", d=HD),
                                    gathered[:, l, tiles, 0:C].rearrange("p k (a d) -> p k a d", d=HD),
                                    weighted[:, i, tiles, C:TB].unsqueeze(3).broadcast_to([P, G, H, HD]),
                                    ALU.mult).then_inc(s_mul[l], 1)

            def add(it, l):
                for g, b in enumerate(blocks_of(mybir.EngineType.DVE, it, l)):
                    dve.wait_ge(s_main[l % 2], (it * (LOTS // 2) + l // 2) * GROUPS + g + 1)
                    dve.wait_ge(s_ready, 1)
                    place = acc[:, ds(b, 1), :].rearrange("p a c -> p (a c)")
                    v.tensor_tensor(place, place, banks[4 + g][:, 0:TB], ALU.add).then_inc(s_sum[g], 1)
                    dve.wait_ge(s_sum[g], it * LOTS + l + 1)

            def lot(it, l):
                product(*after(it, l, 1))
                add(it, l)
                weigh(*after(it, l, 2))

            def feed_forward(it):
                new_chain()
                part = acc[:, ds(it * BATCH, BATCH), :]
                wait_freed(dve, s_out, 16 * it)
                step(v.tensor_scalar(recip[:, :, :], part[:, :, C:TB], 1e-37, None, ALU.max))
                step(v.reciprocal(recip[:, :, :], recip[:, :, :]))
                step(v.tensor_tensor(xf[:, :, :].rearrange("p b (a d) -> p b a d", d=HD),
                                     part[:, :, 0:C].rearrange("p b (a d) -> p b a d", d=HD),
                                     recip[:, :, :].unsqueeze(3).broadcast_to([P, BATCH, H, HD]), ALU.mult))
                dve.wait_ge(s_xin, 16 * it + 16)
                step(v.tensor_tensor(x[:, :, :], x[:, :, :], xf[:, :, :], ALU.add))
                for u in range(BATCH):
                    v.bn_stats(stats[:, u, :], x[:, u, :]).then_inc(s_dve, 1)
                done[0] += BATCH
                dve.wait_ge(s_dve, done[0])
                for u in range(BATCH):
                    v.bn_aggr(mv[:, u, :], stats[:, u, :]).then_inc(s_dve, 1)
                done[0] += BATCH
                dve.wait_ge(s_dve, done[0])
                v.tensor_scalar(inv[:, :], mv[:, :, 1], EPS_LN, None, ALU.add).then_inc(s_var, 1)
                dve.wait_ge(s_std, it + 1)
                step(v.reciprocal(inv[:, :], std[:, :]))
                for u in range(BATCH):
                    last = v.tensor_scalar(xf[:, u, :], x[:, u, :], mv[:, u, 0:1], inv[:, u:u + 1],
                                           ALU.subtract, ALU.mult)
                last.then_inc(s_xf, 1)
                dve.wait_ge(s_lg, it + 1)
                logits = banks[7][:, 0:BATCH * NE].rearrange("p (u e) -> p u e", e=NE)
                step(v.tensor_reduce(top[:, :], logits, AX.X, ALU.max))
                v.tensor_tensor(gate[:, :, :], logits, top[:, :].unsqueeze(2).broadcast_to([P, BATCH, NE]),
                                ALU.subtract).then_inc(s_lgs, 1)
                dve.wait_ge(s_ex, it + 1)
                step(v.tensor_reduce(top[:, :], gate_e[:, :, :], AX.X, ALU.add))
                step(v.reciprocal(top[:, :], top[:, :]))
                v.tensor_tensor(gate[:, :, :], gate_e[:, :, :], top[:, :].unsqueeze(2).broadcast_to([P, BATCH, NE]),
                                ALU.mult).then_inc(s_ga, 1)
                dve.wait_ge(s_ga, it + 1)
                mine = gate[:, :, :].unsqueeze(3).broadcast_to([P, BATCH, NE, NE])
                others = gate[:, :, :].unsqueeze(2).broadcast_to([P, BATCH, NE, NE])
                step(v.tensor_tensor(cmp2[:, :, :, :], others, mine, ALU.is_equal))
                step(v.tensor_tensor(cmp2[:, :, :, :], cmp2[:, :, :, :],
                                     lower[:, :, :].unsqueeze(1).broadcast_to([P, BATCH, NE, NE]), ALU.mult))
                step(v.tensor_tensor(cmp[:, :, :, :], others, mine, ALU.is_gt))
                step(v.tensor_tensor(cmp[:, :, :, :], cmp[:, :, :, :], cmp2[:, :, :, :], ALU.add))
                step(v.tensor_reduce(wgt[:, :, :], cmp[:, :, :, :], AX.X, ALU.add))
                dve.wait_ge(s_ga2, it + 1)
                step(v.scalar_tensor_tensor(wgt[:, :, :], wgt[:, :, :], 1.5, gate_e[:, :, :], ALU.is_lt, ALU.mult))
                step(v.tensor_reduce(top[:, :], wgt[:, :, :], AX.X, ALU.add))
                step(v.reciprocal(top[:, :], top[:, :]))
                v.tensor_tensor(wgt[:, :, :], wgt[:, :, :], top[:, :].unsqueeze(2).broadcast_to([P, BATCH, NE]),
                                ALU.mult).then_inc(s_wg, 1)
                for a in range(2):
                    dve.wait_ge(s_he2, it * 2 + a + 1)
                    dve.wait_ge(s_wb, it * 2 + a + 1)
                    v.tensor_tensor(he2[:, a, :], he2[:, a, :], banks[a][:, :], ALU.mult).then_inc(s_hw, 1)
                for u in range(BATCH):
                    dve.wait_ge(s_o, it * BATCH + u + 1)
                    v.tensor_tensor(xo[:, u, :], x[:, u, :], banks[2 + u % 2][:, 0:C], ALU.add).then_inc(s_x, 1)

            weigh(0, 0)
            product(0, 0)
            weigh(0, 1)
            dve.wait_ge(s_set, 2)
            all_segments(dve, lot, lambda k: None, feed_forward)


LOADS3 = 9 + 3 * NE + 4


def graph_layer(nc, A):
    ctx = ExitStack()
    with ctx:
        sb = lambda name, shape, dt=F32: ctx.enter_context(nc.sbuf_tensor(name, shape, dt))
        sh = {
            "ident": sb("ident", [P, P]), "iota_row": sb("iota_row", [P, P]), "ones_row": sb("ones_row", [1, P]),
            "node_col": sb("node_col", [P, 1]),
            "t8": sb("t8", [P, NBP, 2 * H]), "ad": sb("ad", [P, NBP, H]), "blk": sb("blk", [1, P * BLK_COLS], I32), "bounds": sb("bounds", [1, ITERS + 1], I32),
            "table": nc.dram_tensor("table", (NBP * P, TB), F32, kind="Internal").ap(),
            "mixed": nc.dram_tensor("mixed", (NBP * P, C), F32, kind="Internal").ap(),
            "list": nc.dram_tensor("edge_list", (LIST, 2), I32, kind="Internal").ap(),
            "blk_dram": nc.dram_tensor("blk_dram", (P * BLK_COLS,), I32, kind="Internal").ap(),
            "RMAX": bass.bass_isa.ReduceOp.max,
        }
        stage_sort_and_mix(nc, A, sh)
        stage_edges_and_feed_forward(nc, A, sh)


_INS = ["x", "src", "dst", "L0_gnn_W", "L0_gnn_b", "L0_gnn_a_src", "L0_gnn_a_dst", "L0_mix_Wqkv", "L0_mix_ln1_g",
        "L0_mix_ln1_b", "L0_mix_W1", "L0_mix_b1", "L0_mix_W2", "L0_mix_b2", "L0_mix_ln2_g", "L0_mix_ln2_b",
        "L0_ffn_sW1", "L0_ffn_sb1", "L0_ffn_sW2", "L0_ffn_sb2", "L0_ffn_sW3", "L0_ffn_sb3", "L0_ffn_eW1",
        "L0_ffn_eb1", "L0_ffn_eW2", "L0_ffn_eb2", "L0_ffn_eW3", "L0_ffn_eb3", "L0_ffn_gW", "L0_ffn_gb"]


def kernel(**inputs):
    import concourse.bacc as _bacc
    from concourse.bass_utils import run_bass_kernel_spmd as _run

    nc = _bacc.Bacc("TRN2", target_bir_lowering=False, num_devices=1)
    arrays, args = {}, {}
    for name in _INS:
        a = np.ascontiguousarray(inputs[name])
        arrays[f"in_{name}"] = a
        args[name] = nc.dram_tensor(f"in_{name}", a.shape, mybir.dt.from_np(a.dtype), kind="ExternalInput").ap()
    args["out"] = nc.dram_tensor("out", (N, C), F32, kind="ExternalOutput").ap()
    graph_layer(nc, args)
    r = _run(nc, [arrays], core_ids=[0])
    return r.results[0]["out"]
```

```python
import numpy as np
import concourse.bass as bass
from concourse import mybir
from contextlib import ExitStack

F32, BF16, I32, U16 = mybir.dt.float32, mybir.dt.bfloat16, mybir.dt.int32, mybir.dt.uint16
ALU = mybir.AluOpType
ACT = mybir.ActivationFunctionType
AX = mybir.AxisListType
ds = bass.ds

P = 128
N, C, H = 6250, 256, 4
HD = C // H
E_ALL = 206250
NB = -(-N // P)
TAIL = N - (NB - 1) * P
BATCH = 4
NBP = -(-NB // BATCH) * BATCH
ITERS = NBP // BATCH
TAIL_BATCH, LAST_BATCH = ITERS - 1, ITERS - 2
W4 = BATCH * P
NBK = NB + 1
TE = -(-E_ALL // P)
TE_LAST = E_ALL - (P - 1) * TE
SUB = 31
SUBS = (16, 15)
FIRST_UNITS, PART_UNITS = 2, 10
PARTS = (TE // SUB - FIRST_UNITS) // PART_UNITS
PART = PART_UNITS * SUB
G = 2
GR = G * P
GROUPS = 4
LOTS = 6
IT_MAX = -(-((E_ALL + NB * (GR - 1)) // GR) // (LOTS * GROUPS)) + 2 * ITERS
NG = (IT_MAX * LOTS + 4) * GROUPS
BLK_COLS = -(-NG // P)
LIST = (NG + 1) * GR
TB = C + H
NO_NODE = 200.0
NO_TARGET = NBP * P
TINY_SUM, BOUND_GAP, LOWER_BY, MAX_SWEEPS = 1e-20, 46.0, 40.0, 16000
EPS_LN, EPS_ATTN, SLOPE = 1e-5, 1e-6, 0.2
MH, MD = 8, 32
KVC = 132
SH1, SH2, EH1, EH2, NE = 256, 128, 128, 64, 4
BUCKETS_A_TURN = 10
assert NB - (ITERS - 1) * BATCH == 1
assert NBP - NB >= 2
assert TE == (FIRST_UNITS + PARTS * PART_UNITS) * SUB and sum(SUBS) == SUB
assert NBK % BUCKETS_A_TURN == 0 and NB <= NBK < P


def wait_freed(engine, semaphore, count):
    if not (isinstance(count, int) and count == 0):
        engine.wait_ge(semaphore, count)


def first_and_rest(engine, count, body):
    body(0)
    with engine.Fori(1, count) as it:
        body(it)


def stage_sort_and_mix(nc, A, sh):
    ctx = ExitStack()
    with ctx:
        sb = lambda name, shape, dt=F32: ctx.enter_context(nc.sbuf_tensor(name, shape, dt))
        sem = lambda name: ctx.enter_context(nc.semaphore(name))
        x = sb("x_all", [P, NBP, C])
        xn = sb("xn_all", [P, NBP, C])
        ident, iota_row, ones_row = sh["ident"], sh["iota_row"], sh["ones_row"]
        node_col = sh["node_col"]
        banks = [ctx.enter_context(nc.psum_tensor(f"bank1_{i}", [P, 512], F32)) for i in range(8)]

        pos = sb("pos", [P, TE], I32)
        payload = sb("payload", [P, TE, 2], I32)
        spare = xn[:, :, :].rearrange("p b c -> p (b c)")
        at = [0]

        def carve(words):
            at[0] += words
            return spare[:, at[0] - words:at[0]]

        src_i = carve(TE).bitcast(I32)
        dst_i = carve(TE).bitcast(I32)
        int_tmp = carve(TE).bitcast(I32)
        bucket = carve(TE // 2).bitcast(BF16)
        hit = [carve(TE // 2).bitcast(BF16) for i in range(2)]
        running = [carve(PART).bitcast(I32) for i in range(2)]
        places = carve(PART).bitcast(I32)
        pad_rows = carve(2 * (LIST // (2 * P))).rearrange("p (r w) -> p r w", w=2)
        grp_cmp = carve(BLK_COLS * (NB - 1))
        assert at[0] <= NBP * C
        counts = sb("counts", [P, NBK])
        totals = sb("totals", [P, NBK])
        grp_i = sb("grp_i", [P, NBK], I32)
        grp_end = sb("grp_end", [P, NBK])
        base = sb("base", [P, NBK])
        carry = sb("carry", [P, NBK])
        grp_no = sb("grp_no", [P, BLK_COLS])
        grp_blk = sb("grp_blk", [P, BLK_COLS])
        grp_blk_i = sb("grp_blk_i", [P, BLK_COLS], I32)
        it_cmp = sb("it_cmp", [P, ITERS, IT_MAX])
        it_end = sb("it_end", [P, ITERS + 1])
        it_least = sb("it_least", [P, ITERS])
        before = sb("before", [P, P])
        ones_sq = sb("ones_sq", [P, P])
        stage_pos = [sb(f"stage_pos{i}", [P, SUBS[i]], I32) for i in range(2)]
        stage_pay = [sb(f"stage_pay{i}", [P, SUBS[i], 2], I32) for i in range(2)]

        NW = 3 * C + 3 * C
        w_nat = sb("w_nat", [P, NW // P, C])
        wT = sb("wT", [P, 2, NW])
        QKV, WG, W1, W2 = 0, 3 * C, 4 * C, 5 * C
        a_mat = sb("a_mat", [P, 2, 2 * H])
        b_col = sb("b_col", [P, 2])
        b_row = sb("b_row", [1, C + 2 * H])
        g_w = sb("g_w", [P, 2, C + 2 * H])
        b1_col = sb("b1_col", [P, 2])
        b2_row = sb("b2_row", [1, C])
        ln = sb("ln", [P, 4, C])
        valid = sb("valid", [P, NBP])
        tail_rows = sb("tail_rows", [P, 1])
        tail_groups = sb("tail_groups", [P, 1])
        kv_bd = sb("kv_bd", [P, 2, KVC])

        stats = sb("stats", [P, BATCH, 6])
        mv = sb("mv", [P, BATCH, 2])
        std = sb("std", [P, BATCH])
        inv = sb("inv", [P, BATCH])
        xT = sb("xT", [P, 2, W4])
        wh = sb("wh", [P, BATCH, C + 2 * H])
        k_min = sb("k_min", [P, 2, C])
        k_exp = sb("k_exp", [P, 2, C])
        kk = sb("kk", [P, 2, C])
        vv = sb("vv", [P, 2, 2, KVC])
        q_min = sb("q_min", [P, 2, W4])
        qT = sb("qT", [P, 2, W4])
        den = sb("den", [P, BATCH, MH])
        y = sb("y", [P, BATCH, C])
        x1 = sb("x1", [P, BATCH, C])

        (s_pads_set, s_src, s_dst, s_x, s_w, s_misc, s_fill, s_filled, s_const) = map(sem, (
            "s_pads_set", "s_src", "s_dst", "s_x", "s_w", "s_misc", "s_fill", "s_filled", "s_const"))
        (s_counts, s_base, s_pos, s_staged0, s_staged1, s_scat0, s_scat1, s_blk, s_blkd, s_blkr) = map(sem, (
            "s_counts", "s_base", "s_pos", "s_staged0", "s_staged1", "s_scat0", "s_scat1", "s_blk", "s_blkd", "s_blkr"))
        (s_wtr, s_wtc, s_gw, s_gwc, s_kv0) = map(sem, ("s_wtr", "s_wtc", "s_gw", "s_gwc", "s_kv0"))
        (s_var, s_std, s_xn, s_tr, s_xT, s_g, s_wh, s_tab, s_kv, s_kmin, s_kexp, s_vc, s_kk, s_acc, s_nd) = map(sem, (
            "s_var", "s_std", "s_xn", "s_tr", "s_xT", "s_g", "s_wh", "s_tab", "s_kv", "s_kmin", "s_kexp", "s_vc",
            "s_kk", "s_acc", "s_nd"))
        (s_bd, s_tr2, s_xT2, s_q, s_qmin, s_qexp, s_qT, s_t, s_var2, s_std2, s_x1, s_tr3, s_xT3, s_h, s_h1, s_y2,
         s_y2r) = map(sem, ("s_bd", "s_tr2", "s_xT2", "s_q", "s_qmin", "s_qexp", "s_qT", "s_t", "s_var2", "s_std2",
                            "s_x1", "s_tr3", "s_xT3", "s_h", "s_h1", "s_y2", "s_y2r"))
        s_dve, s_pool, s_xc, s_mixed, s_mout, s_zero_row = map(sem, (
            "s_dve", "s_pool", "s_xc", "s_mixed", "s_mout", "s_zero_row"))
        s_staged, s_scat = (s_staged0, s_staged1), (s_scat0, s_scat1)
        block = ctx.enter_context(nc.Block())

        @block.sync
        def _(sp):
            sp.wait_ge(s_pads_set, 4)
            for dst, src, s in ((src_i, A["src"], s_src), (dst_i, A["dst"], s_dst)):
                sp.dma_start(dst[0:P - 1, :], src[0:(P - 1) * TE].rearrange("(p t) -> p t", t=TE)).then_inc(s, 16)
                sp.dma_start(dst[P - 1:P, 0:TE_LAST],
                             src[(P - 1) * TE:E_ALL].rearrange("(p t) -> p t", p=1)).then_inc(s, 16)
            sp.dma_start(w_nat[:, 0:6, :], A["L0_mix_Wqkv"].rearrange("(a p) c -> p a c", p=P)).then_inc(s_w, 16)
            for i, name in enumerate(("L0_gnn_W", "L0_mix_W1", "L0_mix_W2")):
                sp.dma_start(w_nat[:, 6 + 2 * i:8 + 2 * i, :],
                             A[name].rearrange("(a p) c -> p a c", p=P)).then_inc(s_w, 16)
            for i, name in enumerate(("L0_gnn_a_dst", "L0_gnn_a_src")):
                for h in range(H):
                    sp.dma_start(a_mat[HD * (h % 2):HD * (h % 2) + HD, h // 2, H * i + h:H * i + h + 1],
                                 A[name][h, :].rearrange("(d a) -> d a", a=1)).then_inc(s_misc, 16)
            sp.dma_start(b_row[:, 0:C], A["L0_gnn_b"].rearrange("(a c) -> a c", a=1)).then_inc(s_misc, 16)
            sp.dma_start(b2_row[:, :], A["L0_mix_b2"].rearrange("(a c) -> a c", a=1)).then_inc(s_misc, 16)
            for dst, name in ((b_col, "L0_gnn_b"), (b1_col, "L0_mix_b1")):
                for a in range(2):
                    sp.dma_start(dst[:, a:a + 1],
                                 A[name][a * P:(a + 1) * P].rearrange("(p a) -> p a", a=1)).then_inc(s_misc, 16)
            for i, name in enumerate(("ln1_g", "ln1_b", "ln2_g", "ln2_b")):
                sp.dma_start(ln[:, i, :], A["L0_mix_" + name].partition_broadcast(P)).then_inc(s_misc, 16)
            sp.dma_start(x[:, 0:NB - 1, :],
                         A["x"][0:(NB - 1) * P, :].rearrange("(b p) c -> p b c", p=P)).then_inc(s_x, 16)
            sp.dma_start(x[0:TAIL, NB - 1, :], A["x"][(NB - 1) * P:N, :]).then_inc(s_x, 16)
            sp.dma_start(sh["table"][NO_TARGET:NO_TARGET + 1, :],
                         x[0:1, NB:NB + 2, :].rearrange("p b c -> p (b c)")[:, 0:TB]).then_inc(s_zero_row, 16)
            sp.wait_ge(s_fill, 2)
            for half in range(2):
                sp.dma_start(sh["list"][half * (LIST // 2):(half + 1) * (LIST // 2), :]
                             .rearrange("(p r) w -> p r w", p=P), pad_rows.bitcast(I32)).then_inc(s_filled, 16)
            def columns(it):
                first = 0
                for half, n in enumerate(SUBS):
                    wait_freed(sp, s_scat[half], it * (16 * n))
                    sp.dma_start(stage_pos[half][:, :], pos[:, ds(it * SUB + first, n)]).then_inc(s_staged[half], 16)
                    sp.dma_start(stage_pay[half][:, :, :], payload[:, ds(it * SUB + first, n), :])\
                        .then_inc(s_staged[half], 16)
                    first += n

            sp.wait_ge(s_pos, 1)
            first_and_rest(sp, FIRST_UNITS, columns)
            sp.wait_ge(s_blk, 1)
            sp.dma_start(sh["blk_dram"].rearrange("(p r) -> p r", r=BLK_COLS), grp_blk_i[:, :]).then_inc(s_blkd, 16)
            sp.wait_ge(s_blkd, 16)
            sp.dma_start(sh["blk"][0:1, :], sh["blk_dram"].rearrange("(a g) -> a g", a=1)).then_inc(s_blkr, 16)
            sp.wait_ge(s_blkr, 16)
            sp.wait_ge(s_zero_row, 16)
            for part in range(PARTS):
                sp.wait_ge(s_pos, part + 2)
                first = FIRST_UNITS + part * PART_UNITS
                with sp.Fori(first, first + PART_UNITS) as it:
                    columns(it)

        @block.gpsimd
        def _(pool):
            g = nc.gpsimd
            done = [0]

            def step(ins):
                done[0] += 1
                ins.then_inc(s_pool, 1)
                pool.wait_ge(s_pool, done[0])

            step(g.memset(ident[:, :], 0.0))
            step(g.affine_select(out=ident[:, :], in_=ident[:, :], compare_op=ALU.not_equal, fill=1.0, base=0,
                                 pattern=[[-1, P]], channel_multiplier=1))
            step(g.memset(ones_sq[:, :], 1.0))
            step(g.affine_select(out=before[:, :], in_=ones_sq[:, :], compare_op=ALU.is_gt, fill=0.0, base=0,
                                 pattern=[[1, P]], channel_multiplier=-1))
            step(g.iota(iota_row[:, :], [[1, P]], base=0, channel_multiplier=0, allow_small_or_imprecise_dtypes=True))
            step(g.iota(node_col[:, :], [[1, 1]], base=0, channel_multiplier=1, allow_small_or_imprecise_dtypes=True))
            step(g.iota(grp_no[:, :], [[1, BLK_COLS]], base=0, channel_multiplier=BLK_COLS,
                        allow_small_or_imprecise_dtypes=True))
            step(g.affine_select(out=tail_rows[:, :], in_=ones_sq[:, 0:1], compare_op=ALU.is_gt, fill=0.0, base=TAIL,
                                 pattern=[[0, 1]], channel_multiplier=-1))
            g.memset(ones_row[:, :], 1.0).then_inc(s_const, 1)
            g.memset(pad_rows[:, :, 0].bitcast(I32), NO_TARGET).then_inc(s_fill, 1)
            g.memset(pad_rows[:, :, 1], NO_NODE).then_inc(s_fill, 1)
            due = [pool.alloc_register(f"due_staged{half}") for half in range(2)]
            for half in range(2):
                pool.reg_mov(due[half], 32)
            pool.wait_ge(s_filled, 32)
            with pool.Fori(0, TE // SUB) as it:
                for half, n in enumerate(SUBS):
                    pool.wait_ge(s_staged[half], due[half])
                    pool.reg_add(due[half], due[half], 32)
                    for t in range(n):
                        g.indirect_dma_start(sh["list"], bass.IndirectOffsetOnAxis(ap=stage_pos[half][:, t:t + 1], axis=0),
                                             stage_pay[half][:, t, :], None).then_inc(s_scat[half], 16)
            for half, n in enumerate(SUBS):
                pool.wait_ge(s_scat[half], 16 * n * (TE // SUB))

        @block.vector
        def _(dve):
            v = nc.vector
            done = [0]

            def step(ins):
                done[0] += 1
                ins.then_inc(s_dve, 1)
                dve.wait_ge(s_dve, done[0])

            last_t = slice(TE_LAST, TE)
            v.memset(src_i[96:P, last_t], NB * P).then_inc(s_pads_set, 1)
            v.memset(dst_i[96:P, last_t], 0).then_inc(s_pads_set, 1)
            v.memset(a_mat[:, :, :], 0.0).then_inc(s_pads_set, 1)
            v.memset(x[:, NB - 1:NBP, :], 0.0).then_inc(s_pads_set, 1)
            dve.wait_ge(s_src, 32)
            step(v.tensor_scalar(int_tmp, src_i, 7, None, ALU.logical_shift_right))
            step(v.tensor_copy(bucket, int_tmp))
            dve.wait_ge(s_const, 1)
            with dve.Fori(0, NBK // BUCKETS_A_TURN) as turn:
                for i in range(BUCKETS_A_TURN):
                    b = turn * BUCKETS_A_TURN + i
                    if i >= 2:
                        dve.wait_ge(s_counts, b - 1)
                    v.tensor_scalar(hit[i % 2], bucket, iota_row[:, ds(b, 1)], 0.0, ALU.is_equal, ALU.add,
                                    accum_out=counts[:, ds(b, 1)]).then_inc(s_counts, 1)
                dve.wait_ge(s_counts, (turn + 1) * BUCKETS_A_TURN)
            step(v.tensor_scalar(int_tmp, src_i, P - 1, None, ALU.bitwise_and))
            step(v.tensor_copy(payload[:, :, 1].bitcast(F32), int_tmp))
            dve.wait_ge(s_dst, 32)
            step(v.tensor_copy(payload[:, :, 0], dst_i))
            dve.wait_ge(s_base, 1)
            step(v.tensor_scalar(totals[:, :], banks[7][:, 0:NBK], float(GR - 1), None, ALU.add))
            step(v.tensor_copy(grp_i[:, :], totals[:, :]))
            step(v.tensor_scalar(grp_i[:, :], grp_i[:, :], GR.bit_length() - 1, None, ALU.logical_shift_right))
            step(v.tensor_copy(totals[:, :], grp_i[:, :]))
            step(v.tensor_tensor_scan(grp_end[:, :], totals[:, :], totals[:, :], 0.0, ALU.add, ALU.bypass))
            step(v.tensor_copy(tail_groups[:, :], totals[:, NB - 1:NB]))
            step(v.tensor_scalar(grp_end[:, 0:NB - 1], grp_end[:, 0:NB - 1], tail_groups[:, 0:1], None, ALU.add))
            step(v.tensor_copy(grp_end[:, NB - 1:NB], tail_groups[:, :]))
            step(v.tensor_tensor(totals[:, :], grp_end[:, :], totals[:, :], ALU.subtract))
            step(v.memset(totals[:, NB:NBK], float(NG)))
            step(v.scalar_tensor_tensor(base[:, :], totals[:, :], float(GR), banks[7][:, 64:64 + NBK], ALU.mult, ALU.add))
            step(v.tensor_scalar(carry[:, :], base[:, :], -1.0, None, ALU.add))
            def part_places(first, width, number):
                def counted(ins):
                    done[0] += 1
                    ins.then_inc(s_dve, 1)

                with dve.Fori(0, NBK // BUCKETS_A_TURN) as turn:
                    done[0] = 0
                    dve.sem_clear(s_dve)
                    for pair in range(BUCKETS_A_TURN // 2):
                        buckets = [turn * BUCKETS_A_TURN + 2 * pair + i for i in range(2)]
                        so_far = 8 * pair
                        for i, b in enumerate(buckets):
                            if pair:
                                dve.wait_ge(s_dve, so_far - (0 if i else 3))
                            counted(v.tensor_scalar(hit[i][:, 0:width], bucket[:, ds(first, width)],
                                                    iota_row[:, ds(b, 1)], None, ALU.is_equal))
                        for i, b in enumerate(buckets):
                            dve.wait_ge(s_dve, so_far + 1 + i)
                            counted(v.tensor_tensor_scan(running[i][:, 0:width], hit[i][:, 0:width],
                                                         hit[i][:, 0:width], carry[:, ds(b, 1)],
                                                         ALU.add, ALU.bypass))
                        dve.wait_ge(s_dve, so_far + 3)
                        counted(v.copy_predicated(places[:, 0:width], hit[0][:, 0:width].bitcast(U16),
                                                  running[0][:, 0:width]))
                        counted(v.tensor_copy(carry[:, ds(buckets[0], 1)], running[0][:, width - 1:width]))
                        dve.wait_ge(s_dve, so_far + 4)
                        counted(v.tensor_copy(carry[:, ds(buckets[1], 1)], running[1][:, width - 1:width]))
                        dve.wait_ge(s_dve, so_far + 5)
                        counted(v.copy_predicated(places[:, 0:width], hit[1][:, 0:width].bitcast(U16),
                                                  running[1][:, 0:width]))
                    dve.wait_ge(s_dve, done[0])
                v.tensor_copy(pos[:, ds(first, width)], places[:, 0:width]).then_inc(s_pos, 1)
                dve.wait_ge(s_pos, number)

            part_places(0, FIRST_UNITS * SUB, 1)
            done[0] = 0
            dve.sem_clear(s_dve)
            ge = grp_cmp.rearrange("p (r b) -> p r b", b=NB - 1)
            step(v.tensor_tensor(ge, grp_no[:, :].unsqueeze(2).broadcast_to([P, BLK_COLS, NB - 1]),
                                 grp_end[:, 0:NB - 1].unsqueeze(1).broadcast_to([P, BLK_COLS, NB - 1]), ALU.is_ge))
            step(v.tensor_reduce(grp_blk[:, :], ge, AX.X, ALU.add))
            step(v.tensor_scalar(grp_no[:, :], grp_no[:, :], tail_groups[:, 0:1], None, ALU.is_lt))
            step(v.tensor_scalar(grp_no[:, :], grp_no[:, :], float(NB - 1), None, ALU.mult))
            step(v.tensor_tensor(grp_blk[:, :], grp_blk[:, :], grp_no[:, :], ALU.add))
            v.tensor_copy(grp_blk_i[:, :], grp_blk[:, :]).then_inc(s_blk, 1)
            for k in range(ITERS):
                last_block = BATCH * k - 1 if k else NB - 1
                last = v.tensor_scalar(it_cmp[:, k, :], iota_row[:, 0:IT_MAX], float(LOTS * GROUPS),
                                       grp_end[:, last_block:last_block + 1], ALU.mult, ALU.is_lt)
            step(last)
            step(v.memset(it_end[:, 0:1], 1.0))
            step(v.tensor_reduce(it_end[:, 1:ITERS + 1], it_cmp[:, :, :], AX.X, ALU.add))
            step(v.memset(it_least[:, :], 2.0))
            step(v.memset(it_least[:, 1:2], 1.0))
            step(v.tensor_tensor_scan(it_cmp[:, :, 0], it_least[:, :], it_end[:, 1:ITERS + 1], 0.0, ALU.add, ALU.max))
            step(v.tensor_copy(it_end[:, 1:ITERS + 1], it_cmp[:, :, 0]))
            step(v.tensor_copy(sh["bounds"][:, :], it_end[0:1, :]))
            with dve.Fori(0, PARTS) as part:
                part_places(part * PART + FIRST_UNITS * SUB, PART, part + 2)
            done[0] = 0
            dve.sem_clear(s_dve)
            done[0] = 0
            dve.sem_clear(s_dve)
            step(v.memset(valid[:, :], 1.0))
            step(v.memset(valid[:, NB - 1:NBP], 0.0))
            step(v.tensor_copy(valid[:, NB - 1:NB], tail_rows[:, :]))
            step(v.memset(kv_bd[:, :, :], 0.0))
            dve.wait_ge(s_gwc, 1)
            v.memset(banks[6][:, 0:258], 0.0).then_inc(s_kv0, 1)
            dve.wait_ge(s_x, 32)
            dve.wait_ge(s_filled, 32)

            def one_turn(it):
                done[0] = 0
                dve.sem_clear(s_dve)
                for u in range(BATCH):
                    v.bn_stats(stats[:, u, :], x[:, ds(it * BATCH + u, 1), :].rearrange("p a c -> p (a c)"))\
                        .then_inc(s_dve, 1)
                done[0] += BATCH
                dve.wait_ge(s_dve, done[0])
                for u in range(BATCH):
                    v.bn_aggr(mv[:, u, :], stats[:, u, :]).then_inc(s_dve, 1)
                done[0] += BATCH
                dve.wait_ge(s_dve, done[0])
                v.tensor_scalar(inv[:, :], mv[:, :, 1], EPS_LN, None, ALU.add).then_inc(s_var, 1)
                dve.wait_ge(s_std, it + 1)
                step(v.reciprocal(inv[:, :], std[:, :]))
                for u in range(BATCH):
                    last = v.tensor_scalar(y[:, u, :],
                                           x[:, ds(it * BATCH + u, 1), :].rearrange("p a c -> p (a c)"),
                                           mv[:, u, 0:1], inv[:, u:u + 1], ALU.subtract, ALU.mult)
                last.then_inc(s_xn, 1)
                dve.wait_ge(s_xn, it + 1)
                v.tensor_copy(xn[:, ds(it * BATCH, BATCH), :], y[:, :, :])
                for u in range(BATCH):
                    bank = banks[4 + u % 2]
                    dve.wait_ge(s_kv, it * BATCH + u + 1)
                    v.tensor_scalar(k_min[:, u % 2, :], bank[:, 0:C], 0.0, None, ALU.min).then_inc(s_kmin, 1)
                    wait_freed(dve, s_acc, it * BATCH + max(u - 1, 0))
                    v.tensor_copy(vv[:, u % 2, :, P:P + 1],
                                  valid[:, ds(it * BATCH + u, 1)].unsqueeze(1).broadcast_to([P, 2, 1])).then_inc(s_nd, 1)
                    dve.wait_ge(s_kexp, it * BATCH + u + 1)
                    dve.wait_ge(s_vc, it * BATCH + u + 1)
                    v.scalar_tensor_tensor(kk[:, u % 2, :], bank[:, 0:C], 0.0, k_exp[:, u % 2, :], ALU.max, ALU.add)\
                        .then_inc(s_kk, 1)

            first_and_rest(dve, ITERS, one_turn)

            dve.wait_ge(s_acc, NBP)
            for half in range(2):
                for j in range(4):
                    r = slice(MD * j, MD * j + MD)
                    o = half * 129
                    v.tensor_copy(kv_bd[r, half, MD * j:MD * j + MD], banks[6][r, o + MD * j:o + MD * j + MD])
                    last = v.tensor_copy(kv_bd[r, half, P + j:P + j + 1], banks[6][r, o + P:o + P + 1])
            last.then_inc(s_bd, 1)

            def one_turn(it):
                done[0] = 0
                dve.sem_clear(s_dve)

                def norm(count, gamma):
                    for u in range(BATCH):
                        v.bn_stats(stats[:, u, :], y[:, u, :]).then_inc(s_dve, 1)
                    done[0] += BATCH
                    dve.wait_ge(s_dve, done[0])
                    for u in range(BATCH):
                        v.bn_aggr(mv[:, u, :], stats[:, u, :]).then_inc(s_dve, 1)
                    done[0] += BATCH
                    dve.wait_ge(s_dve, done[0])
                    v.tensor_scalar(inv[:, :], mv[:, :, 1], EPS_LN, None, ALU.add).then_inc(s_var2, 1)
                    dve.wait_ge(s_std2, it * 2 + count)
                    step(v.reciprocal(inv[:, :], std[:, :]))
                    for u in range(BATCH):
                        last = v.tensor_scalar(y[:, u, :], y[:, u, :], mv[:, u, 0:1], inv[:, u:u + 1],
                                               ALU.subtract, ALU.mult)
                    step(last)
                    step(v.tensor_tensor(y[:, :, :], y[:, :, :],
                                         ln[:, gamma, :].unsqueeze(1).broadcast_to([P, BATCH, C]), ALU.mult))

                v.tensor_copy(y[:, :, :], xn[:, ds(it * BATCH, BATCH), :]).then_inc(s_xc, 1)
                for m in range(2):
                    dve.wait_ge(s_q, it * 2 + m + 1)
                    v.tensor_scalar(q_min[:, m, :], banks[2 + m][:, :], 0.0, None, ALU.min).then_inc(s_qmin, 1)
                for m in range(2):
                    dve.wait_ge(s_qexp, it * 2 + m + 1)
                    v.scalar_tensor_tensor(qT[:, m, :], banks[2 + m][:, :], 0.0, q_min[:, m, :], ALU.max, ALU.add)\
                        .then_inc(s_qT, 1)
                for u in range(BATCH):
                    halves = banks[4 + u][:, 0:2 * KVC].rearrange("p (a w) -> p a w", w=KVC)
                    dve.wait_ge(s_t, it * BATCH + u + 1)
                    step(v.tensor_scalar(den[:, u, :].rearrange("p (a h) -> p a h", a=2), halves[:, :, P:KVC],
                                         EPS_ATTN, None, ALU.add))
                    step(v.reciprocal(den[:, u, :], den[:, u, :]))
                    for a in range(2):
                        last = v.tensor_tensor(
                            y[:, u, a * P:(a + 1) * P].rearrange("p (h d) -> p h d", d=MD),
                            halves[:, a, 0:P].rearrange("p (h d) -> p h d", d=MD),
                            den[:, u, 4 * a:4 * a + 4].unsqueeze(2).broadcast_to([P, 4, MD]), ALU.mult)
                    step(last)
                step(v.tensor_tensor(y[:, :, :], y[:, :, :], xn[:, ds(it * BATCH, BATCH), :], ALU.add))
                norm(1, 0)
                v.tensor_tensor(x1[:, :, :], y[:, :, :], ln[:, 1, :].unsqueeze(1).broadcast_to([P, BATCH, C]), ALU.add)\
                    .then_inc(s_x1, 1)
                for u in range(BATCH):
                    dve.wait_ge(s_y2, it * BATCH + u + 1)
                    last = v.tensor_tensor(y[:, u, :], banks[4 + u][:, 0:C], x1[:, u, :], ALU.add)
                last.then_inc(s_y2r, 1)
                dve.wait_ge(s_y2r, it + 1)
                norm(2, 2)
                step(v.tensor_tensor(y[:, :, :], y[:, :, :],
                                     ln[:, 3, :].unsqueeze(1).broadcast_to([P, BATCH, C]), ALU.add))
                v.tensor_tensor(x[:, ds(it * BATCH, BATCH), :], x[:, ds(it * BATCH, BATCH), :], y[:, :, :], ALU.add)\
                    .then_inc(s_mixed, 1)
                dve.wait_ge(s_mixed, it + 1)

            first_and_rest(dve, ITERS, one_turn)

        @block.scalar
        def _(act):
            s = nc.scalar
            for i in range(2 * NW // 512):
                act.wait_ge(s_wtr, i + 1)
                s.copy(wT[:, i // 3, 512 * (i % 3):512 * (i % 3) + 512], banks[i][:, :]).then_inc(s_wtc, 1)
            act.wait_ge(s_gw, 1)
            for k in range(2):
                s.copy(g_w[:, k, C:C + 2 * H], banks[6][:, 8 * k:8 * k + 8])
            s.copy(b_row[:, C:C + 2 * H], banks[6][0:1, 16:24])
            act.wait_ge(s_wtc, 6)
            s.copy(g_w[:, :, 0:C], wT[:, :, WG:WG + C]).then_inc(s_gwc, 1)
            def one_turn(it):
                act.wait_ge(s_var, it + 1)
                s.activation(std[:, :], inv[:, :], ACT.Sqrt).then_inc(s_std, 1)
                act.wait_ge(s_tr, it + 1)
                for k in range(2):
                    last = s.copy(xT[:, k, :], banks[k][:, :])
                last.then_inc(s_xT, 1)
                for u in range(BATCH):
                    n = it * BATCH + u
                    act.wait_ge(s_g, n + 1)
                    if u == 0:
                        wait_freed(act, s_tab, it * 16)
                        act.wait_ge(s_gwc, 1)
                    s.copy(wh[:, u, :], banks[2 + u % 2][:, 0:C + 2 * H]).then_inc(s_wh, 1)
                    act.wait_ge(s_kmin, n + 1)
                    s.activation(k_exp[:, u % 2, :], k_min[:, u % 2, :], ACT.Exp).then_inc(s_kexp, 1)
                    act.wait_ge(s_nd, n + 1)
                    s.copy(vv[:, u % 2, :, 0:P], banks[4 + u % 2][:, C:2 * C].rearrange("p (a d) -> p a d", a=2))\
                        .then_inc(s_vc, 1)
                act.wait_ge(s_wh, it * BATCH + BATCH)
                act.wait_ge(s_gwc, 1)
                act.dma_start(sh["table"][ds(it * W4, W4), :].rearrange("(b p) c -> p b c", p=P),
                              wh[:, :, 0:TB]).then_inc(s_tab, 16)
                s.copy(sh["ad"][:, ds(it * BATCH, BATCH), :], wh[:, :, C:C + H])
                s.copy(sh["t8"][:, ds(it * BATCH, BATCH), 0:H], wh[:, :, C + H:C + 2 * H])

            first_and_rest(act, ITERS, one_turn)
            def one_turn(it):
                act.wait_ge(s_tr2, it + 1)
                for k in range(2):
                    last = s.copy(xT[:, k, :], banks[k][:, :])
                last.then_inc(s_xT2, 1)
                for m in range(2):
                    act.wait_ge(s_qmin, it * 2 + m + 1)
                    s.activation(q_min[:, m, :], q_min[:, m, :], ACT.Exp).then_inc(s_qexp, 1)
                act.wait_ge(s_var2, it * 2 + 1)
                s.activation(std[:, :], inv[:, :], ACT.Sqrt).then_inc(s_std2, 1)
                act.wait_ge(s_tr3, it + 1)
                for k in range(2):
                    last = s.copy(xT[:, k, :], banks[k][:, :])
                last.then_inc(s_xT3, 1)
                for m in range(2):
                    act.wait_ge(s_h, it * 2 + m + 1)
                    s.activation(qT[:, m, :], banks[2 + m][:, :], ACT.Gelu, bias=b1_col[:, m:m + 1]).then_inc(s_h1, 1)
                act.wait_ge(s_var2, it * 2 + 2)
                s.activation(std[:, :], inv[:, :], ACT.Sqrt).then_inc(s_std2, 1)
                if not isinstance(it, int):
                    mixed_out(it - 1)

            def mixed_out(it):
                act.wait_ge(s_mixed, it + 1)
                act.wait_ge(s_gwc, 1)
                act.dma_start(sh["mixed"][ds(it * W4, W4), :].rearrange("(b p) c -> p b c", p=P),
                              x[:, ds(it * BATCH, BATCH), :]).then_inc(s_mout, 16)

            first_and_rest(act, ITERS, one_turn)
            mixed_out(ITERS - 1)
            act.wait_ge(s_mout, 16 * ITERS)
            act.wait_ge(s_tab, 16 * ITERS)

        @block.tensor
        def _(pe):
            t = nc.tensor
            pe.wait_ge(s_const, 1)
            pe.wait_ge(s_w, 64)
            for i in range(2 * NW // 512):
                for j in range(4):
                    chunk = 4 * (i % 3) + j
                    last = t.transpose(banks[i][:, P * j:P * j + P], w_nat[:, chunk, P * (i // 3):P * (i // 3) + P],
                                       ident[:, :])
                last.then_inc(s_wtr, 1)
            pe.wait_ge(s_misc, 16 * 18)
            for k in range(2):
                for o in range(2):
                    t.matmul(banks[6][:, 8 * k:8 * k + 8], w_nat[:, 6 + o, P * k:P * k + P], a_mat[:, o, :],
                             start=o == 0, stop=o == 1)
            for o in range(2):
                last = t.matmul(banks[6][0:1, 16:24], b_col[:, o:o + 1], a_mat[:, o, :], start=o == 0, stop=o == 1)
            last.then_inc(s_gw, 1)
            pe.wait_ge(s_counts, NBK)
            t.matmul(banks[7][:, 0:NBK], ones_sq[:, :], counts[:, :], start=True, stop=True)
            t.matmul(banks[7][:, 64:64 + NBK], before[:, :], counts[:, :], start=True, stop=True).then_inc(s_base, 1)
            pe.wait_ge(s_gwc, 1)
            pe.wait_ge(s_kv0, 1)
            def one_turn(it):
                pe.wait_ge(s_xn, it + 1)
                for k in range(2):
                    for u in range(BATCH):
                        last = t.transpose(banks[k][:, P * u:P * u + P], y[:, u, P * k:P * k + P], ident[:, :])
                last.then_inc(s_tr, 1)
                pe.wait_ge(s_xT, it + 1)
                for u in range(BATCH):
                    n = it * BATCH + u
                    wait_freed(pe, s_wh, it * BATCH + max(u - 1, 0))
                    for k in range(2):
                        t.matmul(banks[2 + u % 2][:, 0:C + 2 * H], xT[:, k, P * u:P * u + P], g_w[:, k, :],
                                 start=k == 0, stop=False)
                    t.matmul(banks[2 + u % 2][:, 0:C + 2 * H], ones_row[:, :], b_row[:, :], start=False, stop=True)\
                        .then_inc(s_g, 1)
                    wait_freed(pe, s_kk, it * BATCH + max(u - 1, 0))
                    wait_freed(pe, s_vc, it * BATCH + max(u - 1, 0))
                    for k in range(2):
                        last = t.matmul(banks[4 + u % 2][:, :], xT[:, k, P * u:P * u + P], wT[:, k, C:3 * C],
                                        start=k == 0, stop=k == 1)
                    last.then_inc(s_kv, 1)
                    pe.wait_ge(s_kk, n + 1)
                    pe.wait_ge(s_vc, n + 1)
                    for a in range(2):
                        last = t.matmul(banks[6][:, 129 * a:129 * a + 129], kk[:, u % 2, P * a:P * a + P],
                                        vv[:, u % 2, a, 0:129], start=False, stop=False, skip_group_check=True)
                    last.then_inc(s_acc, 1)

            first_and_rest(pe, ITERS, one_turn)
            pe.wait_ge(s_bd, 1)
            def one_turn(it):
                pe.wait_ge(s_xc, it + 1)
                for k in range(2):
                    for u in range(BATCH):
                        last = t.transpose(banks[k][:, P * u:P * u + P], y[:, u, P * k:P * k + P], ident[:, :])
                last.then_inc(s_tr2, 1)
                pe.wait_ge(s_xT2, it + 1)
                for m in range(2):
                    for k in range(2):
                        last = t.matmul(banks[2 + m][:, :], wT[:, k, P * m:P * m + P], xT[:, k, :],
                                        start=k == 0, stop=k == 1)
                    last.then_inc(s_q, 1)
                pe.wait_ge(s_qT, it * 2 + 2)
                wait_freed(pe, s_y2r, it)
                for u in range(BATCH):
                    for a in range(2):
                        last = t.matmul(banks[4 + u][:, KVC * a:KVC * a + KVC], qT[:, a, P * u:P * u + P],
                                        kv_bd[:, a, :], start=True, stop=True)
                    last.then_inc(s_t, 1)
                pe.wait_ge(s_x1, it + 1)
                for k in range(2):
                    for u in range(BATCH):
                        last = t.transpose(banks[k][:, P * u:P * u + P], x1[:, u, P * k:P * k + P], ident[:, :])
                last.then_inc(s_tr3, 1)
                pe.wait_ge(s_xT3, it + 1)
                for m in range(2):
                    for k in range(2):
                        last = t.matmul(banks[2 + m][:, :], wT[:, k, W1 + P * m:W1 + P * m + P], xT[:, k, :],
                                        start=k == 0, stop=k == 1)
                    last.then_inc(s_h, 1)
                pe.wait_ge(s_h1, it * 2 + 2)
                for u in range(BATCH):
                    for k in range(2):
                        t.matmul(banks[4 + u][:, 0:C], qT[:, k, P * u:P * u + P], wT[:, k, W2:W2 + C],
                                 start=k == 0, stop=False)
                    t.matmul(banks[4 + u][:, 0:C], ones_row[:, :], b2_row[:, :], start=False, stop=True)\
                        .then_inc(s_y2, 1)

            first_and_rest(pe, ITERS, one_turn)


def stage_edges_and_feed_forward(nc, A, sh):
    TILES = GROUPS * G
    QUAD = 4
    ctx = ExitStack()
    with ctx:
        sb = lambda name, shape, dt=F32: ctx.enter_context(nc.sbuf_tensor(name, shape, dt))
        sem = lambda name: ctx.enter_context(nc.semaphore(name))
        sems = lambda name, n: [sem(f"{name}{i}") for i in range(n)]
        banks = [ctx.enter_context(nc.psum_tensor(f"bank2_{i}", [P, 512], F32)) for i in range(8)]
        t8, ad, blk, bounds = sh["t8"], sh["ad"], sh["blk"], sh["bounds"]
        iota_row, node_col, ident = sh["iota_row"], sh["node_col"], sh["ident"]
        ones_row = sh["ones_row"]
        acc = sb("acc", [P, NBP, TB])
        col = [sb(f"col{i}", [P, GROUPS, G, 2], I32) for i in range(LOTS)]
        row = [sb(f"row{i}", [1, TILES * P, 2], I32) for i in range(2)]
        ones_bf = sb("ones_bf", [1, P], BF16)
        gathered = sb("gathered", [P, LOTS, TILES, TB])
        weighted = sb("weighted", [P, 2, TILES, TB])
        onehot = sb("onehot", [P, 2, TILES, P])
        dist = sb("dist", [P, 2, QUAD * P])
        node_sum = dist[:, 0, 0:NBP * H].rearrange("p (b h) -> p b h", h=H)
        onehot_t = sb("onehot_t", [P, 2, TILES, P])
        z = sb("z", [P, 2, TILES, H])
        e = sb("e", [P, 2, TILES, H])
        minus_node = sb("minus_node", [P, 1])
        ad_max = sb("ad_max", [P, 2 * H])
        ad_top = sb("ad_top", [P, 2 * H])
        spread_of = sb("spread_of", [P, H])
        too_wide = sb("too_wide", [P, 1])
        lower_by = sb("lower_by", [P, 1])
        plan_f = sb("plan_f", [P, 2])
        plan = sb("plan", [P, 2], I32)
        sweep_col = sb("sweep_col", [P, G, 2], I32)
        sweep_rows = weighted[:, 1, 0:G, :]
        sweep_scores = weighted[:, 1, G:2 * G, 0:H]

        s_col, s_gath, s_sel, s_mul = (sems(n, LOTS) for n in ("s_col", "s_gath", "s_sel", "s_mul"))
        s_row, s_as, s_d, s_p, s_main = (sems(n, 2) for n in ("s_row", "s_as", "s_d", "s_p", "s_main"))
        s_sum = sems("s_sum", GROUPS)
        s_max, s_top, s_plan, s_ready, s_bc, s_dist, s_ot = map(sem, (
            "s_max", "s_top", "s_plan", "s_ready", "s_bc", "s_dist", "s_ot"))
        w_used, w_col, w_rows, w_kept, w_in, w_sel, w_tr, w_ot, w_as, w_e, w_exp, w_sum = map(sem, (
            "w_used", "w_col", "w_rows", "w_kept", "w_in", "w_sel", "w_tr", "w_ot", "w_as", "w_e", "w_exp", "w_sum"))
        s_dve = sem("s_dve2")

        sW1, sW2, sW3 = sb("sW1", [P, 2, SH1]), sb("sW2", [P, 2, SH2]), sb("sW3", [P, C])
        eW1, eW2, eW3 = sb("eW1", [P, NE, 2, EH1]), sb("eW2", [P, NE, EH2]), sb("eW3", [P, 2, C])
        sb1, sb2, eb1, eb2 = sb("sb1", [P, 2]), sb("sb2", [P, 1]), sb("eb1", [P, NE]), sb("eb2", [P, 2])
        bias3 = sb("bias3", [NE + 1, C])
        gW, gb = sb("gW", [P, 2, NE]), sb("gb", [1, NE])
        expert_rows = sb("expert_rows", [NE + 1, 2 * P])
        lower = sb("lower", [P, NE, NE])
        recip = sb("recip", [P, BATCH, H])
        stats, mv = sb("stats3", [P, BATCH, 6]), sb("mv3", [P, BATCH, 2])
        std, inv = sb("std3", [P, BATCH]), sb("inv3", [P, BATCH])
        x = sb("x_batch", [P, BATCH, C])
        xf = sb("xf", [P, BATCH, C])
        xo = xf
        xT = sb("xT3", [P, 2, W4])
        top = sb("top", [P, BATCH])
        gate = sb("gate", [P, BATCH, NE])
        gate_e = sb("gate_e", [P, BATCH, NE])
        cmp = sb("cmp", [P, BATCH, NE, NE])
        cmp2 = sb("cmp2", [P, BATCH, NE, NE])
        wgt = sb("wgt", [P, BATCH, NE])
        wT = sb("wT3", [NE + 1, W4])
        h2, he1, he2 = sb("h2", [P, W4]), sb("he1", [P, NE, W4]), sb("he2", [P, 2, W4])
        h1 = he2
        (s_w, s_xin, s_var, s_std, s_xf, s_tr, s_xT, s_lg, s_lgs, s_ex, s_ga, s_ga2, s_wg, s_wt, s_wT) = map(sem, (
            "f_w", "f_xin", "f_var", "f_std", "f_xf", "f_tr", "f_xT", "f_lg", "f_lgs", "f_ex", "f_ga", "f_ga2",
            "f_wg", "f_wt", "f_wT"))
        (s_p1, s_h1, s_p2, s_h2, s_q1, s_he1, s_q2, s_he2, s_wb, s_hw, s_o, s_x, s_out) = map(sem, (
            "f_p1", "f_h1", "f_p2", "f_h2", "f_q1", "f_he1", "f_q2", "f_he2", "f_wb", "f_hw", "f_o", "f_x", "f_out"))
        s_pool, s_set, s_ff, s_bn = sem("f_pool"), sem("f_set"), sem("f_dve"), sem("f_bn")
        bank_nodes, bank_scores, bank_sums, f0, f1, f2, f3 = (
            banks[0], banks[1], banks[2:4], banks[4], banks[5], banks[6], banks[7])
        out_banks = (f1, f2, f0, f3)
        block = ctx.enter_context(nc.Block())

        def is_tail(batch):
            return isinstance(batch, int) and batch == TAIL_BATCH

        def blocks_in(batch):
            return 1 if is_tail(batch) else BATCH

        def turn_of(batch):
            return (0, 0) if is_tail(batch) else (batch + 1, batch * BATCH + 1)

        def after(it, l, lots):
            return it + (l + lots) // LOTS, (l + lots) % LOTS

        def blocks_of(engine, it, l):
            _, values = nc.values_load_multi_w_load_instructions(
                blk[0:1, ds((it * LOTS + l) * GROUPS, GROUPS)], engines=[engine], min_val=0, max_val=NB - 1,
                skip_runtime_bounds_check_because="a count of NB - 1 blocks at the most")
            return values

        def take(engine, semaphore, count):
            engine.wait_ge(semaphore, count)
            engine.sem_clear(semaphore)

        def collect(engine, group):
            with engine.Fori(0, engine.value_load(plan[0:1, 1:2], min_val=1, max_val=NG)) as g:
                group(g)

        def sweeps(engine, group, end_sweep=None):
            count = engine.value_load(plan[0:1, 0:1], min_val=1, max_val=MAX_SWEEPS)
            groups = engine.value_load(plan[0:1, 1:2], min_val=1, max_val=NG)
            with engine.Fori(0, count) as sweep:
                with engine.Fori(0, groups) as g:
                    group(g)
                if end_sweep:
                    end_sweep()

        def all_segments(engine, lot, piece):
            def bound(k, before_last=0):
                return engine.value_load(bounds[0:1, ds(k, 1)], min_val=2, max_val=IT_MAX - 1 - before_last)

            for l in range(LOTS):
                lot(0, l, lambda slot: None)
            with engine.Fori(1, bound(1)) as it:
                for l in range(LOTS):
                    lot(it, l, lambda slot: None)
            for slot in range(PIECES):
                piece(slot, TAIL_BATCH)
            with engine.Fori(bound(1), bound(2)) as it:
                for l in range(LOTS):
                    lot(it, l, lambda slot: None)
            with engine.Fori(0, LAST_BATCH) as k:
                begin, end = bound(k + 2, 2), bound(k + 3)
                for l in range(LOTS):
                    lot(begin, l, lambda slot: piece(slot, k))
                with engine.Fori(engine.snap(begin + 1), end) as it:
                    for l in range(LOTS):
                        lot(it, l, lambda slot: None)
            for slot in range(PIECES):
                piece(slot, LAST_BATCH)

        @block.sync
        def _(sp):
            def column(it, l):
                wait_freed(sp, s_gath[l], it * (16 * TILES))
                wait_freed(sp, s_sel[l], it)
                sp.dma_start(col[l][:, :, :, :],
                             sh["list"][ds((it * LOTS + l) * (TILES * P), TILES * P), :]
                             .rearrange("(g p k) w -> p g (k w)", g=GROUPS, p=P)).then_inc(s_col[l], 16)

            def group_column(g, signal):
                sp.dma_start(sweep_col[:, :, :], sh["list"][ds(g * GR, GR), :]
                             .rearrange("(p k) w -> p (k w)", p=P)).then_inc(signal, 16)

            def edge_scores(g):
                return sh["edge_scores"][ds(g * GR, GR), :].rearrange("(p k) h -> p k h", p=P)

            def keep_scores(g):
                group_column(g, w_col)
                sp.wait_ge(w_rows, g * (16 * G) + 16 * G)
                sp.dma_start(edge_scores(g), sweep_rows[:, :, C:TB]).then_inc(w_kept, 16)
                take(sp, w_kept, 16)

            def sweep_load(g):
                take(sp, w_used, 1)
                group_column(g, w_in)
                sp.dma_start(sweep_scores, edge_scores(g)).then_inc(w_in, 16)

            for l in range(LOTS):
                column(0, l)
            sp.wait_ge(s_plan, 1)
            collect(sp, keep_scores)
            sweeps(sp, sweep_load)
            loads = [(sW1[:, :, :], A["L0_ffn_sW1"].rearrange("(k p) o -> p k o", p=P)),
                     (sW2[:, :, :], A["L0_ffn_sW2"].rearrange("(k p) o -> p k o", p=P)),
                     (sW3[:, :], A["L0_ffn_sW3"]),
                     (eW2[:, :, :], A["L0_ffn_eW2"].rearrange("e h g -> h e g")),
                     (eW3[:, :, :], A["L0_ffn_eW3"].rearrange("(a e) g o -> (e g) a o", e=2)),
                     (sb2[:, :], A["L0_ffn_sb2"].rearrange("(p a) -> p a", a=1)),
                     (bias3[NE:NE + 1, :], A["L0_ffn_sb3"].rearrange("(a o) -> a o", a=1)),
                     (bias3[0:NE, :], A["L0_ffn_eb3"]),
                     (gb[:, :], A["L0_ffn_gb"].rearrange("(a o) -> a o", a=1))]
            for i in range(NE):
                loads.append((eW1[:, i, :, :], A["L0_ffn_eW1"][i].rearrange("(k p) h -> p k h", p=P)))
                loads.append((eb1[:, i:i + 1], A["L0_ffn_eb1"][i].rearrange("(p a) -> p a", a=1)))
                loads.append((eb2[64 * (i % 2):64 * (i % 2) + 64, i // 2:i // 2 + 1],
                              A["L0_ffn_eb2"][i].rearrange("(p a) -> p a", a=1)))
            for k in range(2):
                loads.append((sb1[:, k:k + 1], A["L0_ffn_sb1"][k * P:k * P + P].rearrange("(p a) -> p a", a=1)))
                loads.append((gW[:, k, :], A["L0_ffn_gW"][k * P:k * P + P, :]))
            assert len(loads) == LOADS3
            for dst, src in loads:
                sp.dma_start(dst, src).then_inc(s_w, 16)
            end = sp.value_load(bounds[0:1, ITERS:ITERS + 1], min_val=2, max_val=IT_MAX - 1)
            with sp.Fori(1, end) as it:
                for l in range(LOTS):
                    column(it, l)
            for l in range(2):
                column(sp.snap(end), l)

        @block.gpsimd
        def _(pool):
            g = nc.gpsimd
            pool.wait_ge(s_max, 2)
            g.partition_all_reduce(ad_top[:, :], ad_max[:, :], P, sh["RMAX"]).then_inc(s_top, 1)
            due = [pool.alloc_register(f"due_col{l}") for l in range(LOTS)]
            for l in range(LOTS):
                pool.reg_mov(due[l], 16)

            def gathers(it, l):
                wait_freed(pool, s_mul[l], it * GROUPS)
                pool.wait_ge(s_col[l], due[l])
                pool.reg_add(due[l], due[l], 16)
                for t in range(TILES):
                    g.indirect_dma_start(
                        gathered[:, l, t, :], None, sh["table"],
                        bass.IndirectOffsetOnAxis(ap=col[l][:, t // G, t % G, 0:1], axis=0)).then_inc(s_gath[l], 16)

            def sweep_gathers(group):
                take(pool, w_col, 16)
                for k in range(G):
                    g.indirect_dma_start(
                        sweep_rows[:, k, :], None, sh["table"],
                        bass.IndirectOffsetOnAxis(ap=sweep_col[:, k, 0:1], axis=0)).then_inc(w_rows, 16)

            gathers(0, 0)
            pool.wait_ge(s_plan, 1)
            collect(pool, sweep_gathers)
            for l in range(1, LOTS):
                gathers(0, l)
            g.memset(expert_rows[:, :], 1.0).then_inc(s_pool, 1)
            pool.wait_ge(s_pool, 1)
            g.affine_select(out=expert_rows[:, :], in_=expert_rows[:, :], compare_op=ALU.is_ge, fill=0.0, base=0,
                            pattern=[[1, NE * EH2]], channel_multiplier=-EH2).then_inc(s_pool, 1)
            pool.wait_ge(s_pool, 2)
            g.affine_select(out=expert_rows[:, :], in_=expert_rows[:, :], compare_op=ALU.is_gt, fill=0.0, base=EH2,
                            pattern=[[-1, NE * EH2]], channel_multiplier=EH2).then_inc(s_set, 1)
            g.memset(lower[:, :, :], 1.0).then_inc(s_pool, 1)
            pool.wait_ge(s_pool, 3)
            g.affine_select(out=lower[:, :, :], in_=lower[:, :, :], compare_op=ALU.is_gt, fill=0.0, base=0,
                            pattern=[[1, NE], [-1, NE]], channel_multiplier=0).then_inc(s_set, 1)
            end = pool.value_load(bounds[0:1, ITERS:ITERS + 1], min_val=2, max_val=IT_MAX - 1)
            with pool.Fori(1, end) as it:
                for l in range(LOTS):
                    gathers(it, l)
            with pool.Fori(end, pool.snap(end + 1)) as it:
                for l in range(2):
                    gathers(it, l)

        @block.tensor
        def _(pe):
            t = nc.tensor

            def spread(it, l, q):
                pe.wait_ge(s_row[l % 2], 16 * (it * (LOTS // 2) + l // 2) + 16)
                wait_freed(pe, s_dist, (it * LOTS + l) * 2 + q)
                words = row[l % 2][:, :, :].bitcast(BF16).rearrange("a (g p k) w -> a g k p w", g=GROUPS, p=P)
                t.matmul(bank_nodes[:, :], ones_bf[:, :], words[:, 2 * q:2 * q + 2, :, :, 3], start=True, stop=True)\
                    .then_inc(s_bc, 1)

            def by_node(it, l):
                wait_freed(pe, s_d[(l + 1) % 2], it * (LOTS // 2) + (l + 1) // 2)
                pe.wait_ge(s_ot, (it * LOTS + l) * 2 + 2)
                for g, b in enumerate(blocks_of(mybir.EngineType.PE, it, l)):
                    for k in range(G):
                        tile = g * G + k
                        last = t.matmul(bank_scores[:, 8 * tile:8 * tile + 8], onehot_t[:, l % 2, tile, :],
                                        t8[:, ds(b, 1), :].rearrange("p a w -> p (a w)"), start=True, stop=True)
                last.then_inc(s_as[l % 2], 1)

            def sums(it, l, groups):
                for g in groups:
                    pe.wait_ge(s_mul[l], it * GROUPS + g + 1)
                    wait_freed(pe, s_sum[(g + 2) % GROUPS], it * LOTS + l + g // 2)
                    for k in range(G):
                        last = t.matmul(bank_sums[g % 2][:, 0:TB], onehot[:, l % 2, g * G + k, :],
                                        weighted[:, l % 2, g * G + k, :], start=k == 0, stop=k == G - 1)
                    last.then_inc(s_main[l % 2], 1)

            def lot(it, l, piece):
                spread(*after(it, l, 3), 0)
                sums(it, l, (0, 1))
                spread(*after(it, l, 3), 1)
                sums(it, l, (2, 3))
                piece(2 * l)
                by_node(*after(it, l, 2))
                piece(2 * l + 1)

            def dense(bank, pairs, signal):
                for i, (left, right) in enumerate(pairs):
                    last = t.matmul(bank, left, right, start=i == 0, stop=i == len(pairs) - 1)
                last.then_inc(signal, 1)

            def first_layer(bank, e, it):
                w = P * blocks_in(it)
                dense(bank[:, 0:w], [(eW1[:, e, k, :], xT[:, k, 0:w]) for k in range(2)], s_q1)

            def second_layer(bank, a, it):
                turn, before = turn_of(it)
                w = P * blocks_in(it)
                pe.wait_ge(s_he1, turn * NE + 2 * a + 2)
                for e in range(2 * a, 2 * a + 2):
                    last = t.matmul(bank[64 * (e % 2):64 * (e % 2) + 64, 0:w], eW2[:, e, :], he1[:, e, 0:w],
                                    start=True, stop=True)
                last.then_inc(s_q2, 1)

            def output(u, experts):
                us, bank = slice(P * u, P * u + P), out_banks[u]
                if not experts:
                    t.matmul(bank[:, 0:C], h2[:, us], sW3[:, :], start=True, stop=False)
                    t.matmul(bank[:, 0:C], wT[:, us], bias3[:, :], start=False, stop=False)
                else:
                    t.matmul(bank[:, 0:C], he2[:, 0, us], eW3[:, 0, :], start=False, stop=False)
                    t.matmul(bank[:, 0:C], he2[:, 1, us], eW3[:, 1, :], start=False, stop=True).then_inc(s_o, 1)

            def piece(slot, it):
                turn, before = turn_of(it)
                blocks = blocks_in(it)
                w = P * blocks
                if slot == 4:
                    pe.wait_ge(s_xf, turn + 1)
                    wait_freed(pe, s_x, before)
                    for k in range(2):
                        for u in range(blocks):
                            last = t.transpose((f0, f1)[k][:, P * u:P * u + P], xf[:, u, P * k:P * k + P], ident[:, :])
                    last.then_inc(s_tr, 1)
                    pe.wait_ge(s_xT, turn + 1)
                    for u in range(blocks):
                        us = slice(P * u, P * u + P)
                        for i, (left, right) in enumerate(((xT[:, 0, us], gW[:, 0, :]), (xT[:, 1, us], gW[:, 1, :]),
                                                           (ones_row[:, :], gb[:, :]))):
                            last = t.matmul(f2[:, NE * u:NE * u + NE], left, right, start=i == 0, stop=i == 2)
                    last.then_inc(s_lg, 1)
                    for m in range(2):
                        dense((f0, f1)[m][:, 0:w], [(sW1[:, k, P * m:P * m + P], xT[:, k, 0:w]) for k in range(2)], s_p1)
                elif slot == 5:
                    first_layer(f3, 0, it)
                    pe.wait_ge(s_lgs, turn + 1)
                    first_layer(f2, 1, it)
                elif slot == 6:
                    pe.wait_ge(s_h1, turn * 2 + 2)
                    dense(f0[:, 0:w], [(sW2[:, k, :], h1[:, k, 0:w]) for k in range(2)], s_p2)
                    first_layer(f1, 2, it)
                elif slot == 7:
                    pe.wait_ge(s_he1, turn * NE + 1)
                    first_layer(f3, 3, it)
                    second_layer(f2, 0, it)
                elif slot == 8:
                    pe.wait_ge(s_h2, turn + 1)
                    pe.wait_ge(s_wg, turn + 1)
                    for u in range(blocks):
                        last = t.transpose(f0[0:NE, P * u:P * u + P], wgt[:, u, :], ident[:, :])
                    last.then_inc(s_wt, 1)
                    second_layer(f1, 1, it)
                elif slot == 9:
                    pe.wait_ge(s_wT, turn + 1)
                    for a in range(2):
                        dense((f0, f3)[a][:, 0:w], [(expert_rows[:, P * a:P * a + P], wT[:, 0:w])], s_wb)
                    pe.wait_ge(s_he2, turn * 2 + 2)
                    for u in range(min(blocks, 2)):
                        output(u, False)
                elif slot == 10:
                    pe.wait_ge(s_hw, turn * 2 + 2)
                    for u in range(min(blocks, 2)):
                        output(u, True)
                    for u in range(2, blocks):
                        output(u, False)
                elif slot == 11:
                    for u in range(2, blocks):
                        output(u, True)

            def sweep_products(g):
                take(pe, w_sel, 1)
                for k in range(G):
                    last = t.transpose(bank_nodes[:, P * k:P * k + P], onehot[:, 0, k, :], ident[:, :])
                last.then_inc(w_tr, 1)
                take(pe, w_ot, 1)
                block_of = pe.value_load(blk[0:1, ds(g, 1)], min_val=0, max_val=NB - 1)
                for k in range(G):
                    last = t.matmul(bank_scores[:, 8 * k:8 * k + 8], onehot_t[:, 0, k, :],
                                    t8[:, ds(block_of, 1), :].rearrange("p a w -> p (a w)"), start=True, stop=True)
                last.then_inc(w_as, 1)
                take(pe, w_exp, 1)
                for k in range(G):
                    last = t.matmul(bank_sums[0][:, 0:H], onehot[:, 0, k, :], weighted[:, 0, k, C:TB],
                                    start=k == 0, stop=k == G - 1)
                last.then_inc(w_sum, 1)

            pe.wait_ge(s_plan, 1)
            sweeps(pe, sweep_products)
            pe.wait_ge(s_ready, 1)
            for l in range(2):
                spread(0, l, 0)
                spread(0, l, 1)
                by_node(0, l)
            spread(0, 2, 0)
            spread(0, 2, 1)
            pe.wait_ge(s_w, 16 * LOADS3)
            pe.wait_ge(s_set, 2)
            all_segments(pe, lot, piece)

        @block.scalar
        def _(act):
            s = nc.scalar

            def load_row(it, l):
                act.dma_start(row[l % 2][:, :, :], sh["list"][ds((it * LOTS + l) * (TILES * P), TILES * P), :]
                              .rearrange("(a e) w -> a e w", a=1)).then_inc(s_row[l % 2], 16)

            def transposed(it, l):
                n, m = it * LOTS + l, it * (LOTS // 2) + l // 2
                for q in range(2):
                    act.wait_ge(s_bc, n * 2 + q + 1)
                    s.activation(dist[:, q, :], bank_nodes[:, :], ACT.Abs, bias=minus_node[:, 0:1]).then_inc(s_dist, 1)
                    act.wait_ge(s_dist, n * 2 + q + 1)
                    wait_freed(act, s_as[l % 2], m)
                    s.activation(onehot_t[:, l % 2, q * QUAD:(q + 1) * QUAD, :].rearrange("p t e -> p (t e)"),
                                 dist[:, q, :], ACT.Relu, bias=1.0, scale=-1.0).then_inc(s_ot, 1)
                load_row(*after(it, l, 2))

            def weights(it, l):
                m = it * (LOTS // 2) + l // 2
                act.wait_ge(s_d[l % 2], m + 1)
                wait_freed(act, s_main[l % 2], m * GROUPS)
                s.activation(weighted[:, l % 2, :, C:TB], e[:, l % 2, :, :], ACT.Exp).then_inc(s_p[l % 2], 1)

            def lot(it, l, piece):
                transposed(*after(it, l, 3))
                piece(2 * l)
                weights(*after(it, l, 2))
                piece(2 * l + 1)

            def load_x(k):
                act.dma_start(x[:, :, :], sh["mixed"][ds(k * W4, W4), :].rearrange("(b p) c -> p b c", p=P))\
                    .then_inc(s_xin, 16)

            def hidden(out, bank, bias, signal):
                s.activation(out, bank, ACT.Relu, bias=bias).then_inc(signal, 1)

            def expert(e, bank, it):
                turn, before = turn_of(it)
                act.wait_ge(s_q1, turn * NE + e + 1)
                w = P * blocks_in(it)
                hidden(he1[:, e, 0:w], bank[:, 0:w], eb1[:, e:e + 1], s_he1)

            def piece(slot, it):
                turn, before = turn_of(it)
                n = blocks_in(it)
                w = P * n
                if slot == 0 and isinstance(it, int) and it == LAST_BATCH:
                    end = act.value_load(bounds[0:1, ITERS:ITERS + 1], min_val=2, max_val=IT_MAX - 1)
                    for i in range(2):
                        act.wait_ge(s_row[i], end * (16 * (LOTS // 2)) + (48 - 16 * i))
                elif slot == 2:
                    act.wait_ge(s_var, turn + 1)
                    s.activation(std[:, 0:n], inv[:, 0:n], ACT.Sqrt).then_inc(s_std, 1)
                elif slot == 4:
                    act.wait_ge(s_tr, turn + 1)
                    s.copy(xT[:, 0, 0:w], f0[:, 0:w])
                    s.copy(xT[:, 1, 0:w], f1[:, 0:w]).then_inc(s_xT, 1)
                    for m in range(2):
                        act.wait_ge(s_p1, turn * 2 + m + 1)
                        hidden(h1[:, m, 0:w], (f0, f1)[m][:, 0:w], sb1[:, m:m + 1], s_h1)
                elif slot == 5:
                    expert(0, f3, it)
                    expert(1, f2, it)
                    act.wait_ge(s_lgs, turn + 1)
                    s.activation(gate_e[:, 0:n, :], gate[:, 0:n, :], ACT.Exp).then_inc(s_ex, 1)
                elif slot == 6:
                    act.wait_ge(s_ga, turn + 1)
                    s.activation(gate_e[:, 0:n, :], gate[:, 0:n, :], ACT.Exp).then_inc(s_ga2, 1)
                    act.wait_ge(s_p2, turn + 1)
                    hidden(h2[:, 0:w], f0[:, 0:w], sb2[:, 0:1], s_h2)
                    expert(2, f1, it)
                elif slot == 7:
                    expert(3, f3, it)
                    act.wait_ge(s_q2, turn * 2 + 1)
                    hidden(he2[:, 0, 0:w], f2[:, 0:w], eb2[:, 0:1], s_he2)
                elif slot == 8:
                    act.wait_ge(s_wt, turn + 1)
                    s.copy(wT[0:NE, 0:w], f0[0:NE, 0:w]).then_inc(s_wT, 1)
                    act.wait_ge(s_q2, turn * 2 + 2)
                    hidden(he2[:, 1, 0:w], f1[:, 0:w], eb2[:, 1:2], s_he2)
                elif slot == PIECES - 1:
                    act.wait_ge(s_x, before + n)
                    act.wait_ge(s_ready, 1)
                    if is_tail(it):
                        act.dma_start(A["out"][(NB - 1) * P:N, :], xo[0:TAIL, 0, :]).then_inc(s_out, 16)
                        load_x(0)
                    else:
                        act.dma_start(A["out"][ds(it * W4, W4), :].rearrange("(b p) c -> p b c", p=P), xo[:, :, :])\
                            .then_inc(s_out, 16)
                        if not isinstance(it, int):
                            load_x(it + 1)

            def sweep_weights(g):
                take(act, w_e, 1)
                s.activation(weighted[:, 0, 0:G, C:TB], e[:, 0, 0:G, :], ACT.Exp).then_inc(w_exp, 1)

            load_row(0, 0)
            load_row(0, 1)
            act.wait_ge(s_plan, 1)
            sweeps(act, sweep_weights)
            act.wait_ge(s_ready, 1)
            for l in range(2):
                transposed(0, l)
                weights(0, l)
            transposed(0, 2)
            act.wait_ge(s_w, 16 * LOADS3)
            load_x(TAIL_BATCH)
            all_segments(act, lot, piece)
            act.wait_ge(s_out, 16 * ITERS)

        @block.vector
        def _(dve):
            v = nc.vector
            done = [0]

            def step(ins):
                done[0] += 1
                ins.then_inc(s_dve, 1)
                dve.wait_ge(s_dve, done[0])

            def new_chain():
                done[0] = 0
                dve.sem_clear(s_dve)

            step(v.tensor_scalar(node_sum[:, :, :], ad[:, :, :], -1.0, None, ALU.mult))
            v.tensor_reduce(ad_max[:, 0:H], ad[:, 0:NB, :].rearrange("p b h -> p h b"), AX.X, ALU.max)\
                .then_inc(s_max, 1)
            v.tensor_reduce(ad_max[:, H:2 * H], node_sum[:, 0:NB, :].rearrange("p b h -> p h b"), AX.X, ALU.max)\
                .then_inc(s_max, 1)
            dve.wait_ge(s_top, 1)
            step(v.tensor_tensor(t8[:, :, H:2 * H], t8[:, :, 0:H],
                                 ad_top[:, 0:H].unsqueeze(1).broadcast_to([P, NBP, H]), ALU.add))
            step(v.scalar_tensor_tensor(t8[:, :, H:2 * H], t8[:, :, H:2 * H], SLOPE, t8[:, :, H:2 * H],
                                        ALU.mult, ALU.max))
            step(v.tensor_tensor(spread_of[:, :], ad_top[:, 0:H], ad_top[:, H:2 * H], ALU.add))
            step(v.tensor_reduce(plan_f[:, 0:1], spread_of[:, :], AX.X, ALU.max))
            step(v.tensor_scalar(too_wide[:, :], plan_f[:, 0:1], BOUND_GAP, None, ALU.is_gt))
            step(v.tensor_scalar(plan_f[:, 0:1], plan_f[:, 0:1], 1.0 / LOWER_BY, 1.5 - BOUND_GAP / LOWER_BY,
                                 ALU.mult, ALU.add))
            step(v.tensor_scalar(plan_f[:, 0:1], plan_f[:, 0:1], 1.0, float(MAX_SWEEPS), ALU.max, ALU.min))
            step(v.tensor_scalar(plan_f[:, 1:2], too_wide[:, :], float(NG - 1), 1.0, ALU.mult, ALU.add))
            step(v.tensor_copy(plan[:, :], plan_f[:, :]))
            step(v.tensor_scalar(lower_by[:, :], too_wide[:, :], LOWER_BY, None, ALU.mult))
            step(v.memset(node_sum[:, :, :], 0.0))
            v.memset(ones_bf[:, :], 1.0).then_inc(s_plan, 1)
            v.memset(wT[:, :], 1.0).then_inc(w_used, 1)
            v.tensor_scalar(minus_node[:, :], node_col[:, :], -1.0, None, ALU.mult)

            def sweep_group(g):
                block_of = dve.value_load(blk[0:1, ds(g, 1)], min_val=0, max_val=NB - 1)
                take(dve, w_in, 32)
                v.tensor_tensor(onehot[:, 0, 0:G, :], iota_row[:, :].unsqueeze(1).broadcast_to([P, G, P]),
                                sweep_col[:, :, 1:2].bitcast(F32).broadcast_to([P, G, P]), ALU.is_equal)\
                    .then_inc(w_sel, 1)
                take(dve, w_tr, 1)
                v.tensor_copy(onehot_t[:, 0, 0:G, :].rearrange("p k e -> p (k e)"), bank_nodes[:, 0:G * P])\
                    .then_inc(w_ot, 1)
                take(dve, w_as, 1)
                new_chain()
                from_node = bank_scores[:, 0:8 * G].rearrange("p (t w) -> p t w", w=8)
                step(v.tensor_tensor(z[:, 0, 0:G, :], sweep_scores, from_node[:, :, 0:H], ALU.add))
                step(v.scalar_tensor_tensor(z[:, 0, 0:G, :], z[:, 0, 0:G, :], SLOPE, z[:, 0, 0:G, :],
                                            ALU.mult, ALU.max))
                v.tensor_tensor(e[:, 0, 0:G, :], z[:, 0, 0:G, :], from_node[:, :, H:2 * H], ALU.subtract)\
                    .then_inc(w_e, 1)
                take(dve, w_sum, 1)
                place = node_sum[:, ds(block_of, 1), :].rearrange("p a h -> p (a h)")
                step(v.tensor_tensor(place, place, bank_sums[0][:, 0:H], ALU.add))
                v.memset(top[:, :], 0.0).then_inc(w_used, 1)

            def lower_tops():
                new_chain()
                step(v.tensor_scalar(node_sum[:, :, :], node_sum[:, :, :], TINY_SUM, None, ALU.is_lt))
                step(v.tensor_scalar(node_sum[:, :, :], node_sum[:, :, :], lower_by[:, 0:1], None, ALU.mult))
                step(v.tensor_tensor(t8[:, :, H:2 * H], t8[:, :, H:2 * H], node_sum[:, :, :], ALU.subtract))
                step(v.memset(node_sum[:, :, :], 0.0))

            new_chain()
            sweeps(dve, sweep_group, lower_tops)
            v.memset(acc[:, :, :], 0.0).then_inc(s_ready, 1)

            def weigh(it, l):
                m, i = it * (LOTS // 2) + l // 2, l % 2
                wait_freed(dve, s_main[i], m * GROUPS)
                dve.wait_ge(s_col[l], 16 * it + 16)
                within = col[l][:, :, :, :].rearrange("p g k w -> p (g k) w")[:, :, 1:2].bitcast(F32)
                v.tensor_tensor(onehot[:, i, :, :], iota_row[:, :].unsqueeze(1).broadcast_to([P, TILES, P]),
                                within.broadcast_to([P, TILES, P]), ALU.is_equal).then_inc(s_sel[l], 1)
                new_chain()
                dve.wait_ge(s_gath[l], it * (16 * TILES) + 16 * TILES)
                dve.wait_ge(s_as[i], m + 1)
                from_node = bank_scores[:, 0:8 * TILES].rearrange("p (t w) -> p t w", w=8)
                step(v.tensor_tensor(z[:, i, :, :], gathered[:, l, :, C:TB], from_node[:, :, 0:H], ALU.add))
                step(v.scalar_tensor_tensor(z[:, i, :, :], z[:, i, :, :], SLOPE, z[:, i, :, :], ALU.mult, ALU.max))
                v.tensor_tensor(e[:, i, :, :], z[:, i, :, :], from_node[:, :, H:2 * H], ALU.subtract)\
                    .then_inc(s_d[i], 1)

            def product(it, l, g):
                i, tiles = l % 2, slice(g * G, g * G + G)
                dve.wait_ge(s_p[i], it * (LOTS // 2) + l // 2 + 1)
                v.tensor_tensor(weighted[:, i, tiles, 0:C].rearrange("p k (a d) -> p k a d", d=HD),
                                gathered[:, l, tiles, 0:C].rearrange("p k (a d) -> p k a d", d=HD),
                                weighted[:, i, tiles, C:TB].unsqueeze(3).broadcast_to([P, G, H, HD]),
                                ALU.mult).then_inc(s_mul[l], 1)

            def add(it, l, g, block):
                if g:
                    dve.wait_ge(s_sum[g - 1], it * LOTS + l + 1)
                dve.wait_ge(s_main[l % 2], (it * (LOTS // 2) + l // 2) * GROUPS + g + 1)
                dve.wait_ge(s_ready, 1)
                place = acc[:, ds(block, 1), :].rearrange("p a c -> p (a c)")
                v.tensor_tensor(place, place, bank_sums[g % 2][:, 0:TB], ALU.add).then_inc(s_sum[g], 1)

            def lot(it, l, piece):
                blocks = blocks_of(mybir.EngineType.DVE, it, l)
                for half in range(2):
                    for g in (2 * half, 2 * half + 1):
                        add(it, l, g, blocks[g])
                        product(*after(it, l, 1), g)
                    if half:
                        dve.wait_ge(s_sum[GROUPS - 1], it * LOTS + l + 1)
                        weigh(*after(it, l, 2))
                    piece(2 * l + half)

            ff_done = [0]

            def piece(slot, it):
                turn, before = turn_of(it)
                n = blocks_in(it)
                w = P * n
                if slot == 0:
                    ff_done[0] = 0

                def step(ins):
                    ff_done[0] += 1
                    ins.then_inc(s_ff, 1)
                    dve.wait_ge(s_ff, turn * FF_STEPS + ff_done[0])

                if slot == 0:
                    part = acc[:, ds(it * BATCH, n), :]
                    wait_freed(dve, s_out, 16 * turn)
                    step(v.tensor_scalar(recip[:, 0:n, :], part[:, :, C:TB], 1e-37, None, ALU.max))
                    step(v.reciprocal(recip[:, 0:n, :], recip[:, 0:n, :]))
                    step(v.tensor_tensor(xf[:, 0:n, :].rearrange("p b (a d) -> p b a d", d=HD),
                                         part[:, :, 0:C].rearrange("p b (a d) -> p b a d", d=HD),
                                         recip[:, 0:n, :].unsqueeze(3).broadcast_to([P, n, H, HD]), ALU.mult))
                elif slot == 1:
                    dve.wait_ge(s_xin, 16 * turn + 16)
                    step(v.tensor_tensor(x[:, 0:n, :], x[:, 0:n, :], xf[:, 0:n, :], ALU.add))
                    for u in range(min(n, 2)):
                        v.bn_stats(stats[:, u, :], x[:, u, :]).then_inc(s_bn, 1)
                elif slot == 2:
                    for u in range(2, n):
                        v.bn_stats(stats[:, u, :], x[:, u, :]).then_inc(s_bn, 1)
                    dve.wait_ge(s_bn, n)
                    for u in range(n):
                        v.bn_aggr(mv[:, u, :], stats[:, u, :]).then_inc(s_bn, 1)
                    dve.wait_ge(s_bn, 2 * n)
                    v.tensor_scalar(inv[:, 0:n], mv[:, 0:n, 1], EPS_LN, None, ALU.add).then_inc(s_var, 1)
                elif slot == 3:
                    dve.wait_ge(s_std, turn + 1)
                    reciprocal = v.reciprocal(inv[:, 0:n], std[:, 0:n])
                    dve.sem_clear(s_bn)
                    step(reciprocal)
                    for u in range(n):
                        last = v.tensor_scalar(xf[:, u, :], x[:, u, :], mv[:, u, 0:1], inv[:, u:u + 1],
                                               ALU.subtract, ALU.mult)
                    last.then_inc(s_xf, 1)
                elif slot == 5:
                    dve.wait_ge(s_lg, turn + 1)
                    logits = f2[:, 0:n * NE].rearrange("p (u e) -> p u e", e=NE)
                    step(v.tensor_reduce(top[:, 0:n], logits, AX.X, ALU.max))
                    v.tensor_tensor(gate[:, 0:n, :], logits, top[:, 0:n].unsqueeze(2).broadcast_to([P, n, NE]),
                                    ALU.subtract).then_inc(s_lgs, 1)
                elif slot == 6:
                    dve.wait_ge(s_ex, turn + 1)
                    step(v.tensor_reduce(top[:, 0:n], gate_e[:, 0:n, :], AX.X, ALU.add))
                    step(v.reciprocal(top[:, 0:n], top[:, 0:n]))
                    v.tensor_tensor(gate[:, 0:n, :], gate_e[:, 0:n, :], top[:, 0:n].unsqueeze(2).broadcast_to([P, n, NE]),
                                    ALU.mult).then_inc(s_ga, 1)
                elif slot == 7:
                    dve.wait_ge(s_ga, turn + 1)
                    mine = gate[:, 0:n, :].unsqueeze(3).broadcast_to([P, n, NE, NE])
                    others = gate[:, 0:n, :].unsqueeze(2).broadcast_to([P, n, NE, NE])
                    step(v.tensor_tensor(cmp2[:, 0:n, :, :], others, mine, ALU.is_equal))
                    step(v.tensor_tensor(cmp2[:, 0:n, :, :], cmp2[:, 0:n, :, :],
                                         lower[:, :, :].unsqueeze(1).broadcast_to([P, n, NE, NE]), ALU.mult))
                    step(v.tensor_tensor(cmp[:, 0:n, :, :], others, mine, ALU.is_gt))
                    step(v.tensor_tensor(cmp[:, 0:n, :, :], cmp[:, 0:n, :, :], cmp2[:, 0:n, :, :], ALU.add))
                    step(v.tensor_reduce(wgt[:, 0:n, :], cmp[:, 0:n, :, :], AX.X, ALU.add))
                    dve.wait_ge(s_ga2, turn + 1)
                    step(v.scalar_tensor_tensor(wgt[:, 0:n, :], wgt[:, 0:n, :], 1.5, gate_e[:, 0:n, :],
                                                ALU.is_lt, ALU.mult))
                    step(v.tensor_reduce(top[:, 0:n], wgt[:, 0:n, :], AX.X, ALU.add))
                    step(v.reciprocal(top[:, 0:n], top[:, 0:n]))
                    v.tensor_tensor(wgt[:, 0:n, :], wgt[:, 0:n, :], top[:, 0:n].unsqueeze(2).broadcast_to([P, n, NE]),
                                    ALU.mult).then_inc(s_wg, 1)
                elif slot == 9:
                    for a in range(2):
                        dve.wait_ge(s_he2, turn * 2 + a + 1)
                        dve.wait_ge(s_wb, turn * 2 + a + 1)
                        v.tensor_tensor(he2[:, a, 0:w], he2[:, a, 0:w], (f0, f3)[a][:, 0:w], ALU.mult).then_inc(s_hw, 1)
                elif slot == PIECES - 1:
                    assert ff_done[0] == FF_STEPS
                    for u in range(n):
                        dve.wait_ge(s_o, before + u + 1)
                        v.tensor_tensor(xo[:, u, :], x[:, u, :], out_banks[u][:, 0:C], ALU.add).then_inc(s_x, 1)

            weigh(0, 0)
            for g in range(GROUPS):
                product(0, 0, g)
            weigh(0, 1)
            dve.wait_ge(s_set, 2)
            all_segments(dve, lot, piece)


LOADS3 = 9 + 3 * NE + 4
PIECES = 2 * LOTS
FF_STEPS = 16


def graph_layer(nc, A):
    ctx = ExitStack()
    with ctx:
        sb = lambda name, shape, dt=F32: ctx.enter_context(nc.sbuf_tensor(name, shape, dt))
        sh = {
            "ident": sb("ident", [P, P]), "iota_row": sb("iota_row", [P, P]), "ones_row": sb("ones_row", [1, P]),
            "node_col": sb("node_col", [P, 1]),
            "t8": sb("t8", [P, NBP, 2 * H]),
            "ad": sb("ad", [P, NBP, H]),
            "blk": sb("blk", [1, P * BLK_COLS], I32),
            "bounds": sb("bounds", [1, ITERS + 1], I32),
            "table": nc.dram_tensor("table", (NBP * P + 1, TB), F32, kind="Internal").ap(),
            "mixed": nc.dram_tensor("mixed", (NBP * P, C), F32, kind="Internal").ap(),
            "edge_scores": nc.dram_tensor("edge_scores", (LIST, H), F32, kind="Internal").ap(),
            "list": nc.dram_tensor("edge_list", (LIST, 2), I32, kind="Internal").ap(),
            "blk_dram": nc.dram_tensor("blk_dram", (P * BLK_COLS,), I32, kind="Internal").ap(),
            "RMAX": bass.bass_isa.ReduceOp.max,
        }
        stage_sort_and_mix(nc, A, sh)
        stage_edges_and_feed_forward(nc, A, sh)


_INS = ["x", "src", "dst", "L0_gnn_W", "L0_gnn_b", "L0_gnn_a_src", "L0_gnn_a_dst", "L0_mix_Wqkv", "L0_mix_ln1_g",
        "L0_mix_ln1_b", "L0_mix_W1", "L0_mix_b1", "L0_mix_W2", "L0_mix_b2", "L0_mix_ln2_g", "L0_mix_ln2_b",
        "L0_ffn_sW1", "L0_ffn_sb1", "L0_ffn_sW2", "L0_ffn_sb2", "L0_ffn_sW3", "L0_ffn_sb3", "L0_ffn_eW1",
        "L0_ffn_eb1", "L0_ffn_eW2", "L0_ffn_eb2", "L0_ffn_eW3", "L0_ffn_eb3", "L0_ffn_gW", "L0_ffn_gb"]


def kernel(**inputs):
    import concourse.bacc as _bacc
    from concourse.bass_utils import run_bass_kernel_spmd as _run

    nc = _bacc.Bacc("TRN2", target_bir_lowering=False, num_devices=1)
    arrays, args = {}, {}
    for name in _INS:
        a = np.ascontiguousarray(inputs[name])
        arrays[f"in_{name}"] = a
        args[name] = nc.dram_tensor(f"in_{name}", a.shape, mybir.dt.from_np(a.dtype), kind="ExternalInput").ap()
    args["out"] = nc.dram_tensor("out", (N, C), F32, kind="ExternalOutput").ap()
    graph_layer(nc, args)
    r = _run(nc, [arrays], core_ids=[0])
    return r.results[0]["out"]
```
